# Optimizing a Trainium2 kernel written in Bass

```python
import numpy as np
import jax
import jax.numpy as jnp

def _softmax(x, axis=-1):
    return jax.nn.softmax(x, axis=axis)

def _gelu(x):
    return jax.nn.gelu(x, approximate=True)

def _silu(x):
    return jax.nn.silu(x)

def _sigmoid(x):
    return jax.nn.sigmoid(x)

def _layernorm(x, axis=-1, eps=1e-05):
    m = jnp.mean(x, axis=axis, keepdims=True)
    v = jnp.var(x, axis=axis, keepdims=True)
    return (x - m) / jnp.sqrt(v + eps)

def _scatter_add(tgt, idx, src, axis=0):
    return tgt.at[idx].add(src)

def _segment_sum(src, seg, n):
    return jax.ops.segment_sum(src, seg, n)
kernel_name = 'mk_macaron_d2_jaxref_r8_9ea11f'

def setup_inputs(seed: int=0):
    np.random.seed(seed)
    _w = jnp.asarray

    def _L0_attn_setup():
        import jax, jax.numpy as jnp
        import numpy as np
        D_MODEL = 128
        NUM_HEADS = 16
        HEAD_DIM = D_MODEL // NUM_HEADS
        ROPE_THETA = 10000.0

        def apply_rope(x):
            S, d_k = (x.shape[-2], x.shape[-1])
            inv_freq = ROPE_THETA ** (jnp.arange(0, d_k, 2, dtype=jnp.float32) / d_k)
            ang = jnp.arange(S, dtype=jnp.float32)[:, None] / inv_freq[None, :]
            cos, sin = (jnp.cos(ang), jnp.sin(ang))
            xp = x.reshape(x.shape[:-1] + (d_k // 2, 2))
            x0, x1 = (xp[..., 0], xp[..., 1])
            out = jnp.stack([x0 * cos - x1 * sin, x0 * sin + x1 * cos], axis=-1)
            return out.reshape(x.shape)
        key = jax.random.key(seed)
        k1, k2, k3 = jax.random.split(key, 3)
        B, S = (2, 256)
        std = 2.0 / (D_MODEL + 3 * D_MODEL)
        std_o = 2.0 / (D_MODEL + D_MODEL)
        return {'x': jax.random.normal(k1, (B, S, D_MODEL), dtype=jnp.float32), 'W_qkv': jax.random.normal(k2, (3 * D_MODEL, D_MODEL), dtype=jnp.float32) * std, 'W_o': jax.random.normal(k3, (D_MODEL, D_MODEL), dtype=jnp.float32) * std_o}
    _L0_attn_in = _L0_attn_setup()

    def _L0_ffn_setup():
        import jax, jax.numpy as jnp
        import numpy as np
        D_MODEL = 128
        D_OUT = 128
        RANK = 16
        NUM_TRUE = 8
        NUM_NULL = 2
        TOP_K = 2
        SCALING = 32.0 / 16.0
        key = jax.random.key(seed)
        ks = jax.random.split(key, 6)
        x = jax.random.normal(ks[0], (4, 512, D_MODEL), dtype=jnp.float32)
        base_w = jax.random.normal(ks[1], (D_OUT, D_MODEL), dtype=jnp.float32) / np.sqrt(D_MODEL)
        base_b = jax.random.normal(ks[2], (D_OUT,), dtype=jnp.float32) * 0.01
        gate_w = jax.random.normal(ks[3], (NUM_TRUE + NUM_NULL, D_MODEL), dtype=jnp.float32) / np.sqrt(D_MODEL)
        lora_A = jax.random.normal(ks[4], (NUM_TRUE, RANK, D_MODEL), dtype=jnp.float32) / np.sqrt(D_MODEL)
        lora_B = jax.random.normal(ks[5], (NUM_TRUE, D_OUT, RANK), dtype=jnp.float32) * 0.01
        return {'x': x, 'base_w': base_w, 'base_b': base_b, 'gate_w': gate_w, 'lora_A': lora_A, 'lora_B': lora_B}
    _L0_ffn_in = _L0_ffn_setup()

    def _L1_attn_setup():
        import jax, jax.numpy as jnp
        import numpy as np
        from jax import lax
        B, L, D, H = (4, 256, 128, 16)
        DK = D // H
        DV = D // H
        SCALE = DK ** (-0.5)

        def _gla_forward(hidden_states, Wq, Wf, Wi, Wo):
            b, l, d = hidden_states.shape
            q_logits = hidden_states @ Wq
            f_logits = hidden_states @ Wf
            v = hidden_states @ Wi
            q = jax.nn.softmax(q_logits, axis=-1)
            k = 1.0 - jax.nn.softmax(f_logits, axis=-1)
            g = jax.nn.log_softmax(f_logits, axis=-1)

            def split_heads(x, hd):
                return x.reshape(b, l, H, hd).transpose(1, 0, 2, 3)
            q_t = split_heads(q, DK)
            k_t = split_heads(k, DK)
            g_t = split_heads(g, DK)
            v_t = split_heads(v, DV)

            def step(S, inp):
                qt, kt, vt, gt = inp
                S = S * jnp.exp(gt)[..., None] + kt[..., None] * vt[..., None, :]
                ot = jnp.einsum('bhk,bhkv->bhv', qt * SCALE, S)
                return (S, ot)
            S0 = jnp.zeros((b, H, DK, DV), hidden_states.dtype)
            _, o = lax.scan(step, S0, (q_t, k_t, v_t, g_t))
            o = o.transpose(1, 0, 2, 3).reshape(b, l, d)
            return o @ Wo
        key = jax.random.key(seed)
        ks = jax.random.split(key, 5)
        std = 0.02
        return {'hidden_states': jax.random.normal(ks[0], (B, L, D), jnp.float32), 'Wq': jax.random.normal(ks[1], (D, D), jnp.float32) * std, 'Wf': jax.random.normal(ks[2], (D, D), jnp.float32) * std, 'Wi': jax.random.normal(ks[3], (D, D), jnp.float32) * std, 'Wo': jax.random.normal(ks[4], (D, D), jnp.float32) * std}
    _L1_attn_in = _L1_attn_setup()

    def _L1_ffn_setup():
        import jax, jax.numpy as jnp
        import numpy as np
        B, T, C = (2, 128, 128)
        H = 512
        E_R, E_S, K = (8, 2, 2)

        def _rmsnorm(x, g):
            eps = jnp.finfo(x.dtype).eps
            return x * jax.lax.rsqrt(jnp.mean(x * x, axis=-1, keepdims=True) + eps) * g

        def _experts_mlp(x, g, W1, b1, W2, b2):
            xn = _rmsnorm(x, g)
            h = jnp.einsum('btc,ech->bteh', xn, W1) + b1
            h = jax.nn.gelu(h, approximate=False)
            return jnp.einsum('bteh,ehc->btec', h, W2) + b2
        key = jax.random.key(seed)
        ks = jax.random.split(key, 12)
        s = 0.02
        return {'u': jax.random.normal(ks[0], (B, T, C), dtype=jnp.float32), 'g_shared': jnp.ones((C,), jnp.float32), 'W1_s': jax.random.normal(ks[1], (E_S, C, H), jnp.float32) * s, 'b1_s': jax.random.normal(ks[2], (E_S, H), jnp.float32) * s, 'W2_s': jax.random.normal(ks[3], (E_S, H, C), jnp.float32) * s, 'b2_s': jax.random.normal(ks[4], (E_S, C), jnp.float32) * s, 'g_routed': jnp.ones((C,), jnp.float32), 'W1_r': jax.random.normal(ks[5], (E_R, C, H), jnp.float32) * s, 'b1_r': jax.random.normal(ks[6], (E_R, H), jnp.float32) * s, 'W2_r': jax.random.normal(ks[7], (E_R, H, C), jnp.float32) * s, 'b2_r': jax.random.normal(ks[8], (E_R, C), jnp.float32) * s, 'centroids': jax.random.normal(ks[9], (C, E_R), jnp.float32) * s}
    _L1_ffn_in = _L1_ffn_setup()
    _d = {'L0_attn_x': _L0_attn_in['x'], 'L0_attn_W_qkv': _L0_attn_in['W_qkv'], 'L0_attn_W_o': _L0_attn_in['W_o'], 'L0_ffn_base_w': _L0_ffn_in['base_w'], 'L0_ffn_base_b': _L0_ffn_in['base_b'], 'L0_ffn_gate_w': _L0_ffn_in['gate_w'], 'L0_ffn_lora_A': _L0_ffn_in['lora_A'], 'L0_ffn_lora_B': _L0_ffn_in['lora_B'], 'L1_attn_Wq': _L1_attn_in['Wq'], 'L1_attn_Wf': _L1_attn_in['Wf'], 'L1_attn_Wi': _L1_attn_in['Wi'], 'L1_attn_Wo': _L1_attn_in['Wo'], 'L1_ffn_g_shared': _L1_ffn_in['g_shared'], 'L1_ffn_W1_s': _L1_ffn_in['W1_s'], 'L1_ffn_b1_s': _L1_ffn_in['b1_s'], 'L1_ffn_W2_s': _L1_ffn_in['W2_s'], 'L1_ffn_b2_s': _L1_ffn_in['b2_s'], 'L1_ffn_g_routed': _L1_ffn_in['g_routed'], 'L1_ffn_W1_r': _L1_ffn_in['W1_r'], 'L1_ffn_b1_r': _L1_ffn_in['b1_r'], 'L1_ffn_W2_r': _L1_ffn_in['W2_r'], 'L1_ffn_b2_r': _L1_ffn_in['b2_r'], 'L1_ffn_centroids': _L1_ffn_in['centroids']}
    _x0 = _d['L0_attn_x']
    _d['L0_attn_x'] = jax.random.normal(jax.random.fold_in(jax.random.key(seed), 1), (16, 512, 128), dtype=_x0.dtype)
    del _x0
    return _d

def reference(L0_attn_x, L0_attn_W_qkv, L0_attn_W_o, L0_ffn_base_w, L0_ffn_base_b, L0_ffn_gate_w, L0_ffn_lora_A, L0_ffn_lora_B, L1_attn_Wq, L1_attn_Wf, L1_attn_Wi, L1_attn_Wo, L1_ffn_g_shared, L1_ffn_W1_s, L1_ffn_b1_s, L1_ffn_W2_s, L1_ffn_b2_s, L1_ffn_g_routed, L1_ffn_W1_r, L1_ffn_b1_r, L1_ffn_W2_r, L1_ffn_b2_r, L1_ffn_centroids):

    def _L0_attn_ref(x, W_qkv, W_o):
        import jax, jax.numpy as jnp
        import numpy as np
        D_MODEL = 128
        NUM_HEADS = 16
        HEAD_DIM = D_MODEL // NUM_HEADS
        ROPE_THETA = 10000.0

        def apply_rope(x):
            S, d_k = (x.shape[-2], x.shape[-1])
            inv_freq = ROPE_THETA ** (jnp.arange(0, d_k, 2, dtype=jnp.float32) / d_k)
            ang = jnp.arange(S, dtype=jnp.float32)[:, None] / inv_freq[None, :]
            cos, sin = (jnp.cos(ang), jnp.sin(ang))
            xp = x.reshape(x.shape[:-1] + (d_k // 2, 2))
            x0, x1 = (xp[..., 0], xp[..., 1])
            out = jnp.stack([x0 * cos - x1 * sin, x0 * sin + x1 * cos], axis=-1)
            return out.reshape(x.shape)
        B, S, d_model = x.shape
        H, d_k = (NUM_HEADS, HEAD_DIM)
        qkv = jnp.einsum('bsi,oi->bso', x, W_qkv)
        Q, K, V = jnp.split(qkv, 3, axis=-1)

        def to_heads(t):
            return t.reshape(B, S, H, d_k).transpose(0, 2, 1, 3)
        Q, K, V = (to_heads(Q), to_heads(K), to_heads(V))
        Q, K = (apply_rope(Q), apply_rope(K))
        scores = jnp.einsum('bhqd,bhkd->bhqk', Q, K) / jnp.sqrt(jnp.float32(d_k))
        causal = jnp.tril(jnp.ones((S, S), dtype=bool))
        scores = jnp.where(causal, scores, -jnp.inf)
        attn = jax.nn.softmax(scores, axis=-1)
        out = jnp.einsum('bhqk,bhkd->bhqd', attn, V)
        out = out.transpose(0, 2, 1, 3).reshape(B, S, d_model)
        return jnp.einsum('bsi,oi->bso', out, W_o)

    def _L0_ffn_ref(x, base_w, base_b, gate_w, lora_A, lora_B):
        import jax, jax.numpy as jnp
        import numpy as np
        D_MODEL = 128
        D_OUT = 128
        RANK = 16
        NUM_TRUE = 8
        NUM_NULL = 2
        TOP_K = 2
        SCALING = 32.0 / 16.0
        xf = x.reshape(-1, x.shape[-1])
        logits = jnp.einsum('td,ed->te', xf, gate_w)
        probs = jax.nn.softmax(logits, axis=-1)
        weights, selected = jax.lax.top_k(probs, TOP_K)
        true_mask = (selected < NUM_TRUE).astype(weights.dtype)
        tw = weights * true_mask
        denom = tw.sum(axis=-1, keepdims=True)
        denom = jnp.where(denom > 0, denom, jnp.ones_like(denom))
        nw = tw / denom
        onehot = jax.nn.one_hot(selected, NUM_TRUE, dtype=nw.dtype)
        ew = jnp.einsum('tk,tke->te', nw, onehot)
        z = jnp.einsum('td,erd->ter', xf, lora_A)
        moe = jnp.einsum('ter,te,eor->to', z, ew, lora_B) * SCALING
        base = jnp.einsum('td,od->to', xf, base_w) + base_b
        out = (base + moe).reshape(x.shape[:-1] + (D_OUT,))
        return out

    def _L1_attn_ref(hidden_states, Wq, Wf, Wi, Wo):
        import jax, jax.numpy as jnp
        import numpy as np
        from jax import lax
        B, L, D, H = (4, 256, 128, 16)
        DK = D // H
        DV = D // H
        SCALE = DK ** (-0.5)

        def _gla_forward(hidden_states, Wq, Wf, Wi, Wo):
            b, l, d = hidden_states.shape
            q_logits = hidden_states @ Wq
            f_logits = hidden_states @ Wf
            v = hidden_states @ Wi
            q = jax.nn.softmax(q_logits, axis=-1)
            k = 1.0 - jax.nn.softmax(f_logits, axis=-1)
            g = jax.nn.log_softmax(f_logits, axis=-1)

            def split_heads(x, hd):
                return x.reshape(b, l, H, hd).transpose(1, 0, 2, 3)
            q_t = split_heads(q, DK)
            k_t = split_heads(k, DK)
            g_t = split_heads(g, DK)
            v_t = split_heads(v, DV)

            def step(S, inp):
                qt, kt, vt, gt = inp
                S = S * jnp.exp(gt)[..., None] + kt[..., None] * vt[..., None, :]
                ot = jnp.einsum('bhk,bhkv->bhv', qt * SCALE, S)
                return (S, ot)
            S0 = jnp.zeros((b, H, DK, DV), hidden_states.dtype)
            _, o = lax.scan(step, S0, (q_t, k_t, v_t, g_t))
            o = o.transpose(1, 0, 2, 3).reshape(b, l, d)
            return o @ Wo
        return _gla_forward(hidden_states, Wq, Wf, Wi, Wo)

    def _L1_ffn_ref(u, g_shared, W1_s, b1_s, W2_s, b2_s, g_routed, W1_r, b1_r, W2_r, b2_r, centroids):
        import jax, jax.numpy as jnp
        import numpy as np
        B, T, C = (2, 128, 128)
        H = 512
        E_R, E_S, K = (8, 2, 2)

        def _rmsnorm(x, g):
            eps = jnp.finfo(x.dtype).eps
            return x * jax.lax.rsqrt(jnp.mean(x * x, axis=-1, keepdims=True) + eps) * g

        def _experts_mlp(x, g, W1, b1, W2, b2):
            xn = _rmsnorm(x, g)
            h = jnp.einsum('btc,ech->bteh', xn, W1) + b1
            h = jax.nn.gelu(h, approximate=False)
            return jnp.einsum('bteh,ehc->btec', h, W2) + b2
        h_s = _experts_mlp(u, g_shared, W1_s, b1_s, W2_s, b2_s).sum(axis=-2)
        scores = jax.nn.sigmoid(u @ centroids)
        gpk, i_topk = jax.lax.top_k(scores, K)
        gk = gpk / scores.sum(axis=-1, keepdims=True)
        routed_all = _experts_mlp(u, g_routed, W1_r, b1_r, W2_r, b2_r)
        routed_topk = jnp.take_along_axis(routed_all, i_topk[..., None], axis=2)
        h_r = (gk[..., None] * routed_topk).sum(axis=-2)
        return u + h_s + h_r
    x = L0_attn_x
    x = x + 0.5 * _L0_ffn_ref(_layernorm(x, axis=-1), L0_ffn_base_w, L0_ffn_base_b, L0_ffn_gate_w, L0_ffn_lora_A, L0_ffn_lora_B)
    x = x + _L0_attn_ref(_layernorm(x, axis=-1), L0_attn_W_qkv, L0_attn_W_o)
    x = x + 0.5 * _L0_ffn_ref(_layernorm(x, axis=-1), L0_ffn_base_w, L0_ffn_base_b, L0_ffn_gate_w, L0_ffn_lora_A, L0_ffn_lora_B)
    x = x + 0.5 * _L1_ffn_ref(_layernorm(x, axis=-1), L1_ffn_g_shared, L1_ffn_W1_s, L1_ffn_b1_s, L1_ffn_W2_s, L1_ffn_b2_s, L1_ffn_g_routed, L1_ffn_W1_r, L1_ffn_b1_r, L1_ffn_W2_r, L1_ffn_b2_r, L1_ffn_centroids)
    x = x + _L1_attn_ref(_layernorm(x, axis=-1), L1_attn_Wq, L1_attn_Wf, L1_attn_Wi, L1_attn_Wo)
    x = x + 0.5 * _L1_ffn_ref(_layernorm(x, axis=-1), L1_ffn_g_shared, L1_ffn_W1_s, L1_ffn_b1_s, L1_ffn_W2_s, L1_ffn_b2_s, L1_ffn_g_routed, L1_ffn_W1_r, L1_ffn_b1_r, L1_ffn_W2_r, L1_ffn_b2_r, L1_ffn_centroids)
    return x

_drawn_inputs = setup_inputs


def setup_inputs(seed=0):
    import zlib

    import numpy as np

    out = dict(_drawn_inputs(seed))
    spreads = {'L1_ffn_g_shared': (1.0, 0.6), 'L1_ffn_g_routed': (1.0, 0.6)}
    factors = {'L0_attn_W_qkv': 8.0,
     'L0_attn_W_o': 8.0,
     'L0_ffn_base_b': 7.737,
     'L1_attn_Wq': 8.0,
     'L1_attn_Wf': 8.0,
     'L1_attn_Wi': 8.0,
     'L1_attn_Wo': 8.0,
     'L1_ffn_b1_s': 8.0,
     'L1_ffn_b2_s': 4.367,
     'L1_ffn_W1_r': 8.0,
     'L1_ffn_b1_r': 8.0,
     'L1_ffn_W2_r': 8.0,
     'L1_ffn_b2_r': 8.0,
     'L1_ffn_centroids': 8.0}
    for name, (base, spread) in spreads.items():
        noise = np.random.default_rng([zlib.crc32(name.encode()), seed]).standard_normal(out[name].shape)
        drawn = base * np.exp(spread * noise) if base else spread * noise
        out[name] = jnp.asarray(drawn.astype(out[name].dtype))
    for name, factor in factors.items():
        out[name] = (out[name] * factor).astype(out[name].dtype)
    return out
```

```python
from contextlib import ExitStack

import numpy as np

import concourse.bass as bass
from concourse import mybir

ALU = mybir.AluOpType
ACT = mybir.ActivationFunctionType
AX = mybir.AxisListType
F32 = mybir.dt.float32
BF16 = mybir.dt.bfloat16
U32 = mybir.dt.uint32

P = 128
NB, SEQ, D = 16, 512, 128
NT = SEQ // P
TILES = NB * NT
LN_EPS = 1e-5
RMS_EPS = float(np.finfo(np.float32).eps)
PSUM_BANK = 512


class Mem:
    pass


def along(ap, axis, count):
    a = ap.unsqueeze(axis)
    shape = list(a.shape)
    shape[axis] = count
    return a.broadcast_to(shape)


def lora_moe_stage(nc, m, name, w, x_dram=None):
    G = 8
    PASSES = TILES // G
    E_TRUE, E_ALL, RANK = 8, 10, 16
    with ExitStack() as ctx:
        def sb(n, shape, dt=F32):
            return ctx.enter_context(nc.sbuf_tensor(f"{name}_{n}", shape, dt))

        def sem(n):
            return ctx.enter_context(nc.semaphore(f"{name}_{n}"))

        w_zg = sb("w_zg", [P, P + E_ALL])
        w_base = sb("w_base", [P, P])
        w_loraB = sb("w_loraB", [P, P])
        bias = sb("bias", [P, P])
        stats = sb("stats", [P, G, 6])
        mv = sb("mv", [P, G, 2])
        var_eps = sb("var_eps", [P, G])
        rstd = sb("rstd", [P, G])
        xn = sb("xn", [P, G, P])
        xT = sb("xT", [P, G, P])
        gmax = sb("gmax", [P, G])
        gexp = sb("gexp", [P, G, E_ALL])
        top = sb("top", [P, G, 8])
        idx = sb("idx", [P, G, 8], U32)
        idxf = sb("idxf", [P, G, 2])
        tw = sb("tw", [P, G, 2])
        den = sb("den", [P, G])
        rden = sb("rden", [P, G])
        hot0 = sb("hot0", [P, G, E_TRUE])
        hot1 = sb("hot1", [P, G, E_TRUE])
        ew = sb("ew", [P, G, E_TRUE])
        zw = sb("zw", [P, G, P])
        zwT = sb("zwT", [P, G, P])

        weights_in = sem("weights_in")
        x_in = sem("x_in")
        half_bias = sem("half_bias")
        var_ready = sem("var_ready")
        rstd_ready = sem("rstd_ready")
        xn_ready = sem("xn_ready")
        xT_psum = sem("xT_psum")
        xT_ready = sem("xT_ready")
        zg_ready = sem("zg_ready")
        gates_shifted = sem("gates_shifted")
        gates_exp = sem("gates_exp")
        zw_ready = sem("zw_ready")
        zwT_psum = sem("zwT_psum")
        zwT_ready = sem("zwT_ready")
        y_ready = sem("y_ready")

        ps_T = m.psum[:, 0:2, :].rearrange("p k (t c) -> p (k t) c", c=P)
        ps_zg = m.psum[:, 2:6, :].rearrange("p k (t c) -> p (k t) c", c=256)
        ps_y = m.psum[:, 6:8, :].rearrange("p k (t c) -> p (k t) c", c=P)
        x_of = m.x

        block = ctx.enter_context(nc.Block())

        @block.sync
        def _(sp):
            sp.dma_start(w_zg[:, 0:P], w["loraA_T"]).then_inc(weights_in, 16)
            sp.dma_start(w_zg[:, P:P + E_ALL], w["gate_T"]).then_inc(weights_in, 16)
            sp.dma_start(w_base[:, :], w["base_T"]).then_inc(weights_in, 16)
            sp.dma_start(w_loraB[:, :], w["loraB_T"]).then_inc(weights_in, 16)
            sp.dma_start(bias[:, :], w["bias"].partition_broadcast(P)).then_inc(weights_in, 16)
            if x_dram is not None:
                sp.dma_start(m.ident[:, :], w["ident"]).then_inc(weights_in, 16)
                sp.dma_start(m.iota8[:, :], w["iota8"]).then_inc(weights_in, 16)
                x_view = x_dram.rearrange("b (t p) d -> p (b t) d", p=P)
                sp.dma_start(x_of[:, 0:G, :], x_view[:, 0:G, :]).then_inc(x_in, 16)
                with sp.Fori(1, PASSES) as i:
                    sp.wait_ge(x_in, i * 16)
                    sp.dma_start(x_of[:, bass.ds(i * G, G), :], x_view[:, bass.ds(i * G, G), :]).then_inc(x_in, 16)

        n_weights = 16 * (7 if x_dram is not None else 5)

        @block.gpsimd
        def _(pool):
            with pool.Fori(0, PASSES) as i:
                pool.wait_ge(var_ready, i + 1)
                pool.tensor_tensor(rstd[:, :], var_eps[:, :], m.minus_half[:, 0:G], ALU.pow).then_inc(rstd_ready, 1)

        @block.scalar
        def _(act):
            with act.Fori(0, PASSES) as i:
                act.wait_ge(xT_psum, i + 1)
                act.activation(xT[:, :, :], ps_T, ACT.Copy).then_inc(xT_ready, 1)
                act.wait_ge(gates_shifted, i + 1)
                act.activation(gexp[:, :, :], gexp[:, :, :], ACT.Exp).then_inc(gates_exp, 1)
                act.wait_ge(zwT_psum, i + 1)
                act.activation(zwT[:, :, :], ps_T, ACT.Copy).then_inc(zwT_ready, 1)

        @block.tensor
        def _(pe):
            pe.wait_ge(weights_in, n_weights)
            with pe.Fori(0, PASSES) as i:
                pe.wait_ge(xn_ready, i + 1)
                for t in range(G):
                    last = pe.transpose(ps_T[:, t, :], xn[:, t, :], m.ident[:, :])
                last.then_inc(xT_psum, 1)
                pe.wait_ge(xT_ready, i + 1)
                for t in range(G):
                    last = pe.matmul(ps_zg[:, t, 0:P + E_ALL], xT[:, t, :], w_zg[:, :], start=True, stop=True)
                last.then_inc(zg_ready, 1)
                pe.wait_ge(zw_ready, i + 1)
                for t in range(G):
                    last = pe.transpose(ps_T[:, t, :], zw[:, t, :], m.ident[:, :])
                last.then_inc(zwT_psum, 1)
                pe.wait_ge(zwT_ready, i + 1)
                for t in range(G):
                    pe.matmul(ps_y[:, t, :], xT[:, t, :], w_base[:, :], start=True, stop=False)
                    last = pe.matmul(ps_y[:, t, :], zwT[:, t, :], w_loraB[:, :], start=False, stop=True)
                last.then_inc(y_ready, 1)

        @block.vector
        def _(dve):
            if x_dram is not None:
                dve.memset(m.minus_half[:, :], -0.5)
                dve.memset(m.half[:, :], 0.5)
                dve.memset(x_of[:, TILES:TILES + 2 * NT, :], 0.0)
            dve.wait_ge(weights_in, n_weights)
            dve.tensor_scalar(bias[:, :], bias[:, :], 0.5, None, ALU.mult).then_inc(half_bias, 1)
            dve.wait_ge(half_bias, 1)
            with dve.Fori(0, PASSES) as i:
                x = x_of[:, bass.ds(i * G, G), :]
                if x_dram is not None:
                    dve.wait_ge(x_in, i * 16 + 16)
                for t in range(G):
                    last = dve.bn_stats(stats[:, t, :], x_of[:, i * G + t, :])
                dve.drain()
                for t in range(G):
                    last = dve.bn_aggr(mv[:, t, :], stats[:, t, :])
                dve.drain()
                dve.tensor_scalar(var_eps[:, :], mv[:, :, 1], LN_EPS, None, ALU.add).then_inc(var_ready, 1)
                dve.wait_ge(rstd_ready, i + 1)
                for t in range(G):
                    last = dve.tensor_scalar(xn[:, t, :], x_of[:, i * G + t, :], mv[:, t, 0:1], rstd[:, t:t + 1],
                                             ALU.subtract, ALU.mult)
                last.then_inc(xn_ready, 1)
                dve.wait_ge(zg_ready, i + 1)
                dve.tensor_reduce(gmax[:, :], ps_zg[:, :, P:P + E_ALL], AX.X, ALU.max)
                dve.drain()
                dve.tensor_tensor(gexp[:, :, :], ps_zg[:, :, P:P + E_ALL], along(gmax[:, :], 2, E_ALL),
                                  ALU.subtract).then_inc(gates_shifted, 1)
                dve.wait_ge(gates_exp, i + 1)
                dve.memset(den[:, :], 0.0)
                for t in range(G):
                    last = dve.max(top[:, t, :], gexp[:, t, :])
                dve.drain()
                for t in range(G):
                    last = dve.max_index(idx[:, t, :], top[:, t, :], gexp[:, t, :])
                dve.drain()
                dve.tensor_copy(idxf[:, :, :], idx[:, :, 0:2])
                dve.drain()
                dve.scalar_tensor_tensor(out=tw[:, :, :], in0=idxf[:, :, :], scalar=float(E_TRUE),
                                         in1=top[:, :, 0:2], op0=ALU.is_lt, op1=ALU.mult)
                dve.drain()
                dve.tensor_tensor(den[:, :], tw[:, :, 0], tw[:, :, 1], ALU.add)
                dve.drain()
                dve.scalar_tensor_tensor(out=den[:, :], in0=den[:, :], scalar=0.0, in1=den[:, :],
                                         op0=ALU.is_le, op1=ALU.add)
                dve.drain()
                dve.reciprocal(rden[:, :], den[:, :])
                dve.drain()
                dve.scalar_tensor_tensor(out=tw[:, :, :], in0=tw[:, :, :], scalar=2.0,
                                         in1=along(rden[:, :], 2, 2), op0=ALU.mult, op1=ALU.mult)
                dve.drain()
                iota = along(m.iota8[:, :], 1, G)
                for k, hot in enumerate((hot0, hot1)):
                    last = dve.tensor_tensor(hot[:, :, :], iota, along(idxf[:, :, k], 2, E_TRUE), ALU.is_equal)
                dve.drain()
                for k, hot in enumerate((hot0, hot1)):
                    last = dve.tensor_tensor(hot[:, :, :], hot[:, :, :], along(tw[:, :, k], 2, E_TRUE), ALU.mult)
                dve.drain()
                dve.tensor_tensor(ew[:, :, :], hot0[:, :, :], hot1[:, :, :], ALU.add)
                dve.drain()
                dve.tensor_tensor(zw[:, :, :].rearrange("p t (e r) -> p t e r", r=RANK),
                                  ps_zg[:, :, 0:P].rearrange("p t (e r) -> p t e r", r=RANK),
                                  along(ew[:, :, :], 3, RANK), ALU.mult).then_inc(zw_ready, 1)
                dve.wait_ge(y_ready, i + 1)
                dve.scalar_tensor_tensor(out=x, in0=ps_y, scalar=0.5, in1=x, op0=ALU.mult, op1=ALU.add)
                dve.drain()
                dve.tensor_tensor(x, x, along(bias[:, :], 1, G), ALU.add)
                dve.drain()


def attention_stage(nc, m, name, w):
    H, DH = 16, 8
    N = SEQ
    SCALE = DH ** -0.5
    PAIRS = ((0, 0), (0, 1), (1, 0), (0, 2), (2, 0), (1, 1))
    K_QK = 72
    K_ALL = K_QK + 3
    UNITS = H * NT
    RING = 8
    V_W = 32
    with ExitStack() as ctx:
        def sb(n, shape, dt=F32):
            return ctx.enter_context(nc.sbuf_tensor(f"{name}_{n}", shape, dt))

        def sem(n):
            return ctx.enter_context(nc.semaphore(f"{name}_{n}"))

        w_proj = sb("w_proj", [P, 4, P])
        w_v = sb("w_v", [P, P])
        w_o = sb("w_o", [P, P])
        cos = sb("cos", [P, N])
        sin = sb("sin", [P, N])
        ident_b = sb("ident_b", [P, P], BF16)
        mask_qk = sb("mask_qk", [P, P], BF16)
        mask_kq = sb("mask_kq", [P, P], BF16)
        stats = sb("stats", [P, NT, 6])
        mv = sb("mv", [P, NT, 2])
        var_eps = sb("var_eps", [P, NT])
        rstd = sb("rstd", [P, NT])
        xn = sb("xn", [P, NT, P])
        xT = sb("xT", [P, N])
        rot = sb("rot", [P, N])
        rot_sin = sb("rot_sin", [P, N])
        parts = [sb("qparts", [P, 3, N], BF16), sb("kparts", [P, 3, N], BF16)]
        v_new = sb("v_new", [P, NT, P])
        qs = [sb(f"qs{k}", [K_ALL, H, N], BF16) for k in range(2)]
        ks = [sb(f"ks{k}", [K_ALL, H, N], BF16) for k in range(2)]
        v_aug = [sb(f"v_aug{k}", [P, NT, H, V_W]) for k in range(2)]
        rowmax = sb("rowmax", [P, NT, H])
        mparts = sb("mparts", [P, NT, P // H, H], BF16)
        mT = sb("mT", [3 * H, N], BF16)
        probs = sb("probs", [P, RING, N])
        oT = sb("oT", [P, N])
        inv = sb("inv", [P, NT, 4])
        o_tok = sb("o_tok", [P, NT, P])
        o_tokT = sb("o_tokT", [P, N])
        junk = sb("junk", [P, 4])

        weights_in = sem("weights_in")
        stacks_set = sem("stacks_set")
        var_ready = sem("var_ready")
        rstd_ready = sem("rstd_ready")
        xn_ready = sem("xn_ready")
        xT_psum = sem("xT_psum")
        xT_ready = sem("xT_ready")
        proj_psum = sem("proj_psum")
        rope_read = sem("rope_read")
        rot_used = sem("rot_used")
        parts_ready = sem("parts_ready")
        v_psum = sem("v_psum")
        v_read = sem("v_read")
        v_ready = sem("v_ready")
        stack_in = sem("stack_in")
        score_psum = sem("score_psum")
        max_read = sem("max_read")
        mparts_ready = sem("mparts_ready")
        mT_psum = sem("mT_psum")
        mT_ready = sem("mT_ready")
        m_in = sem("m_in")
        exp_psum = sem("exp_psum")
        exp_ready = sem("exp_ready")
        pv_done = sem("pv_done")
        o_read = sem("o_read")
        oT_psum = sem("oT_psum")
        o_norm = sem("o_norm")
        o_tokT_psum = sem("o_tokT_psum")
        o_tokT_ready = sem("o_tokT_ready")
        out_psum = sem("out_psum")
        x_done = sem("x_done")

        ps_exp = [m.psum[:, 0, :], m.psum[:, 1, :]]
        ps_score = [m.psum[:, 2, :], m.psum[:, 3, :]]
        ps_o = [m.psum[:, 4, :], m.psum[:, 5, :]]
        ps_a, ps_b = m.psum[:, 6, :], m.psum[:, 7, :]
        tiles = lambda bank: bank.rearrange("p (t c) -> p t c", c=P)
        ps_mT = m.psum[:, 7, 0:N // 2].bitcast(BF16)
        x_of = m.x
        BODIES = NB // 2
        BLOCKS = 2 * len(PAIRS)
        N_WEIGHTS = 16 * 8

        block = ctx.enter_context(nc.Block())

        @block.sync
        def _(sp):
            for dst, src in ((w_proj, "w_proj"), (w_v, "w_v"), (w_o, "wo_T"), (cos, "cos"), (sin, "sin"),
                             (ident_b, "ident_b"), (mask_qk, "mask_qk"), (mask_kq, "mask_kq")):
                sp.dma_start(dst[:], w[src]).then_inc(weights_in, 16)

            def stack(k, count):
                sp.wait_ge(parts_ready, count)
                for side, stacks in enumerate((qs, ks)):
                    for n, pair in enumerate(PAIRS):
                        sp.dma_start(stacks[k][n * DH:(n + 1) * DH, :, :],
                                     parts[side][:, pair[side], :]).then_inc(stack_in, 16)

            def maxima(k, count):
                sp.wait_ge(mT_ready, count)
                sp.dma_start(qs[k][K_QK:K_ALL, :, :], mT[:, :]).then_inc(m_in, 16)

            sp.wait_ge(stacks_set, 8)
            stack(0, 1)
            sp.wait_ge(stack_in, 16 * BLOCKS)
            stack(1, 2)
            maxima(0, 1)
            with sp.Fori(0, BODIES) as i:
                for k in range(2):
                    sp.wait_ge(exp_psum, (i * 2 + k) * UNITS + UNITS)
                    stack(k, i * 2 + (k + 3))
                    maxima(1 - k, i * 2 + (k + 2))
            sp.wait_ge(stack_in, 16 * BLOCKS * (NB + 2))
            sp.wait_ge(m_in, 16 * (NB + 1))

        @block.gpsimd
        def _(pool):
            for k in range(2):
                pool.memset(qs[k][:, :, :], 0.0).then_inc(stacks_set, 1)
                pool.memset(ks[k][:, :, :], -1.0).then_inc(stacks_set, 1)
                pool.memset(v_aug[k][:, :, :, :], 0.0).then_inc(stacks_set, 1)
                pool.drain()
                pool.memset(v_aug[k][:, :, :, DH:DH + 1], 1.0).then_inc(stacks_set, 1)

            def split(count):
                pool.wait_ge(var_ready, count)
                pool.tensor_tensor(rstd[:, :], var_eps[:, :], m.minus_half[:, 0:NT], ALU.pow).then_inc(rstd_ready, 1)
                for side in range(2):
                    part = parts[side]
                    pool.wait_ge(rope_read, count * 4 + (side * 2 - 2))
                    pool.tensor_tensor(rot[:, :], rot[:, :], rot_sin[:, :], ALU.add)
                    pool.drain()
                    pool.tensor_copy(part[:, 0, :], rot[:, :])
                    pool.drain()
                    pool.tensor_tensor(rot[:, :], rot[:, :], part[:, 0, :], ALU.subtract)
                    pool.drain()
                    pool.tensor_copy(part[:, 1, :], rot[:, :])
                    pool.drain()
                    pool.tensor_tensor(part[:, 2, :], rot[:, :], part[:, 1, :], ALU.subtract).then_inc(rot_used, 1)
                    if side == 1:
                        pool.drain()
                        pool.memset(junk[:, 0:1], 0.0).then_inc(parts_ready, 1)

            split(1)
            pool.wait_ge(stack_in, 16 * BLOCKS)
            split(2)
            with pool.Fori(0, BODIES) as i:
                for k in range(2):
                    pool.wait_ge(stack_in, i * (32 * BLOCKS) + 16 * BLOCKS * (k + 2))
                    split(i * 2 + (k + 3))

        @block.scalar
        def _(act):
            def turn(count):
                act.wait_ge(xT_psum, count)
                act.activation(xT[:, :], ps_a, ACT.Copy).then_inc(xT_ready, 1)

            def read_v(count):
                act.wait_ge(v_psum, count)
                act.activation(v_new[:, :, :], tiles(ps_a), ACT.Copy).then_inc(v_read, 1)

            act.activation(junk[:, 2:3], m.half[:, 0:1], ACT.Exp).then_inc(exp_ready, 1)
            act.activation(junk[:, 3:4], m.half[:, 0:1], ACT.Exp).then_inc(exp_ready, 1)
            act.activation(oT[:, 0:1], m.half[:, 0:1], ACT.Exp).then_inc(o_read, 1)
            act.activation(oT[:, 1:2], m.half[:, 0:1], ACT.Exp).then_inc(o_read, 1)
            act.drain()
            def values(k):
                act.activation(v_aug[k][:, :, :, 0:DH], v_new[:, :, :].rearrange("p t (h d) -> p t h d", d=DH),
                               ACT.Copy).then_inc(v_ready, 1)

            act.wait_ge(stacks_set, 8)
            for s in range(2):
                turn(s + 1)
                read_v(s + 1)
                act.drain()
                values(s)
            with act.Fori(0, BODIES) as i:
                for k in range(2):
                    def read_o(g):
                        act.wait_ge(pv_done, (i * 2 + k) * (4 * NT) + NT * (g + 1))
                        if g > 0:
                            act.wait_ge(oT_psum, (i * 2 + k) * 4 + g)
                        act.activation(oT[:, :], ps_o[g % 2], ACT.Copy).then_inc(o_read, 1)

                    for j in range(UNITS):
                        kt = j // 4 % NT
                        act.wait_ge(exp_psum, (i * 2 + k) * UNITS + (j + 1))
                        if j >= RING:
                            act.wait_ge(pv_done, (i * 2 + k) * (4 * NT) + (j // 4 - 1))
                        act.activation(probs[:, j % RING, 0:N - kt * P], ps_exp[j % 2][:, 0:N - kt * P], ACT.Exp,
                                       scale=SCALE).then_inc(exp_ready, 1)
                        if j == 4:
                            turn(i * 2 + (k + 3))
                        if j == 24:
                            read_v(i * 2 + (k + 3))
                        if j >= 22 and (j - 22) % 16 == 0:
                            read_o((j - 22) // 16)
                    read_o(3)
                    values(k)
                    act.wait_ge(o_tokT_psum, i * 2 + (k + 1))
                    act.activation(o_tokT[:, :], ps_a, ACT.Copy).then_inc(o_tokT_ready, 1)

        @block.tensor
        def _(pe):
            def turn(count):
                pe.wait_ge(xn_ready, count)
                for t in range(NT):
                    last = pe.transpose(ps_a[:, t * P:(t + 1) * P], xn[:, t, :], m.ident[:, :])
                last.then_inc(xT_psum, 1)

            def project(side, count):
                if side == 0:
                    pe.wait_ge(xT_ready, count)
                    pe.wait_ge(x_done, count)
                else:
                    pe.wait_ge(rope_read, count * 4 - 2)
                pe.matmul(ps_a, w_proj[:, 2 * side, :], xT[:, :], start=True, stop=True)
                pe.matmul(ps_b, w_proj[:, 2 * side + 1, :], xT[:, :], start=True, stop=True).then_inc(proj_psum, 1)

            def values(count):
                pe.wait_ge(rope_read, count * 4)
                for t in range(NT):
                    last = pe.matmul(ps_a[:, t * P:(t + 1) * P], xT[:, t * P:(t + 1) * P], w_v[:, :],
                                     start=True, stop=True)
                last.then_inc(v_psum, 1)

            def score(k, n, j):
                h, qt = j // NT, j % NT
                pe.wait_ge(max_read, n * UNITS + (j + 1))
                if j == 0:
                    pe.wait_ge(stack_in, n * (16 * BLOCKS) + 16 * BLOCKS)
                bank = ps_score[j % 2]
                pe.matmul(bank[:, 0:(qt + 1) * P], qs[k][0:K_QK, h, qt * P:(qt + 1) * P],
                          ks[k][0:K_QK, h, 0:(qt + 1) * P], start=True, stop=False)
                pe.matmul(bank[:, qt * P:(qt + 1) * P], ident_b[:, :], mask_qk[:, :],
                          start=False, stop=True).then_inc(score_psum, 1)

            def turn_maxima(n):
                pe.wait_ge(mparts_ready, n + 1)
                for t in range(NT):
                    last = pe.transpose(ps_mT[:, t * P:(t + 1) * P], mparts[:, t].rearrange("p a h -> p (a h)"),
                                        ident_b[:, :])
                last.then_inc(mT_psum, 1)

            for k in range(2):
                if k == 0:
                    pe.wait_ge(weights_in, N_WEIGHTS)
                turn(k + 1)
                if k == 1:
                    pe.wait_ge(v_read, 1)
                project(0, k + 1)
                project(1, k + 1)
                values(k + 1)
                if k == 0:
                    pe.wait_ge(v_read, 1)
            pe.wait_ge(v_read, 2)
            for j in range(UNITS):
                score(0, 0, j)
            turn_maxima(0)
            with pe.Fori(0, BODIES) as i:
                for k in range(2):
                    s = i * 2 + k

                    def exponent(j):
                        g, kt, hh = j // 16, j // 4 % NT, j % 4
                        n = N - kt * P
                        pe.wait_ge(exp_ready, s * UNITS + (j + 1))
                        if j == 0:
                            pe.wait_ge(m_in, s * 16 + 16)
                        bank = ps_exp[j % 2]
                        pe.matmul(bank[:, 0:n], ks[k][:, 4 * g + hh, kt * P:(kt + 1) * P],
                                  qs[k][:, 4 * g + hh, kt * P:N], start=True, stop=False)
                        pe.matmul(bank[:, 0:P], ident_b[:, :], mask_kq[:, :],
                                  start=False, stop=True).then_inc(exp_psum, 1)

                    def weigh(q):
                        g, kt = q // NT, q % NT
                        n = N - kt * P
                        pe.wait_ge(exp_ready, s * UNITS + (2 + 4 * q + 4))
                        if q == 0:
                            pe.wait_ge(v_ready, s + 1)
                        if kt == 0:
                            pe.wait_ge(o_read, s * 4 + (g + 1))
                        for hh in range(4):
                            last = pe.matmul(ps_o[g % 2][32 * hh:32 * hh + 32, kt * P:N], v_aug[k][:, kt, 4 * g + hh, :],
                                             probs[:, (4 * q + hh) % RING, 0:n], start=(kt == 0), stop=(kt == NT - 1),
                                             tile_position=(0, 32 * hh))
                        last.then_inc(pv_done, 1)

                    def turn_o(g):
                        pe.wait_ge(o_read, s * 4 + (2 + g + 1))
                        if g > 0:
                            pe.wait_ge(o_norm, s * 4 + g)
                        else:
                            pe.wait_ge(rope_read, (s + 3) * 4)
                        for t in range(NT):
                            last = pe.transpose(ps_b[:, t * P:(t + 1) * P], oT[:, t * P:(t + 1) * P], m.ident[:, :])
                        last.then_inc(oT_psum, 1)

                    for j in range(UNITS):
                        exponent(j)
                        score(1 - k, s + 1, j)
                        if j % 4 == 3 and j > 3:
                            weigh(j // 4 - 1)
                        if j == 2:
                            turn(s + 3)
                        if j == 6:
                            project(0, s + 3)
                        if j == 12:
                            project(1, s + 3)
                        if j == 20:
                            values(s + 3)
                        if j >= 26 and (j - 26) % 16 == 0:
                            turn_o((j - 26) // 16)
                    weigh(UNITS // 4 - 1)
                    turn_o(3)
                    pe.wait_ge(o_norm, s * 4 + 4)
                    turn_maxima(s + 1)
                    pe.wait_ge(v_read, s + 3)
                    for t in range(NT):
                        last = pe.transpose(ps_a[:, t * P:(t + 1) * P], o_tok[:, t, :], m.ident[:, :])
                    last.then_inc(o_tokT_psum, 1)
                    pe.wait_ge(o_tokT_ready, s + 1)
                    pe.wait_ge(mT_ready, s + 2)
                    for t in range(NT):
                        last = pe.matmul(ps_b[:, t * P:(t + 1) * P], o_tokT[:, t * P:(t + 1) * P], w_o[:, :],
                                         start=True, stop=True)
                    last.then_inc(out_psum, 1)

        @block.vector
        def _(dve):
            def layer_norm(tile, count):
                for t in range(NT):
                    dve.bn_stats(stats[:, t, :], x_of[:, tile + t, :])
                dve.drain()
                for t in range(NT):
                    dve.bn_aggr(mv[:, t, :], stats[:, t, :])
                dve.drain()
                dve.tensor_scalar(var_eps[:, :], mv[:, :, 1], LN_EPS, None, ALU.add).then_inc(var_ready, 1)
                dve.wait_ge(rstd_ready, count)
                for t in range(NT):
                    last = dve.tensor_scalar(xn[:, t, :], x_of[:, tile + t, :], mv[:, t, 0:1], rstd[:, t:t + 1],
                                             ALU.subtract, ALU.mult)
                last.then_inc(xn_ready, 1)

            def rotate(side, count):
                dve.wait_ge(proj_psum, count * 2 + (side - 1))
                if side == 1:
                    dve.wait_ge(rot_used, count * 2 - 1)
                dve.tensor_tensor(rot[:, :], ps_a, cos[:, :], ALU.mult).then_inc(rope_read, 1)
                dve.tensor_tensor(rot_sin[:, :], ps_b, sin[:, :], ALU.mult).then_inc(rope_read, 1)

            def row_max(n, j):
                h, qt = j // NT, j % NT
                dve.wait_ge(score_psum, n * UNITS + (j + 1))
                dve.tensor_reduce(rowmax[:, qt, h:h + 1], ps_score[j % 2][:, 0:(qt + 1) * P], AX.X,
                                  ALU.max).then_inc(max_read, 1)

            def split_maxima(n):
                dve.drain()
                dve.tensor_copy(mparts[:, :, 0, :], rowmax[:, :, :])
                dve.drain()
                dve.tensor_tensor(rowmax[:, :, :], rowmax[:, :, :], mparts[:, :, 0, :], ALU.subtract)
                dve.drain()
                dve.tensor_copy(mparts[:, :, 1, :], rowmax[:, :, :])
                dve.drain()
                dve.tensor_tensor(mparts[:, :, 2, :], rowmax[:, :, :], mparts[:, :, 1, :],
                                  ALU.subtract).then_inc(mparts_ready, 1)

            def read_maxima(n):
                dve.wait_ge(mT_psum, n + 1)
                if not isinstance(n, int):
                    dve.wait_ge(m_in, n * 16)
                dve.tensor_copy(mT[:, :], ps_mT[0:3 * H]).then_inc(mT_ready, 1)

            dve.memset(rowmax[:, 0, 0:1], 0.0).then_inc(max_read, 1)
            dve.memset(rowmax[:, 0, 1:2], 0.0).then_inc(max_read, 1)
            dve.memset(rowmax[:, 0, 2:3], 0.0).then_inc(x_done, 1)
            dve.memset(rowmax[:, 0, 3:4], 0.0).then_inc(x_done, 1)
            dve.memset(rowmax[:, 0, 4:5], 0.0).then_inc(x_done, 1)
            dve.memset(mparts[:, :, 3:P // H, :], 0.0)
            dve.drain()
            dve.wait_ge(weights_in, N_WEIGHTS)
            for s in range(2):
                layer_norm(s * NT, s + 1)
                if s == 1:
                    dve.wait_ge(rot_used, 2)
                rotate(0, s + 1)
                rotate(1, s + 1)
            for j in range(UNITS):
                row_max(0, j)
            split_maxima(0)
            read_maxima(0)
            with dve.Fori(0, BODIES) as i:
                for k in range(2):
                    s = i * 2 + k

                    def normalise(g):
                        dve.wait_ge(oT_psum, s * 4 + (g + 1))
                        o = tiles(ps_b).rearrange("p t (h c) -> p t h c", c=V_W)
                        dve.reciprocal(inv[:, :, :], o[:, :, :, DH])
                        dve.drain()
                        dve.tensor_tensor(o_tok[:, :, 4 * DH * g:4 * DH * (g + 1)].rearrange("p t (h d) -> p t h d", d=DH),
                                          o[:, :, :, 0:DH], along(inv[:, :, :], 3, DH), ALU.mult).then_inc(o_norm, 1)

                    layer_norm((s + 2) * NT, s + 3)
                    for j in range(UNITS):
                        row_max(s + 1, j)
                        if j == 9:
                            dve.wait_ge(rot_used, (s + 2) * 2)
                            rotate(0, s + 3)
                        if j == 18:
                            rotate(1, s + 3)
                        if j >= 30 and (j - 30) % 16 == 0:
                            normalise((j - 30) // 16)
                    split_maxima(s + 1)
                    normalise(3)
                    read_maxima(s + 1)
                    dve.wait_ge(out_psum, s + 1)
                    x = x_of[:, bass.ds(s * NT, NT), :]
                    dve.tensor_tensor(x, tiles(ps_b), x, ALU.add).then_inc(x_done, 1)
                    dve.drain()


def expert_stage(nc, m, name, w):
    G = NT
    PASSES = TILES // G
    N = G * P
    E_S, E_R, HID = 2, 8, 512
    E = E_S + E_R
    C = HID // P
    T_GATES, T_BIAS, T_NEXT = 2, 3, 6
    with ExitStack() as ctx:
        def sb(n, shape, dt=F32):
            return ctx.enter_context(nc.sbuf_tensor(f"{name}_{n}", shape, dt))

        def sem(n):
            return ctx.enter_context(nc.semaphore(f"{name}_{n}"))

        w1 = sb("w1", [P, E, HID])
        w2 = sb("w2", [P, E, C, P])
        b1 = sb("b1", [P, E * C])
        b2 = sb("b2", [E, P])
        cent = sb("cent", [P, E_R])
        g_col = sb("g_col", [P, 2])
        euler = sb("euler", [P, G, E_R])
        stats = sb("stats", [P, G, 6])
        mv = sb("mv", [P, G, 2])
        var_eps = sb("var_eps", [P, G])
        rstd = sb("rstd", [P, G])
        ms_eps = sb("ms_eps", [P, G])
        rms_inv = sb("rms_inv", [P, G])
        rms = sb("rms", [P, G])
        rr = sb("rr", [P, G])
        xn = sb("xn", [P, G, P])
        acc = sb("acc", [P, G, P])
        xT = sb("xT", [P, N])
        xsT = sb("xsT", [P, N])
        xrT = sb("xrT", [P, N])
        logit = sb("logit", [P, G, E_R])
        score = sb("score", [P, G, E_R])
        ssum = sb("ssum", [P, G])
        top = sb("top", [P, G, 8])
        idx = sb("idx", [P, G, 8], U32)
        idxf = sb("idxf", [P, G, 2])
        gk = sb("gk", [P, G, 2])
        hot0 = sb("hot0", [P, G, E_R])
        hot1 = sb("hot1", [P, G, E_R])
        gates = sb("gates", [P, G, E])
        gT = sb("gT", [E, N])
        h = sb("h", [P, 2, C, N])

        weights_in = sem("weights_in")
        pool_const = sem("pool_const")
        var_ready = sem("var_ready")
        rstd_ready = sem("rstd_ready")
        ms_ready = sem("ms_ready")
        rms_ready = sem("rms_ready")
        xn_ready = sem("xn_ready")
        xT_psum = sem("xT_psum")
        xT_ready = sem("xT_ready")
        logit_psum = sem("logit_psum")
        logit_ready = sem("logit_ready")
        exp_ready = sem("exp_ready")
        gates_ready = sem("gates_ready")
        gT_psum = sem("gT_psum")
        gT_ready = sem("gT_ready")
        bias_psum = sem("bias_psum")
        h_psum = sem("h_psum")
        h_ready = sem("h_ready")
        y_ready = sem("y_ready")
        y_used = sem("y_used")

        ps_h = m.psum[:, 0:C, :]
        ps_y = m.psum[:, C:C + 2, :].rearrange("p k (t c) -> p k t c", c=P)
        ps_T = m.psum[:, 6, :].rearrange("p (t c) -> p t c", c=P)
        ps_logit = m.psum[:, 6, 0:G * E_R].rearrange("p (t e) -> p t e", e=E_R)
        ps_gT = m.psum[0:E, 7, :]
        x_of = m.x

        block = ctx.enter_context(nc.Block())

        @block.sync
        def _(sp):
            for dst, src in ((w1, "w1"), (w2, "w2"), (b1, "b1"), (b2, "b2"), (cent, "cent"), (g_col, "g_col")):
                sp.dma_start(dst[:], w[src]).then_inc(weights_in, 16)

        N_WEIGHTS = 16 * 6

        @block.gpsimd
        def _(pool):
            pool.memset(euler[:, :, :], float(np.e)).then_inc(pool_const, 1)
            pool.wait_ge(pool_const, 1)

            def rms_of(count):
                pool.wait_ge(var_ready, count)
                pool.tensor_tensor(rstd[:, :], var_eps[:, :], m.minus_half[:, 0:G], ALU.pow).then_inc(rstd_ready, 1)
                pool.wait_ge(ms_ready, count)
                pool.tensor_tensor(rms_inv[:, :], ms_eps[:, :], m.minus_half[:, 0:G], ALU.pow)
                pool.tensor_tensor(rms[:, :], ms_eps[:, :], m.half[:, 0:G], ALU.pow).then_inc(rms_ready, 1)

            rms_of(1)
            with pool.Fori(0, PASSES) as i:
                pool.wait_ge(logit_ready, i + 1)
                pool.tensor_tensor(score[:, :, :], euler[:, :, :], logit[:, :, :], ALU.pow).then_inc(exp_ready, 1)
                rms_of(i + 2)

        @block.scalar
        def _(act):
            def turn(count):
                act.wait_ge(xT_psum, count)
                act.activation(xT[:, :], m.psum[:, 6, :], ACT.Copy)
                act.activation(xsT[:, :], m.psum[:, 6, :], ACT.Copy, scale=g_col[:, 0:1])
                act.activation(xrT[:, :], m.psum[:, 6, :], ACT.Copy, scale=g_col[:, 1:2]).then_inc(xT_ready, 1)

            act.wait_ge(weights_in, N_WEIGHTS)
            turn(1)
            with act.Fori(0, PASSES) as i:
                for e in range(E):
                    for c in range(C):
                        act.wait_ge(h_psum, i * (E * C) + (e * C + c + 1))
                        if e >= 2 and c == 0:
                            act.wait_ge(y_ready, i * E + (e - 1))
                        act.activation(h[:, e % 2, c, :], ps_h[:, c, :], ACT.Gelu,
                                       bias=b1[:, e * C + c:e * C + c + 1]).then_inc(h_ready, 1)
                    if e == T_GATES:
                        act.wait_ge(gT_psum, i + 1)
                        act.activation(gT[:, :], ps_gT, ACT.Copy).then_inc(gT_ready, 1)
                turn(i + 2)

        @block.tensor
        def _(pe):
            def turn(count):
                pe.wait_ge(xn_ready, count)
                for t in range(G):
                    last = pe.transpose(ps_T[:, t, :], xn[:, t, :], m.ident[:, :])
                last.then_inc(xT_psum, 1)

            pe.wait_ge(weights_in, N_WEIGHTS)
            turn(1)
            with pe.Fori(0, PASSES) as i:
                def up(e):
                    src = xsT if e < E_S else xrT
                    for c in range(C):
                        if e >= 1:
                            pe.wait_ge(h_ready, i * (E * C) + ((e - 1) * C + c + 1))
                        pe.matmul(ps_h[:, c, :], w1[:, e, c * P:(c + 1) * P], src[:, :],
                                  start=True, stop=True).then_inc(h_psum, 1)

                def down(e):
                    pe.wait_ge(h_ready, i * (E * C) + (e + 1) * C)
                    pe.wait_ge(y_used, i * E + (e + 1))
                    for t in range(G):
                        for c in range(C):
                            last = pe.matmul(ps_y[:, e % 2, t, :], h[:, e % 2, c, t * P:(t + 1) * P], w2[:, e, c, :],
                                             start=(c == 0), stop=(c == C - 1))
                    last.then_inc(y_ready, 1)

                pe.wait_ge(xT_ready, i + 1)
                for t in range(G):
                    last = pe.matmul(ps_logit[:, t, :], xT[:, t * P:(t + 1) * P], cent[:, :], start=True, stop=True)
                last.then_inc(logit_psum, 1)
                up(0)
                for e in range(1, E):
                    up(e)
                    if e == T_GATES:
                        pe.wait_ge(gates_ready, i + 1)
                        for t in range(G):
                            last = pe.transpose(ps_gT[:, t * P:(t + 1) * P], gates[:, t, :], m.ident[:, :])
                        last.then_inc(gT_psum, 1)
                    if e == T_BIAS:
                        pe.wait_ge(gT_ready, i + 1)
                        for t in range(G):
                            last = pe.matmul(ps_T[:, t, :], gT[:, t * P:(t + 1) * P], b2[:, :], start=True, stop=True)
                        last.then_inc(bias_psum, 1)
                    if e == E - 1:
                        turn(i + 2)
                    down(e - 1)
                down(E - 1)

        @block.vector
        def _(dve):
            def layer_norm(tile, count):
                for t in range(G):
                    dve.bn_stats(stats[:, t, :], x_of[:, tile + t, :])
                dve.drain()
                for t in range(G):
                    dve.bn_aggr(mv[:, t, :], stats[:, t, :])
                dve.drain()
                dve.tensor_scalar(var_eps[:, :], mv[:, :, 1], LN_EPS, None, ALU.add).then_inc(var_ready, 1)
                dve.wait_ge(rstd_ready, count)
                dve.tensor_tensor(ms_eps[:, :], mv[:, :, 1], rstd[:, :], ALU.mult)
                dve.drain()
                dve.tensor_tensor(ms_eps[:, :], ms_eps[:, :], rstd[:, :], ALU.mult)
                dve.drain()
                dve.tensor_scalar(ms_eps[:, :], ms_eps[:, :], RMS_EPS, None, ALU.add).then_inc(ms_ready, 1)
                dve.wait_ge(rms_ready, count)
                dve.tensor_tensor(rr[:, :], rstd[:, :], rms_inv[:, :], ALU.mult)
                dve.drain()
                for t in range(G):
                    last = dve.tensor_scalar(xn[:, t, :], x_of[:, tile + t, :], mv[:, t, 0:1], rr[:, t:t + 1],
                                             ALU.subtract, ALU.mult)
                last.then_inc(xn_ready, 1)

            dve.memset(gates[:, :, :], 1.0).then_inc(y_used, 1)
            dve.memset(idxf[:, :, :], 0.0).then_inc(y_used, 1)
            layer_norm(0, 1)
            with dve.Fori(0, PASSES) as i:
                for t in range(G):
                    dve.tensor_scalar(acc[:, t, :], x_of[:, i * G + t, :], mv[:, t, 0:1], rstd[:, t:t + 1],
                                      ALU.subtract, ALU.mult)
                dve.wait_ge(logit_psum, i + 1)
                dve.scalar_tensor_tensor(out=logit[:, :, :], in0=ps_logit, scalar=-1.0,
                                         in1=along(rms[:, :], 2, E_R), op0=ALU.mult, op1=ALU.mult).then_inc(logit_ready, 1)
                dve.wait_ge(exp_ready, i + 1)
                dve.tensor_scalar(score[:, :, :], score[:, :, :], 1.0, None, ALU.add)
                dve.drain()
                dve.reciprocal(score[:, :, :], score[:, :, :])
                dve.drain()
                dve.tensor_reduce(ssum[:, :], score[:, :, :], AX.X, ALU.add)
                for t in range(G):
                    dve.max(top[:, t, :], score[:, t, :])
                dve.drain()
                for t in range(G):
                    dve.max_index(idx[:, t, :], top[:, t, :], score[:, t, :])
                dve.reciprocal(ssum[:, :], ssum[:, :])
                dve.drain()
                dve.tensor_copy(idxf[:, :, :], idx[:, :, 0:2])
                dve.tensor_tensor(gk[:, :, :], top[:, :, 0:2], along(ssum[:, :], 2, 2), ALU.mult)
                dve.drain()
                for k, hot in enumerate((hot0, hot1)):
                    dve.tensor_tensor(hot[:, :, :], along(m.iota8[:, :], 1, G), along(idxf[:, :, k], 2, E_R), ALU.is_equal)
                dve.drain()
                for k, hot in enumerate((hot0, hot1)):
                    dve.tensor_tensor(hot[:, :, :], hot[:, :, :], along(gk[:, :, k], 2, E_R), ALU.mult)
                dve.drain()
                dve.tensor_tensor(gates[:, :, E_S:E], hot0[:, :, :], hot1[:, :, :], ALU.add).then_inc(gates_ready, 1)
                for e in range(E):
                    dve.wait_ge(y_ready, i * E + (e + 1))
                    if e < E_S:
                        dve.tensor_tensor(acc[:, :, :], ps_y[:, e % 2], acc[:, :, :], ALU.add).then_inc(y_used, 1)
                    else:
                        for t in range(G):
                            last = dve.scalar_tensor_tensor(out=acc[:, t, :], in0=ps_y[:, e % 2, t, :],
                                                            scalar=gates[:, t, e:e + 1], in1=acc[:, t, :],
                                                            op0=ALU.mult, op1=ALU.add)
                        last.then_inc(y_used, 1)
                    dve.drain()
                    if e == T_GATES:
                        dve.wait_ge(bias_psum, i + 1)
                        dve.tensor_tensor(acc[:, :, :], ps_T, acc[:, :, :], ALU.add)
                        dve.drain()
                    if e == T_NEXT:
                        layer_norm(i * G + G, i + 2)
                x = x_of[:, bass.ds(i * G, G), :]
                dve.scalar_tensor_tensor(out=x, in0=acc[:, :, :], scalar=0.5, in1=x, op0=ALU.mult, op1=ALU.add)
                dve.drain()


def gla_stage(nc, m, name, w):
    DH = 8
    N = SEQ
    SCALE = DH ** -0.5
    DV_BANKS = 4
    TERMS = DH + 1
    with ExitStack() as ctx:
        def sb(n, shape, dt=F32):
            return ctx.enter_context(nc.sbuf_tensor(f"{name}_{n}", shape, dt))

        def sem(n):
            return ctx.enter_context(nc.semaphore(f"{name}_{n}"))

        w_qf = sb("w_qf", [P, 2 * P])
        w_i = sb("w_i", [P, P])
        w_irep = sb("w_irep", [P, DH, P])
        w_orep = sb("w_orep", [P, DH, P])
        w_o = sb("w_o", [P, P])
        head_ones = sb("head_ones", [P, P])
        stats = sb("stats", [P, NT, 6])
        mv = sb("mv", [P, NT, 2])
        var_eps = sb("var_eps", [P, NT])
        rstd = sb("rstd", [P, NT])
        xn = sb("xn", [P, NT, P])
        xT = sb("xT", [P, N])
        dxT = [sb(f"dxT{k}", [P, N]) for k in range(2)]
        xTk = [sb(f"xT{k}", [P, N]) for k in range(2)]
        nmax = sb("nmax", [P, 2 * NT])
        qf = sb("qf", [P, 2 * NT, P])
        qfsum = sb("qfsum", [P, 2 * NT])
        qfinv = sb("qfinv", [P, 2 * NT])
        qT = [sb(f"qT{k}", [P, N]) for k in range(2)]
        pT = [sb(f"pT{k}", [P, N]) for k in range(2)]
        vT = sb("vT", [P, N])
        state = [sb(f"state{k}", [P, TERMS, N]) for k in range(2)]

        weights_in = sem("weights_in")
        var_ready = sem("var_ready")
        rstd_ready = sem("rstd_ready")
        xn_ready = sem("xn_ready")
        xT_psum = sem("xT_psum")
        xT_ready = sem("xT_ready")
        dx_ready = sem("dx_ready")
        qf_psum = sem("qf_psum")
        nmax_ready = sem("nmax_ready")
        qf_exp = sem("qf_exp")
        qf_ready = sem("qf_ready")
        qpT_psum = sem("qpT_psum")
        qpT_ready = sem("qpT_ready")
        dv_psum = sem("dv_psum")
        dv_used = sem("dv_used")
        o_used = sem("o_used")
        term_ready = sem("term_ready")
        vT_ready = sem("vT_ready")
        o_psum = sem("o_psum")

        ps_T = m.psum[:, 0, :]
        ps_qf = m.psum[:, 1:3, :].rearrange("p k (t c) -> p (k t) c", c=P)
        ps_qT, ps_pT = m.psum[:, 1, :], m.psum[:, 2, :]
        ps_dv = [m.psum[:, 3 + k, :] for k in range(DV_BANKS)]
        ps_o = m.psum[:, 7, :].rearrange("p (t c) -> p t c", c=P)
        x_of = m.x
        SCANS = DH + 2

        block = ctx.enter_context(nc.Block())

        @block.sync
        def _(sp):
            for dst, src in ((w_qf, "w_qf"), (w_i, "w_i"), (w_irep, "w_irep"), (w_orep, "w_orep"),
                             (w_o, "w_o"), (head_ones, "head_ones")):
                sp.dma_start(dst[:], w[src]).then_inc(weights_in, 16)

        N_WEIGHTS = 16 * 6
        BODIES = NB // 2

        @block.gpsimd
        def _(pool):
            def inv_std(count):
                pool.wait_ge(var_ready, count)
                pool.tensor_tensor(rstd[:, :], var_eps[:, :], m.minus_half[:, 0:NT], ALU.pow).then_inc(rstd_ready, 1)

            inv_std(1)
            with pool.Fori(0, BODIES) as i:
                for k in range(2):
                    inv_std(i * 2 + (k + 2))
                    for v in range(DH):
                        pool.wait_ge(dv_used, (i * 2 + k) * TERMS + (DV_BANKS + v + 1))
                        pool.tensor_tensor(state[k][:, v, :], state[k][:, v, :], qT[k][:, :],
                                           ALU.mult).then_inc(term_ready, 1)

        @block.scalar
        def _(act):
            def turn(k, count):
                act.wait_ge(xT_psum, count)
                act.activation(xTk[k][:, :], ps_T, ACT.Copy).then_inc(xT_ready, 1)

            def softmax(k, count):
                act.wait_ge(nmax_ready, count)
                for j in range(2 * NT):
                    last = act.activation(qf[:, j, :], ps_qf[:, j, :], ACT.Exp, bias=nmax[:, j:j + 1],
                                          accum_out=qfsum[:, j:j + 1])
                last.then_inc(qf_exp, 1)

            def turn_qp(k, count):
                act.wait_ge(qpT_psum, count)
                act.activation(qT[k][:, :], ps_qT, ACT.Copy)
                act.activation(pT[k][:, :], ps_pT, ACT.Copy).then_inc(qpT_ready, 1)

            turn(0, 1)
            softmax(0, 1)
            turn_qp(0, 1)
            with act.Fori(0, BODIES) as i:
                for k in range(2):
                    nxt = i * 2 + (k + 2)
                    turn(1 - k, nxt)
                    softmax(1 - k, nxt)
                    turn_qp(1 - k, nxt)
                    act.wait_ge(dv_psum, (i * 2 + k) * SCANS + SCANS)
                    act.activation(vT[:, :], ps_dv[(k * SCANS + SCANS - 1) % DV_BANKS], ACT.Copy).then_inc(vT_ready, 1)

        @block.tensor
        def _(pe):
            def turn(count):
                pe.wait_ge(xn_ready, count)
                for t in range(NT):
                    last = pe.transpose(ps_T[:, t * P:(t + 1) * P], xn[:, t, :], m.ident[:, :])
                last.then_inc(xT_psum, 1)

            def logits(k, count):
                pe.wait_ge(xT_ready, count)
                for t in range(NT):
                    last = pe.matmul(m.psum[:, 1 + t // 2, (t % 2) * 256:(t % 2) * 256 + 256],
                                     xTk[k][:, t * P:(t + 1) * P], w_qf[:, :], start=True, stop=True)
                last.then_inc(qf_psum, 1)

            def turn_qp(count):
                pe.wait_ge(qf_ready, count)
                for t in range(NT):
                    pe.transpose(ps_qT[:, t * P:(t + 1) * P], qf[:, 2 * t, :], m.ident[:, :])
                    last = pe.transpose(ps_pT[:, t * P:(t + 1) * P], qf[:, 2 * t + 1, :], m.ident[:, :])
                last.then_inc(qpT_psum, 1)

            def output(i, k):
                pe.wait_ge(term_ready, (i * 2 + k) * DH + DH)
                pe.wait_ge(dv_used, (i * 2 + k) * TERMS + (DV_BANKS + TERMS))
                pe.wait_ge(o_used, i * 2 + (k + 1))
                for t in range(NT):
                    for v in range(TERMS):
                        last = pe.matmul(ps_o[:, t, :], state[k][:, v, t * P:(t + 1) * P],
                                         w_orep[:, v, :] if v < DH else w_o[:, :], start=(v == 0), stop=(v == DH))
                last.then_inc(o_psum, 1)

            pe.wait_ge(weights_in, N_WEIGHTS)
            turn(1)
            logits(0, 1)
            turn_qp(1)
            with pe.Fori(0, BODIES) as i:
                for k in range(2):
                    nxt = i * 2 + (k + 2)

                    def scan_input(j):
                        n = k * SCANS + j
                        pe.wait_ge(dv_used, (i * 2 + k) * TERMS + (DV_BANKS + (-2, -1, 0, 0, 1, 2, 3, 4, 5, 6)[j]))
                        if j == 0:
                            pe.wait_ge(dx_ready, i * 2 + (k + 1))
                        if j < DH:
                            mm = pe.matmul(ps_dv[n % DV_BANKS], w_irep[:, j, :], dxT[k][:, :], start=True, stop=True)
                        elif j == DH:
                            mm = pe.matmul(ps_dv[n % DV_BANKS], head_ones[:, :], qT[k][:, :], start=True, stop=True)
                        else:
                            mm = pe.matmul(ps_dv[n % DV_BANKS], w_i[:, :], xTk[k][:, :], start=True, stop=True)
                        mm.then_inc(dv_psum, 1)

                    scan_input(0)
                    turn(nxt)
                    for j in (1, 2, 3):
                        scan_input(j)
                    logits(1 - k, nxt)
                    for j in (4, 5, 6):
                        scan_input(j)
                    turn_qp(nxt)
                    for j in (7, 8, 9):
                        scan_input(j)
                output(i, 0)
                output(i, 1)

        @block.vector
        def _(dve):
            def layer_norm(tile, count):
                for t in range(NT):
                    dve.bn_stats(stats[:, t, :], x_of[:, tile + t, :])
                dve.drain()
                for t in range(NT):
                    dve.bn_aggr(mv[:, t, :], stats[:, t, :])
                dve.drain()
                dve.tensor_scalar(var_eps[:, :], mv[:, :, 1], LN_EPS, None, ALU.add).then_inc(var_ready, 1)

            def normalise(tile, count):
                dve.wait_ge(rstd_ready, count)
                for t in range(NT):
                    last = dve.tensor_scalar(xn[:, t, :], x_of[:, tile + t, :], mv[:, t, 0:1], rstd[:, t:t + 1],
                                             ALU.subtract, ALU.mult)
                last.then_inc(xn_ready, 1)

            def difference(k, count):
                dve.wait_ge(xT_ready, count)
                dve.tensor_scalar(dxT[k][:, 0:1], xTk[k][:, 0:1], -1.0, None, ALU.mult)
                dve.tensor_tensor(dxT[k][:, 1:N], xTk[k][:, 0:N - 1], xTk[k][:, 1:N], ALU.subtract).then_inc(dx_ready, 1)

            def maxima(count):
                dve.wait_ge(qf_psum, count)
                dve.tensor_reduce(nmax[:, :], ps_qf, AX.X, ALU.max)
                dve.drain()
                dve.tensor_scalar(nmax[:, :], nmax[:, :], -1.0, None, ALU.mult).then_inc(nmax_ready, 1)

            def divide(count):
                dve.wait_ge(qf_exp, count)
                dve.reciprocal(qfinv[:, :], qfsum[:, :])
                dve.drain()
                for j in range(2 * NT):
                    last = dve.tensor_scalar(qf[:, j, :], qf[:, j, :], qfinv[:, j:j + 1],
                                             SCALE if j % 2 == 0 else 1.0, ALU.mult, ALU.mult)
                last.then_inc(qf_ready, 1)

            dve.wait_ge(weights_in, N_WEIGHTS)
            for k in range(DV_BANKS):
                dve.memset(nmax[:, k:k + 1], 0.0).then_inc(dv_used, 1)
            dve.memset(nmax[:, DV_BANKS:DV_BANKS + 1], 0.0).then_inc(o_used, 1)
            dve.drain()
            layer_norm(0, 1)
            normalise(0, 1)
            difference(0, 1)
            maxima(1)
            divide(1)
            with dve.Fori(0, BODIES) as i:
                def residual(i, k):
                    x = x_of[:, bass.ds((i * 2 + k) * NT, NT), :]
                    dve.wait_ge(o_psum, i * 2 + (k + 1))
                    dve.tensor_tensor(x, ps_o, x, ALU.add).then_inc(o_used, 1)
                    dve.drain()

                for k in range(2):
                    nxt = i * 2 + (k + 2)
                    tile = (i * 2 + (k + 1)) * NT

                    def scan(v):
                        n = k * SCANS + v
                        if v == 0:
                            dve.wait_ge(qpT_ready, i * 2 + (k + 1))
                        dve.wait_ge(dv_psum, i * (2 * SCANS) + (n + 1))
                        dve.tensor_tensor_scan(state[k][:, v, :], ps_dv[n % DV_BANKS], pT[k][:, :], 0.0,
                                               ALU.add, ALU.mult).then_inc(dv_used, 1)

                    layer_norm(tile, nxt)
                    scan(0)
                    normalise(tile, nxt)
                    scan(1)
                    scan(2)
                    difference(1 - k, nxt)
                    scan(3)
                    maxima(nxt)
                    scan(4)
                    scan(5)
                    divide(nxt)
                    scan(6)
                    scan(7)
                    dve.wait_ge(vT_ready, i * 2 + (k + 1))
                    dve.tensor_tensor(state[k][:, DH, :], ps_dv[(k * SCANS + DH) % DV_BANKS], vT[:, :],
                                      ALU.mult).then_inc(dv_used, 1)
                residual(i, 0)
                residual(i, 1)


def store_stage(nc, m, out):
    with ExitStack() as ctx:
        stored = ctx.enter_context(nc.semaphore("stored"))
        block = ctx.enter_context(nc.Block())

        @block.sync
        def _(sp):
            sp.dma_start(out.rearrange("b (t p) d -> p (b t) d", p=P), m.x[:, 0:TILES, :]).then_inc(stored, 16)
            sp.wait_ge(stored, 16)


def build(nc, c, out):
    with ExitStack() as ctx:
        m = Mem()
        m.x = ctx.enter_context(nc.sbuf_tensor("x", [P, TILES + 2 * NT, D], F32))
        m.ident = ctx.enter_context(nc.sbuf_tensor("ident", [P, P], F32))
        m.iota8 = ctx.enter_context(nc.sbuf_tensor("iota8", [P, 8], F32))
        m.minus_half = ctx.enter_context(nc.sbuf_tensor("minus_half", [P, 8], F32))
        m.half = ctx.enter_context(nc.sbuf_tensor("half", [P, 8], F32))
        m.psum = ctx.enter_context(nc.psum_tensor("psum", [P, 8, PSUM_BANK], F32))
        lora = {k: c[k] for k in ("loraA_T", "gate_T", "base_T", "loraB_T", "bias", "ident", "iota8")}
        lora_moe_stage(nc, m, "ffn0a", lora, x_dram=c["x"])
        experts = {k: c[k] for k in ("w1", "w2", "b1", "b2", "cent", "g_col")}
        attn = {k: c[k] for k in ("w_proj", "w_v", "wo_T", "cos", "sin", "ident_b", "mask_qk", "mask_kq")}
        gla = {k: c[k] for k in ("w_qf", "w_i", "w_irep", "w_orep", "w_o", "head_ones")}
        attention_stage(nc, m, "attn", attn)
        lora_moe_stage(nc, m, "ffn0b", lora)
        expert_stage(nc, m, "ffn1a", experts)
        gla_stage(nc, m, "gla", gla)
        expert_stage(nc, m, "ffn1b", experts)
        store_stage(nc, m, out)


def layout(inputs):
    a = {k: np.asarray(v) for k, v in inputs.items()}
    f = lambda v: np.ascontiguousarray(v)
    c = {"x": a["L0_attn_x"]}
    c["loraA_T"] = a["L0_ffn_lora_A"].reshape(P, D).T
    c["gate_T"] = a["L0_ffn_gate_w"].T
    c["base_T"] = a["L0_ffn_base_w"].T
    c["loraB_T"] = a["L0_ffn_lora_B"].transpose(0, 2, 1).reshape(P, D)
    c["bias"] = a["L0_ffn_base_b"]
    c["ident"] = np.eye(P, dtype=np.float32)
    c["iota8"] = np.tile(np.arange(8, dtype=np.float32), (P, 1))
    w1 = np.concatenate([a["L1_ffn_W1_s"], a["L1_ffn_W1_r"]])
    w2 = np.concatenate([a["L1_ffn_W2_s"], a["L1_ffn_W2_r"]])
    b1 = np.concatenate([a["L1_ffn_b1_s"], a["L1_ffn_b1_r"]])
    c["w1"] = w1.transpose(1, 0, 2)
    c["w2"] = w2.reshape(10, 4, P, D).transpose(2, 0, 1, 3)
    c["b1"] = b1.reshape(40, P).T
    c["b2"] = np.concatenate([a["L1_ffn_b2_s"], a["L1_ffn_b2_r"]])
    c["cent"] = a["L1_ffn_centroids"]
    c["g_col"] = np.stack([a["L1_ffn_g_shared"], a["L1_ffn_g_routed"]], axis=1)
    c["w_qf"] = np.concatenate([a["L1_attn_Wq"], a["L1_attn_Wf"]], axis=1)
    c["w_i"] = a["L1_attn_Wi"]
    c["w_irep"] = np.repeat(a["L1_attn_Wi"].reshape(D, 16, 1, 8), 8, axis=2).transpose(0, 3, 1, 2).reshape(D, 8, P)
    c["w_orep"] = np.repeat(a["L1_attn_Wo"].reshape(16, 1, 8, D), 8, axis=1).transpose(0, 1, 2, 3).reshape(P, 8, D)
    c["w_o"] = a["L1_attn_Wo"]
    c["head_ones"] = np.kron(np.eye(16, dtype=np.float32), np.ones((8, 8), np.float32))
    wq, wk, wv = a["L0_attn_W_qkv"].reshape(3, 16, 8, D)
    by_d = lambda t: t.transpose(1, 0, 2).reshape(P, D).T
    swapped = lambda t: t.reshape(16, 4, 2, D)[:, :, ::-1].reshape(16, 8, D)
    c["w_proj"] = np.stack([by_d(wq), by_d(swapped(wq)), by_d(wk), by_d(swapped(wk))], axis=1)
    c["w_v"] = wv.reshape(P, D).T
    c["wo_T"] = a["L0_attn_W_o"].T
    inv_freq = np.float32(10000.0) ** (np.arange(0, 8, 2, dtype=np.float32) / np.float32(8))
    ang = np.arange(SEQ, dtype=np.float32)[None, :] / inv_freq[:, None]
    c["cos"] = np.repeat(np.repeat(np.cos(ang), 2, axis=0), 16, axis=0)
    sin = np.stack([-np.sin(ang), np.sin(ang)], axis=1).reshape(8, SEQ)
    c["sin"] = np.repeat(sin, 16, axis=0)
    BIG = -1e30
    bf = mybir.dt.np(BF16)
    c["ident_b"] = np.eye(P, dtype=np.float32).astype(bf)
    c["mask_qk"] = np.triu(np.full((P, P), BIG, np.float32), 1).astype(bf)
    c["mask_kq"] = np.tril(np.full((P, P), BIG, np.float32), -1).astype(bf)
    return {k: f(v) for k, v in c.items()}


def kernel(**inputs):
    import concourse.bacc as bacc
    from concourse.bass_utils import run_bass_kernel_spmd

    nc = bacc.Bacc("TRN2", target_bir_lowering=False, num_devices=1)
    arrays = {f"in_{k}": v for k, v in layout(inputs).items()}
    c = {k[3:]: nc.dram_tensor(k, v.shape, mybir.dt.from_np(v.dtype), kind="ExternalInput").ap()
         for k, v in arrays.items()}
    nc.disable_value_cache = True
    out = nc.dram_tensor("out_0", (NB, SEQ, D), F32, kind="ExternalOutput").ap()
    build(nc, c, out)
    return run_bass_kernel_spmd(nc, [arrays], core_ids=[0]).results[0]["out_0"]
```

```python
from contextlib import ExitStack

import numpy as np

import concourse.bass as bass
from concourse import mybir

ALU = mybir.AluOpType
ACT = mybir.ActivationFunctionType
AX = mybir.AxisListType
F32 = mybir.dt.float32
F32R = mybir.dt.float32r
BF16 = mybir.dt.bfloat16
U32 = mybir.dt.uint32

P = 128
NB, SEQ, D = 16, 512, 128
NT = SEQ // P
TILES = NB * NT
LN_EPS = 1e-5
RMS_EPS = float(np.finfo(np.float32).eps)
PSUM_BANK = 512


class Mem:
    pass


def along(ap, axis, count):
    a = ap.unsqueeze(axis)
    shape = list(a.shape)
    shape[axis] = count
    return a.broadcast_to(shape)


class Experts:
    E, HID = 10, 512
    JOBS = 2 * E
    RING = 5

    def __init__(self, nc, ctx, w):
        def sb(n, shape, dt=F32):
            return ctx.enter_context(nc.sbuf_tensor(f"experts_{n}", shape, dt))

        self.nc, self.w = nc, w
        self.high = sb("high", [P, self.JOBS, self.HID], F32R)
        self.low = sb("low", [P, self.JOBS, self.HID], F32R)
        self.b1 = sb("b1", [P, self.E * self.HID // P])
        self.b2 = sb("b2", [P, self.E])
        self.cent = sb("cent", [P, 8])
        self.select = sb("select", [P, 8, P], F32R)

    def allocate(self, own):
        nc, R = self.nc, self.RING
        self.raw = own.enter_context(nc.sbuf_tensor("experts_raw", [P, R, self.HID], F32))
        self.scaled = own.enter_context(nc.sbuf_tensor("experts_scaled", [P, R, self.HID], F32))
        self.select_raw = own.enter_context(nc.sbuf_tensor("experts_select_raw", [P, 8, P], F32))
        self.gain = own.enter_context(nc.sbuf_tensor("experts_gain", [P, self.JOBS], F32))
        self.small_in = own.enter_context(nc.semaphore("experts_small_in"))
        self.raw_in = [own.enter_context(nc.semaphore(f"experts_raw_in{r}")) for r in range(R)]
        self.scaled_ready = own.enter_context(nc.semaphore("experts_scaled_ready"))
        self.high_ready = own.enter_context(nc.semaphore("experts_high_ready"))
        self.low_ready = own.enter_context(nc.semaphore("experts_low_ready"))

    def load(self, sp):
        w, R = self.w, self.RING
        for dst, src in ((self.b1, "b1"), (self.b2, "b2"), (self.cent, "cent"), (self.gain, "gain"),
                         (self.select_raw, "select")):
            sp.dma_start(dst[:], w[src]).then_inc(self.small_in, 16)
        for r in range(R):
            sp.dma_start(self.raw[:, r, :], w["w12"][:, r, :]).then_inc(self.raw_in[r], 16)
        with sp.Fori(1, self.JOBS // R) as i:
            for r in range(R):
                sp.wait_ge(self.high_ready, i * R + (r + 1 - R))
                sp.dma_start(self.raw[:, r, :], w["w12"][:, bass.ds(i * R + r, 1), :]).then_inc(self.raw_in[r], 16)

    def split_high(self, act, r, i):
        job = i * self.RING + r
        act.wait_ge(self.raw_in[r], i * 16 + 16)
        if not isinstance(i, int) or i > 0:
            act.wait_ge(self.low_ready, job - (self.RING - 1))
        gain = self.gain[:, bass.ds(job, 1)]
        act.activation(self.scaled[:, r, :], self.raw[:, r, :], ACT.Copy, scale=gain).then_inc(self.scaled_ready, 1)
        act.activation(self.high[:, bass.ds(job, 1), :], self.raw[:, bass.ds(r, 1), :], ACT.Copy,
                       scale=gain).then_inc(self.high_ready, 1)

    def split_low(self, pool, r, i):
        job = i * self.RING + r
        pool.wait_ge(self.scaled_ready, job + 1)
        pool.wait_ge(self.high_ready, job + 1)
        pool.tensor_tensor(self.low[:, bass.ds(job, 1), :], self.scaled[:, bass.ds(r, 1), :],
                           self.high[:, bass.ds(job, 1), :].bitcast(F32), ALU.subtract).then_inc(self.low_ready, 1)


def lora_moe_stage(nc, m, name, w, x_dram=None, experts=None):
    G = 8
    PASSES = TILES // G
    E_TRUE, E_ALL, RANK = 8, 10, 16
    with ExitStack() as ctx:
        def sb(n, shape, dt=F32):
            return ctx.enter_context(nc.sbuf_tensor(f"{name}_{n}", shape, dt))

        def sem(n):
            return ctx.enter_context(nc.semaphore(f"{name}_{n}"))

        w_zg = sb("w_zg", [P, P + E_ALL])
        w_base = sb("w_base", [P, P])
        w_loraB = sb("w_loraB", [P, P])
        bias = sb("bias", [P, P])
        stats = sb("stats", [P, G, 6])
        mv = sb("mv", [P, G, 2])
        var_eps = sb("var_eps", [P, G])
        rstd = sb("rstd", [P, G])
        xn = sb("xn", [P, G, P])
        xT = [sb(f"xT{k}", [P, G, P]) for k in range(2)]
        gmax = sb("gmax", [P, G])
        gexp = sb("gexp", [P, G, E_ALL])
        top = sb("top", [P, G, 8])
        idx = sb("idx", [P, G, 8], U32)
        idxf = sb("idxf", [P, G, 2])
        tw = sb("tw", [P, G, 2])
        den = sb("den", [P, G])
        rden = sb("rden", [P, G])
        hot0 = sb("hot0", [P, G, E_TRUE])
        hot1 = sb("hot1", [P, G, E_TRUE])
        ew = sb("ew", [P, G, E_TRUE])
        zw = sb("zw", [P, G, P])
        zwT = sb("zwT", [P, G, P])

        weights_in = sem("weights_in")
        x_in = sem("x_in")
        half_bias = sem("half_bias")
        var_ready = sem("var_ready")
        rstd_ready = sem("rstd_ready")
        xn_ready = sem("xn_ready")
        xT_psum = sem("xT_psum")
        xT_ready = sem("xT_ready")
        zg_ready = sem("zg_ready")
        gates_shifted = sem("gates_shifted")
        gates_exp = sem("gates_exp")
        zw_ready = sem("zw_ready")
        zwT_psum = sem("zwT_psum")
        zwT_ready = sem("zwT_ready")
        y_ready = sem("y_ready")
        biased = sem("biased")
        x_done = sem("x_done")

        ps_T = m.psum[:, 0:2, :].rearrange("p k (t c) -> p (k t) c", c=P)
        ps_zg = m.psum[:, 2:6, :].rearrange("p k (t c) -> p (k t) c", c=256)
        ps_y = m.psum[:, 6:8, :].rearrange("p k (t c) -> p (k t) c", c=P)
        x_of = m.x

        jobs_of = lambda k: ((0, 1, 2), (3, 4))[k] if experts is not None else ()
        if experts is not None:
            experts.allocate(ctx)

        block = ctx.enter_context(nc.Block())

        @block.sync
        def _(sp):
            sp.dma_start(w_zg[:, 0:P], w["loraA_T"]).then_inc(weights_in, 16)
            sp.dma_start(w_zg[:, P:P + E_ALL], w["gate_T"]).then_inc(weights_in, 16)
            sp.dma_start(w_base[:, :], w["base_T"]).then_inc(weights_in, 16)
            sp.dma_start(w_loraB[:, :], w["loraB_T"]).then_inc(weights_in, 16)
            sp.dma_start(bias[:, :], w["bias"].partition_broadcast(P)).then_inc(weights_in, 16)
            if x_dram is not None:
                sp.dma_start(m.ident[:, :], w["ident"]).then_inc(weights_in, 16)
                sp.dma_start(m.iota8[:, :], w["iota8"]).then_inc(weights_in, 16)
                x_view = x_dram.rearrange("b (t p) d -> p (b t) d", p=P)
                sp.dma_start(x_of[:, m.first:m.first + G, :], x_view[:, 0:G, :]).then_inc(x_in, 16)
                with sp.Fori(1, PASSES) as i:
                    sp.wait_ge(x_in, i * 16)
                    sp.dma_start(x_of[:, bass.ds(i * G + m.first, G), :], x_view[:, bass.ds(i * G, G), :]).then_inc(x_in, 16)
            if experts is not None:
                experts.load(sp)
                sp.wait_ge(experts.small_in, 16 * 5)

        n_weights = 16 * (7 if x_dram is not None else 5)

        def steps(engine, body):
            for k in range(2):
                body(k, 0)
            with engine.Fori(1, PASSES // 2 - 1) as i:
                for k in range(2):
                    body(k, i)
            for k in range(2):
                body(k, PASSES // 2 - 1)

        is_first = lambda n: isinstance(n, int) and n == 0
        is_last = lambda n: isinstance(n, int) and n == PASSES - 1

        @block.gpsimd
        def _(pool):
            def inverse_std(n):
                pool.wait_ge(var_ready, n + 1)
                pool.tensor_tensor(rstd[:, :], var_eps[:, :], m.minus_half[:, 0:G], ALU.pow).then_inc(rstd_ready, 1)

            def body(k, i):
                n = i * 2 + k
                if not is_last(n):
                    inverse_std(n + 1)
                x = x_of[:, bass.ds(n * G + m.first, G), :]
                pool.wait_ge(xn_ready, n + 1)
                pool.tensor_tensor(x, x, along(bias[:, :], 1, G), ALU.add).then_inc(biased, 1)
                for r in jobs_of(k):
                    experts.split_low(pool, r, i)

            inverse_std(0)
            steps(pool, body)

        @block.scalar
        def _(act):
            def copy_xT(k, n):
                act.wait_ge(xT_psum, n + 1)
                act.activation(xT[k][:, :, :], ps_T, ACT.Copy).then_inc(xT_ready, 1)

            def copy_zwT(n):
                act.wait_ge(zwT_psum, n + 1)
                act.activation(zwT[:, :, :], ps_T, ACT.Copy).then_inc(zwT_ready, 1)

            def body(k, i):
                n = i * 2 + k
                if not is_first(n):
                    copy_zwT(n - 1)
                act.wait_ge(gates_shifted, n + 1)
                act.activation(gexp[:, :, :], gexp[:, :, :], ACT.Exp).then_inc(gates_exp, 1)
                if not is_last(n):
                    copy_xT(1 - k, n + 1)
                for r in jobs_of(k):
                    experts.split_high(act, r, i)

            copy_xT(0, 0)
            if experts is not None:
                act.wait_ge(experts.small_in, 16 * 5)
                act.activation(experts.select[:, :, :], experts.select_raw[:, :, :], ACT.Copy)
            steps(act, body)
            copy_zwT(PASSES - 1)

        @block.tensor
        def _(pe):
            def turn(n):
                pe.wait_ge(xn_ready, n + 1)
                for t in range(G):
                    last = pe.transpose(ps_T[:, t, :], xn[:, t, :], m.ident[:, :])
                last.then_inc(xT_psum, 1)

            def first_products(k, n):
                pe.wait_ge(xT_ready, n + 1)
                for t in range(G):
                    last = pe.matmul(ps_zg[:, t, 0:P + E_ALL], xT[k][:, t, :], w_zg[:, :], start=True, stop=True)
                last.then_inc(zg_ready, 1)

            def turn_zw(n):
                pe.wait_ge(zw_ready, n + 1)
                for t in range(G):
                    last = pe.transpose(ps_T[:, t, :], zw[:, t, :], m.ident[:, :])
                last.then_inc(zwT_psum, 1)

            def outputs(k, n):
                if not is_first(n):
                    pe.wait_ge(x_done, n)
                pe.wait_ge(zwT_ready, n + 1)
                for t in range(G):
                    pe.matmul(ps_y[:, t, :], xT[k][:, t, :], w_base[:, :], start=True, stop=False)
                    last = pe.matmul(ps_y[:, t, :], zwT[:, t, :], w_loraB[:, :], start=False, stop=True)
                last.then_inc(y_ready, 1)

            def body(k, i):
                n = i * 2 + k
                if not is_first(n):
                    turn_zw(n - 1)
                    outputs(1 - k, n - 1)
                if not is_last(n):
                    turn(n + 1)
                    pe.wait_ge(zw_ready, n + 1)
                    first_products(1 - k, n + 1)

            pe.wait_ge(weights_in, n_weights)
            turn(0)
            first_products(0, 0)
            steps(pe, body)
            turn_zw(PASSES - 1)
            outputs(1, PASSES - 1)

        @block.vector
        def _(dve):
            def moments(n):
                if x_dram is not None:
                    dve.wait_ge(x_in, n * 16 + 16)
                for t in range(G):
                    dve.bn_stats(stats[:, t, :], x_of[:, n * G + (t + m.first), :])
                dve.drain()
                for t in range(G):
                    dve.bn_aggr(mv[:, t, :], stats[:, t, :])
                dve.drain()
                dve.tensor_scalar(var_eps[:, :], mv[:, :, 1], LN_EPS, None, ALU.add).then_inc(var_ready, 1)

            def normalise(n):
                dve.wait_ge(rstd_ready, n + 1)
                for t in range(G):
                    last = dve.tensor_scalar(xn[:, t, :], x_of[:, n * G + (t + m.first), :], mv[:, t, 0:1], rstd[:, t:t + 1],
                                             ALU.subtract, ALU.mult)
                last.then_inc(xn_ready, 1)

            def shift_gates(n):
                dve.wait_ge(zg_ready, n + 1)
                dve.tensor_reduce(gmax[:, :], ps_zg[:, :, P:P + E_ALL], AX.X, ALU.max)
                dve.drain()
                dve.tensor_tensor(gexp[:, :, :], ps_zg[:, :, P:P + E_ALL], along(gmax[:, :], 2, E_ALL),
                                  ALU.subtract).then_inc(gates_shifted, 1)

            def weigh(n):
                dve.wait_ge(gates_exp, n + 1)
                dve.memset(den[:, :], 0.0)
                for t in range(G):
                    dve.max(top[:, t, :], gexp[:, t, :])
                dve.drain()
                for t in range(G):
                    dve.max_index(idx[:, t, :], top[:, t, :], gexp[:, t, :])
                dve.drain()
                dve.tensor_copy(idxf[:, :, :], idx[:, :, 0:2])
                dve.drain()
                dve.scalar_tensor_tensor(out=tw[:, :, :], in0=idxf[:, :, :], scalar=float(E_TRUE),
                                         in1=top[:, :, 0:2], op0=ALU.is_lt, op1=ALU.mult)
                iota = along(m.iota8[:, :], 1, G)
                for k, hot in enumerate((hot0, hot1)):
                    dve.tensor_tensor(hot[:, :, :], iota, along(idxf[:, :, k], 2, E_TRUE), ALU.is_equal)
                dve.drain()
                dve.tensor_tensor(den[:, :], tw[:, :, 0], tw[:, :, 1], ALU.add)
                dve.drain()
                dve.scalar_tensor_tensor(out=den[:, :], in0=den[:, :], scalar=0.0, in1=den[:, :],
                                         op0=ALU.is_le, op1=ALU.add)
                dve.drain()
                dve.reciprocal(rden[:, :], den[:, :])
                dve.drain()
                dve.scalar_tensor_tensor(out=tw[:, :, :], in0=tw[:, :, :], scalar=2.0,
                                         in1=along(rden[:, :], 2, 2), op0=ALU.mult, op1=ALU.mult)
                dve.drain()
                for k, hot in enumerate((hot0, hot1)):
                    dve.tensor_tensor(hot[:, :, :], hot[:, :, :], along(tw[:, :, k], 2, E_TRUE), ALU.mult)
                dve.drain()
                dve.tensor_tensor(ew[:, :, :], hot0[:, :, :], hot1[:, :, :], ALU.add)
                dve.drain()
                if not is_first(n):
                    dve.wait_ge(zwT_psum, n)
                dve.tensor_tensor(zw[:, :, :].rearrange("p t (e r) -> p t e r", r=RANK),
                                  ps_zg[:, :, 0:P].rearrange("p t (e r) -> p t e r", r=RANK),
                                  along(ew[:, :, :], 3, RANK), ALU.mult).then_inc(zw_ready, 1)

            def residual(n):
                x = x_of[:, bass.ds(n * G + m.first, G), :]
                dve.wait_ge(biased, n + 1)
                dve.wait_ge(y_ready, n + 1)
                dve.scalar_tensor_tensor(out=x, in0=ps_y, scalar=0.5, in1=x, op0=ALU.mult,
                                         op1=ALU.add).then_inc(x_done, 1)

            def body(k, i):
                n = i * 2 + k
                if not is_last(n):
                    moments(n + 1)
                shift_gates(n)
                if not is_last(n):
                    normalise(n + 1)
                weigh(n)
                if not is_first(n):
                    residual(n - 1)

            if x_dram is not None:
                dve.memset(m.minus_half[:, :], -0.5)
                dve.memset(m.half[:, :], 0.5)
                dve.memset(x_of[:, 0:m.first, :], 0.0)
                dve.memset(x_of[:, m.first + TILES:m.first + TILES + 2 * NT, :], 0.0)
            moments(0)
            dve.wait_ge(weights_in, n_weights)
            dve.tensor_scalar(bias[:, :], bias[:, :], 0.5, None, ALU.mult)
            dve.drain()
            normalise(0)
            steps(dve, body)
            residual(PASSES - 1)




def attention_stage(nc, m, name, w):
    H, DH = 16, 8
    N = SEQ
    SCALE = DH ** -0.5
    PAIRS = ((0, 0), (0, 1), (1, 0), (0, 2), (2, 0), (1, 1))
    K_QK = 72
    K_ALL = K_QK + 3
    UNITS = H * NT
    HALF = H // 2
    RING = 8
    E_MAXIMA, E_LAST_O, E_TOKENS, E_OUT, E_TURN, E_Q, E_K, E_V, E_HALF = 2, 3, 7, 10, 12, 16, 21, 26, 36
    A_TOKENS, A_TURN, A_V = 8, 13, 28
    V_MAXIMA, V_LAST_O, V_NORM, V_OUT, V_Q, V_K, V_HALF, V_HALF_READ = 3, 5, 7, 11, 18, 23, 32, 37
    V_W = 32
    with ExitStack() as ctx:
        def sb(n, shape, dt=F32):
            return ctx.enter_context(nc.sbuf_tensor(f"{name}_{n}", shape, dt))

        def sem(n):
            return ctx.enter_context(nc.semaphore(f"{name}_{n}"))

        w_proj = sb("w_proj", [P, 4, P])
        w_v = sb("w_v", [P, P])
        w_o = sb("w_o", [P, P])
        cos = sb("cos", [P, N])
        sin = sb("sin", [P, N])
        ident_b = sb("ident_b", [P, P], BF16)
        mask_qk = sb("mask_qk", [P, P], BF16)
        mask_kq = sb("mask_kq", [P, P], BF16)
        stats = sb("stats", [P, NT, 6])
        mv = sb("mv", [P, NT, 2])
        var_eps = sb("var_eps", [P, NT])
        rstd = sb("rstd", [P, NT])
        xn = sb("xn", [P, NT, P])
        xT = sb("xT", [P, N])
        rot = [sb("q_rot", [P, N]), sb("k_rot", [P, N])]
        rot_sin = [sb("q_rot_sin", [P, N]), sb("k_rot_sin", [P, N])]
        parts = [sb("qparts", [P, 3, N], BF16), sb("kparts", [P, 3, N], BF16)]
        v_new = sb("v_new", [P, NT, P])
        qs = [sb(f"qs{k}", [K_ALL, H, N], BF16) for k in range(2)]
        ks = [sb(f"ks{k}", [K_ALL, H, N], BF16) for k in range(2)]
        v_aug = [sb(f"v_aug{k}", [P, NT, H, V_W]) for k in range(2)]
        rowmax = sb("rowmax", [P, NT, H])
        mparts = [sb(f"mparts{f}", [P, NT, P // HALF, HALF], BF16) for f in range(2)]
        mT = [sb(f"mT{f}", [3 * HALF, N], BF16) for f in range(2)]
        probs = sb("probs", [P, RING, N])
        oT = sb("oT", [P, N])
        inv = sb("inv", [P, NT, 4])
        o_tok = sb("o_tok", [P, NT, P])
        o_tokT = sb("o_tokT", [P, N])
        junk = sb("junk", [P, 4])

        weights_in = sem("weights_in")
        stacks_set = sem("stacks_set")
        var_ready = sem("var_ready")
        rstd_ready = sem("rstd_ready")
        xn_ready = sem("xn_ready")
        xT_psum = sem("xT_psum")
        xT_ready = sem("xT_ready")
        proj_psum = sem("proj_psum")
        rope_read = sem("rope_read")
        rot_used = sem("rot_used")
        parts_ready = sem("parts_ready")
        v_psum = sem("v_psum")
        v_read = sem("v_read")
        v_ready = sem("v_ready")
        stack_in = [sem(f"stack_in{f}") for f in range(2)]
        score_psum = sem("score_psum")
        max_read = sem("max_read")
        mparts_ready = sem("mparts_ready")
        mT_psum = sem("mT_psum")
        mT_ready = sem("mT_ready")
        m_in = [sem(f"m_in{f}") for f in range(2)]
        exp_psum = sem("exp_psum")
        exp_ready = sem("exp_ready")
        pv_done = sem("pv_done")
        o_read = sem("o_read")
        oT_psum = sem("oT_psum")
        o_norm = sem("o_norm")
        o_tokT_psum = sem("o_tokT_psum")
        o_tokT_ready = sem("o_tokT_ready")
        out_psum = sem("out_psum")
        x_done = sem("x_done")

        ps_exp = [m.psum[:, 0, :], m.psum[:, 1, :]]
        ps_score = [m.psum[:, 2, :], m.psum[:, 3, :]]
        ps_o = [m.psum[:, 4, :], m.psum[:, 5, :]]
        ps_a, ps_b = m.psum[:, 6, :], m.psum[:, 7, :]
        tiles = lambda bank: bank.rearrange("p (t c) -> p t c", c=P)
        ps_mT = m.psum[:, 6, 0:N // 2].bitcast(BF16)
        x_of = m.x
        BODIES = NB // 2
        BLOCKS = 2 * len(PAIRS)
        N_WEIGHTS = 16 * 8

        block = ctx.enter_context(nc.Block())

        @block.sync
        def _(sp):
            for dst, src in ((w_proj, "w_proj"), (w_v, "w_v"), (w_o, "wo_T"), (cos, "cos"), (sin, "sin"),
                             (ident_b, "ident_b"), (mask_qk, "mask_qk"), (mask_kq, "mask_kq")):
                sp.dma_start(dst[:], w[src]).then_inc(weights_in, 16)

            def stack(f, k, count):
                sp.wait_ge(parts_ready, count)
                for side, stacks in enumerate((qs, ks)):
                    for n, pair in enumerate(PAIRS):
                        sp.dma_start(stacks[k][n * DH:(n + 1) * DH, f * HALF:(f + 1) * HALF, :],
                                     parts[side][f * P // 2:(f + 1) * P // 2, pair[side], :]).then_inc(stack_in[f], 16)

            def maxima(f, k, n):
                sp.wait_ge(mT_ready, n * 2 + (f + 1))
                sp.dma_start(qs[k][K_QK:K_ALL, f * HALF:(f + 1) * HALF, :], mT[f][:, :]).then_inc(m_in[f], 16)

            sp.wait_ge(stacks_set, 8)
            stack(0, 0, 1)
            stack(1, 0, 1)
            stack(0, 1, 2)
            stack(1, 1, 2)
            maxima(0, 0, 0)
            with sp.Fori(0, BODIES) as i:
                for k in range(2):
                    maxima(1, k, i * 2 + k)
                    for f in range(2):
                        sp.wait_ge(exp_psum, (i * 2 + k) * UNITS + (f + 1) * UNITS // 2)
                        stack(f, k, i * 2 + (k + 3))
                        if f == 0:
                            maxima(0, 1 - k, i * 2 + (k + 1))
            for f in range(2):
                sp.wait_ge(stack_in[f], 16 * BLOCKS * (NB + 2))
            sp.wait_ge(m_in[0], 16 * (NB + 1))
            sp.wait_ge(m_in[1], 16 * NB)

        @block.gpsimd
        def _(pool):
            for k in range(2):
                pool.memset(qs[k][:, :, :], 0.0).then_inc(stacks_set, 1)
                pool.memset(ks[k][:, :, :], -1.0).then_inc(stacks_set, 1)
                pool.memset(v_aug[k][:, :, :, :], 0.0).then_inc(stacks_set, 1)
                pool.drain()
                pool.memset(v_aug[k][:, :, :, DH:DH + 1], 1.0).then_inc(stacks_set, 1)

            def split(count, copied):
                pool.wait_ge(var_ready, count)
                pool.tensor_tensor(rstd[:, :], var_eps[:, :], m.minus_half[:, 0:NT], ALU.pow).then_inc(rstd_ready, 1)
                for side in range(2):
                    part, r = parts[side], rot[side]
                    pool.wait_ge(rope_read, count * 4 + (side * 2 - 2))
                    if side == 0 and copied is not None:
                        for f in range(2):
                            pool.wait_ge(stack_in[f], copied * (16 * BLOCKS))
                    pool.tensor_tensor(part[:, 0, :], r[:, :], rot_sin[side][:, :], ALU.add)
                    pool.tensor_tensor(r[:, :], r[:, :], rot_sin[side][:, :], ALU.add)
                    pool.drain()
                    pool.tensor_tensor(part[:, 1, :], r[:, :], part[:, 0, :], ALU.subtract)
                    pool.tensor_tensor(r[:, :], r[:, :], part[:, 0, :], ALU.subtract)
                    pool.drain()
                    pool.tensor_tensor(part[:, 2, :], r[:, :], part[:, 1, :], ALU.subtract).then_inc(rot_used, 1)
                    if side == 1:
                        pool.drain()
                        pool.memset(junk[:, 0:1], 0.0).then_inc(parts_ready, 1)

            split(1, None)
            split(2, 1)
            with pool.Fori(0, BODIES) as i:
                for k in range(2):
                    split(i * 2 + (k + 3), i * 2 + (k + 2))

        @block.scalar
        def _(act):
            def turn(count):
                act.wait_ge(xT_psum, count)
                act.activation(xT[:, :], ps_a, ACT.Copy).then_inc(xT_ready, 1)

            def read_v(count):
                act.wait_ge(v_psum, count)
                act.activation(v_new[:, :, :], tiles(ps_a), ACT.Copy).then_inc(v_read, 1)

            act.activation(junk[:, 2:3], m.half[:, 0:1], ACT.Exp).then_inc(exp_ready, 1)
            act.activation(junk[:, 3:4], m.half[:, 0:1], ACT.Exp).then_inc(exp_ready, 1)
            act.activation(junk[:, 1:2], m.half[:, 0:1], ACT.Exp).then_inc(o_read, 1)
            act.drain()
            def values(k):
                act.activation(v_aug[k][:, :, :, 0:DH], v_new[:, :, :].rearrange("p t (h d) -> p t h d", d=DH),
                               ACT.Copy).then_inc(v_ready, 1)

            act.wait_ge(stacks_set, 8)
            for s in range(2):
                turn(s + 1)
                read_v(s + 1)
                act.drain()
                if s == 0:
                    values(0)

            def end_of(s):
                act.wait_ge(pv_done, s * (4 * NT) + 2)
                act.wait_ge(oT_psum, s * 4 + 1)
                act.activation(oT[:, :], ps_o[1], ACT.Copy).then_inc(o_read, 1)

            def tokens_of(s):
                act.wait_ge(o_tokT_psum, s + 1)
                act.activation(o_tokT[:, :], ps_a, ACT.Copy).then_inc(o_tokT_ready, 1)

            with act.Fori(0, BODIES) as i:
                for k in range(2):
                    s = i * 2 + k

                    def read_o(g):
                        act.wait_ge(pv_done, s * (4 * NT) + (2 + NT * (g + 1)))
                        act.wait_ge(oT_psum, s * 4 + (g + 2))
                        act.activation(oT[:, :], ps_o[g % 2], ACT.Copy).then_inc(o_read, 1)

                    for j in range(UNITS):
                        kt = j // 4 % NT
                        act.wait_ge(exp_psum, s * UNITS + (j + 1))
                        act.wait_ge(pv_done, s * (4 * NT) + (j // 4 + 1))
                        act.activation(probs[:, j % RING, 0:N - kt * P], ps_exp[j % 2][:, 0:N - kt * P], ACT.Exp,
                                       scale=SCALE).then_inc(exp_ready, 1)
                        if j == 0:
                            end_of(s)
                        if j == 2:
                            values(1 - k)
                        if j == A_TOKENS:
                            tokens_of(s)
                        if j == A_TURN:
                            turn(s + 3)
                        if j == A_V:
                            read_v(s + 3)
                        if j >= 22 and (j - 22) % 16 == 0 and j < UNITS - 4:
                            read_o((j - 22) // 16)
            end_of(NB)
            tokens_of(NB)

        @block.tensor
        def _(pe):
            def turn(count):
                pe.wait_ge(xn_ready, count)
                for t in range(NT):
                    last = pe.transpose(ps_a[:, t * P:(t + 1) * P], xn[:, t, :], m.ident[:, :])
                last.then_inc(xT_psum, 1)

            def project(side, count):
                if side == 0:
                    pe.wait_ge(xT_ready, count)
                    pe.wait_ge(x_done, count)
                else:
                    pe.wait_ge(rope_read, count * 4 - 2)
                pe.matmul(ps_a, w_proj[:, 2 * side, :], xT[:, :], start=True, stop=True)
                pe.matmul(ps_b, w_proj[:, 2 * side + 1, :], xT[:, :], start=True, stop=True).then_inc(proj_psum, 1)

            def values(count):
                pe.wait_ge(rope_read, count * 4)
                for t in range(NT):
                    last = pe.matmul(ps_a[:, t * P:(t + 1) * P], xT[:, t * P:(t + 1) * P], w_v[:, :],
                                     start=True, stop=True)
                last.then_inc(v_psum, 1)

            def score(k, n, j):
                h, qt = j // NT, j % NT
                pe.wait_ge(max_read, n * UNITS + (j + 1))
                if j % (UNITS // 2) == 0:
                    pe.wait_ge(stack_in[2 * j // UNITS], n * (16 * BLOCKS) + 16 * BLOCKS)
                bank = ps_score[j % 2]
                pe.matmul(bank[:, 0:(qt + 1) * P], qs[k][0:K_QK, h, qt * P:(qt + 1) * P],
                          ks[k][0:K_QK, h, 0:(qt + 1) * P], start=True, stop=False)
                pe.matmul(bank[:, qt * P:(qt + 1) * P], ident_b[:, :], mask_qk[:, :],
                          start=False, stop=True).then_inc(score_psum, 1)

            def turn_maxima(f, n):
                pe.wait_ge(mparts_ready, n * 2 + (f + 1))
                for t in range(NT):
                    last = pe.transpose(ps_mT[:, t * P:(t + 1) * P], mparts[f][:, t].rearrange("p a h -> p (a h)"),
                                        ident_b[:, :])
                last.then_inc(mT_psum, 1)

            def turn_last_o(s):
                pe.wait_ge(o_read, s * 4 + 2)
                for t in range(NT):
                    last = pe.transpose(ps_b[:, t * P:(t + 1) * P], oT[:, t * P:(t + 1) * P], m.ident[:, :])
                last.then_inc(oT_psum, 1)

            def turn_tokens(s):
                pe.wait_ge(o_norm, s * 4 + 1)
                if not isinstance(s, int):
                    pe.wait_ge(mT_ready, s * 2 + 2)
                for t in range(NT):
                    last = pe.transpose(ps_a[:, t * P:(t + 1) * P], o_tok[:, t, :], m.ident[:, :])
                last.then_inc(o_tokT_psum, 1)

            def project_out(s):
                pe.wait_ge(o_tokT_ready, s + 1)
                for t in range(NT):
                    last = pe.matmul(ps_b[:, t * P:(t + 1) * P], o_tokT[:, t * P:(t + 1) * P], w_o[:, :],
                                     start=True, stop=True)
                last.then_inc(out_psum, 1)

            for k in range(2):
                if k == 0:
                    pe.wait_ge(weights_in, N_WEIGHTS)
                turn(k + 1)
                if k == 1:
                    pe.wait_ge(v_read, 1)
                project(0, k + 1)
                project(1, k + 1)
                values(k + 1)
                if k == 0:
                    pe.wait_ge(v_read, 1)
            pe.wait_ge(v_read, 2)
            for j in range(UNITS):
                score(0, 0, j)
            turn_maxima(0, 0)
            pe.wait_ge(mT_ready, 1)
            with pe.Fori(0, BODIES) as i:
                for k in range(2):
                    s = i * 2 + k

                    def exponent(j):
                        g, kt, hh = j // 16, j // 4 % NT, j % 4
                        n = N - kt * P
                        pe.wait_ge(exp_ready, s * UNITS + (j + 1))
                        if j % (UNITS // 2) == 0:
                            pe.wait_ge(m_in[2 * j // UNITS], s * 16 + 16)
                        bank = ps_exp[j % 2]
                        pe.matmul(bank[:, 0:n], ks[k][:, 4 * g + hh, kt * P:(kt + 1) * P],
                                  qs[k][:, 4 * g + hh, kt * P:N], start=True, stop=False)
                        pe.matmul(bank[:, 0:P], ident_b[:, :], mask_kq[:, :],
                                  start=False, stop=True).then_inc(exp_psum, 1)

                    def weigh(q):
                        g, kt = q // NT, q % NT
                        n = N - kt * P
                        pe.wait_ge(exp_ready, s * UNITS + (2 + 4 * q + 4))
                        if q == 0:
                            pe.wait_ge(v_ready, s + 1)
                        if kt == 0:
                            pe.wait_ge(o_read, s * 4 + (g + 1))
                        for hh in range(4):
                            last = pe.matmul(ps_o[g % 2][32 * hh:32 * hh + 32, kt * P:N], v_aug[k][:, kt, 4 * g + hh, :],
                                             probs[:, (4 * q + hh) % RING, 0:n], start=(kt == 0), stop=(kt == NT - 1),
                                             tile_position=(0, 32 * hh))
                        last.then_inc(pv_done, 1)

                    def turn_o(g):
                        pe.wait_ge(o_read, s * 4 + (2 + g + 1))
                        if g > 0:
                            pe.wait_ge(o_norm, s * 4 + (g + 1))
                        else:
                            pe.wait_ge(rope_read, (s + 3) * 4)
                        for t in range(NT):
                            last = pe.transpose(ps_b[:, t * P:(t + 1) * P], oT[:, t * P:(t + 1) * P], m.ident[:, :])
                        last.then_inc(oT_psum, 1)

                    for j in range(UNITS):
                        exponent(j)
                        score(1 - k, s + 1, j)
                        if j % 4 == 3 and j > 3:
                            weigh(j // 4 - 1)
                        if j == E_MAXIMA:
                            turn_maxima(1, s)
                        if j == E_LAST_O:
                            turn_last_o(s)
                        if j == E_TOKENS:
                            turn_tokens(s)
                        if j == E_OUT:
                            project_out(s)
                        if j == E_TURN:
                            turn(s + 3)
                        if j == E_Q:
                            project(0, s + 3)
                        if j == E_K:
                            project(1, s + 3)
                        if j == E_V:
                            values(s + 3)
                        if j == E_HALF:
                            pe.wait_ge(v_read, s + 3)
                            turn_maxima(0, s + 1)
                        if j in (27, 43):
                            turn_o((j - 27) // 16)
                    turn_o(2)
                    weigh(UNITS // 4 - 1)
            pe.wait_ge(o_norm, NB * 4)
            turn_last_o(NB)
            turn_tokens(NB)
            project_out(NB)

        @block.vector
        def _(dve):
            def moments(tile):
                for t in range(NT):
                    dve.bn_stats(stats[:, t, :], x_of[:, tile + (t + m.first), :])
                dve.drain()
                for t in range(NT):
                    dve.bn_aggr(mv[:, t, :], stats[:, t, :])
                dve.drain()
                dve.tensor_scalar(var_eps[:, :], mv[:, :, 1], LN_EPS, None, ALU.add).then_inc(var_ready, 1)

            def normalise_x(tile, count):
                dve.wait_ge(rstd_ready, count)
                for t in range(NT):
                    last = dve.tensor_scalar(xn[:, t, :], x_of[:, tile + (t + m.first), :], mv[:, t, 0:1], rstd[:, t:t + 1],
                                             ALU.subtract, ALU.mult)
                last.then_inc(xn_ready, 1)

            def rotate(side, count):
                dve.wait_ge(proj_psum, count * 2 + (side - 1))
                if not isinstance(count, int) or count > 1:
                    dve.wait_ge(rot_used, count * 2 + (side - 3))
                dve.tensor_tensor(rot[side][:, :], ps_a, cos[:, :], ALU.mult).then_inc(rope_read, 1)
                dve.tensor_tensor(rot_sin[side][:, :], ps_b, sin[:, :], ALU.mult).then_inc(rope_read, 1)

            def row_max(n, j):
                h, qt = j // NT, j % NT
                dve.wait_ge(score_psum, n * UNITS + (j + 1))
                dve.tensor_reduce(rowmax[:, qt, h:h + 1], ps_score[j % 2][:, 0:(qt + 1) * P], AX.X,
                                  ALU.max).then_inc(max_read, 1)

            def split_maxima(f):
                r, parts_of = rowmax[:, :, f * HALF:(f + 1) * HALF], mparts[f]
                dve.drain()
                dve.tensor_copy(parts_of[:, :, 0, :], r)
                dve.drain()
                dve.tensor_tensor(r, r, parts_of[:, :, 0, :], ALU.subtract)
                dve.drain()
                dve.tensor_copy(parts_of[:, :, 1, :], r)
                dve.drain()
                dve.tensor_tensor(parts_of[:, :, 2, :], r, parts_of[:, :, 1, :], ALU.subtract).then_inc(mparts_ready, 1)

            def read_maxima(f, n):
                dve.wait_ge(mT_psum, n * 2 + (f + 1))
                dve.tensor_copy(mT[f][:, :], ps_mT[0:3 * HALF]).then_inc(mT_ready, 1)

            def normalise(o, channels, count):
                dve.wait_ge(oT_psum, count)
                dve.reciprocal(inv[:, :, :], o[:, :, :, DH])
                dve.drain()
                dve.tensor_tensor(o_tok[:, :, channels].rearrange("p t (h d) -> p t h d", d=DH),
                                  o[:, :, :, 0:DH], along(inv[:, :, :], 3, DH), ALU.mult).then_inc(o_norm, 1)

            o_heads = tiles(ps_b).rearrange("p t (h c) -> p t h c", c=V_W)
            channels_of = lambda g: slice(4 * DH * g, 4 * DH * (g + 1))

            def add_out(s):
                dve.wait_ge(out_psum, s + 1)
                x = x_of[:, bass.ds(s * NT + m.first - NT, NT), :]
                dve.tensor_tensor(x, tiles(ps_b), x, ALU.add).then_inc(x_done, 1)

            dve.memset(rowmax[:, 0, 0:1], 0.0).then_inc(max_read, 1)
            dve.memset(rowmax[:, 0, 1:2], 0.0).then_inc(max_read, 1)
            dve.memset(rowmax[:, 0, 2:3], 0.0).then_inc(x_done, 1)
            dve.memset(rowmax[:, 0, 3:4], 0.0).then_inc(x_done, 1)
            for f in range(2):
                dve.memset(mparts[f][:, :, 3:P // HALF, :], 0.0)
            dve.memset(ps_o[1], 1.0).then_inc(pv_done, 1)
            dve.memset(oT[:, 0:1], 0.0).then_inc(pv_done, 1)
            dve.memset(o_tok[:, :, :], 0.0).then_inc(oT_psum, 1)
            dve.drain()
            dve.wait_ge(weights_in, N_WEIGHTS)
            for s in range(2):
                moments(s * NT)
                normalise_x(s * NT, s + 1)
                rotate(0, s + 1)
                rotate(1, s + 1)
            for j in range(UNITS):
                row_max(0, j)
                if j == UNITS // 2 - 1:
                    split_maxima(0)
            split_maxima(1)
            read_maxima(0, 0)
            with dve.Fori(0, BODIES) as i:
                for k in range(2):
                    s = i * 2 + k
                    for j in range(UNITS):
                        row_max(s + 1, j)
                        if j == 1:
                            moments((s + 2) * NT)
                        if j == V_MAXIMA:
                            read_maxima(1, s)
                        if j == V_LAST_O:
                            normalise(o_heads, channels_of(3), s * 4 + 2)
                        if j == V_NORM:
                            normalise_x((s + 2) * NT, s + 3)
                        if j == V_OUT:
                            add_out(s)
                        if j == V_Q:
                            rotate(0, s + 3)
                        if j == V_K:
                            rotate(1, s + 3)
                        if j in (31, 47):
                            g = (j - 31) // 16
                            normalise(o_heads, channels_of(g), s * 4 + (g + 3))
                        if j == V_HALF:
                            split_maxima(0)
                        if j == V_HALF_READ:
                            read_maxima(0, s + 1)
                    normalise(o_heads, channels_of(2), s * 4 + 5)
                    split_maxima(1)
            normalise(o_heads, channels_of(3), NB * 4 + 2)
            add_out(NB)




def expert_stage(nc, m, name, ex):
    G = NT
    PASSES = TILES // G
    N = G * P
    E_S, E_R, HID = 2, 8, 512
    E = E_S + E_R
    C = HID // P
    T_GATES, T_SPREAD = 3, 4
    T_STATS, T_RMS, T_NORM = 5, 6, 7
    SPREADS = 6
    POOL_C = 3
    with ExitStack() as ctx:
        def sb(n, shape, dt=F32):
            return ctx.enter_context(nc.sbuf_tensor(f"{name}_{n}", shape, dt))

        def sem(n):
            return ctx.enter_context(nc.semaphore(f"{name}_{n}"))

        euler = sb("euler", [P, G, E_R])
        stats = sb("stats", [P, G, 6])
        mv = sb("mv", [P, G, 2])
        var_eps = sb("var_eps", [P, G])
        rstd = sb("rstd", [P, G])
        ms_eps = sb("ms_eps", [P, G])
        rms_inv = sb("rms_inv", [P, G])
        rms = sb("rms", [P, G])
        rr = sb("rr", [P, G])
        xn = sb("xn", [P, G, P])
        u = sb("u", [P, G, P])
        xT = sb("xT", [P, N])
        xTh = sb("xTh", [P, N], F32R)
        xTl = sb("xTl", [P, N], F32R)
        logit = sb("logit", [P, G, E_R])
        score = sb("score", [P, G, E_R])
        ssum = sb("ssum", [P, G])
        top = sb("top", [P, G, 8])
        idx = sb("idx", [P, G, 8], U32)
        idxf = sb("idxf", [P, G, 2])
        gk = sb("gk", [P, G, 2])
        hot0 = sb("hot0", [P, G, E_R])
        hot1 = sb("hot1", [P, G, E_R])
        gates = sb("gates", [P, G, E])
        g_high = sb("g_high", [P, G, E], F32R)
        g_parts = sb("g_parts", [P, G, 2 * E])
        gTp = sb("gTp", [P, N], F32R)
        spread = sb("spread", [P, SPREADS, N])
        h = sb("h", [P, 2, C, N])
        hh = sb("hh", [P, 2, C, N], F32R)
        hl = sb("hl", [P, 2, C, N], F32R)
        weighted = sb("weighted", [P, 2, N])
        acc = sb("acc", [P, N])

        pool_const = sem("pool_const")
        var_ready = sem("var_ready")
        rstd_ready = sem("rstd_ready")
        ms_ready = sem("ms_ready")
        rms_ready = sem("rms_ready")
        xn_ready = sem("xn_ready")
        xT_psum = sem("xT_psum")
        xT_ready = sem("xT_ready")
        xTl_ready = sem("xTl_ready")
        logit_psum = sem("logit_psum")
        logit_ready = sem("logit_ready")
        exp_ready = sem("exp_ready")
        gates_ready = sem("gates_ready")
        gT_psum = sem("gT_psum")
        gT_ready = sem("gT_ready")
        spread_psum = sem("spread_psum")
        spread_ready = sem("spread_ready")
        h_psum = sem("h_psum")
        h_ready = sem("h_ready")
        high_ready = sem("high_ready")
        low_ready = sem("low_ready")
        pool_low_ready = sem("pool_low_ready")
        y_ready = sem("y_ready")
        y_used = sem("y_used")
        added = sem("added")
        summed = sem("summed")
        sumT_psum = sem("sumT_psum")
        x_done = sem("x_done")

        ps_h = m.psum[:, 0:C, :]
        ps_y = m.psum[:, C:C + 2, :]
        ps_m = m.psum[:, 6, :]
        ps_n = m.psum[:, 7, :]
        tiles = lambda bank: bank.rearrange("p (t c) -> p t c", c=P)
        ps_logit = ps_n[:, 0:G * E_R].rearrange("p (t e) -> p t e", e=E_R)
        x_of = m.x
        Y = E_R + 1

        block = ctx.enter_context(nc.Block())

        @block.gpsimd
        def _(pool):
            pool.memset(euler[:, :, :], float(np.e)).then_inc(pool_const, 1)
            pool.memset(acc[:, :], 0.0).then_inc(summed, 1)
            pool.wait_ge(pool_const, 1)

            def rstd_of(count):
                pool.wait_ge(var_ready, count)
                pool.tensor_tensor(rstd[:, :], var_eps[:, :], m.minus_half[:, 0:G], ALU.pow).then_inc(rstd_ready, 1)

            def rms_of(count):
                pool.wait_ge(ms_ready, count)
                pool.tensor_tensor(rms_inv[:, :], ms_eps[:, :], m.minus_half[:, 0:G], ALU.pow)
                pool.tensor_tensor(rms[:, :], ms_eps[:, :], m.half[:, 0:G], ALU.pow).then_inc(rms_ready, 1)

            rstd_of(1)
            rms_of(1)
            with pool.Fori(0, PASSES) as i:
                for e in range(E):
                    if e >= E_S + 2:
                        pool.wait_ge(y_used, i * Y + (e - E_S + 2))
                        pool.tensor_tensor(acc[:, :], acc[:, :], weighted[:, e % 2, :], ALU.add).then_inc(added, 1)
                        pool.drain()
                    pool.wait_ge(high_ready, i * E + (e + 1))
                    if e >= 2:
                        pool.wait_ge(y_ready, i * E + (e - 1))
                    pool.tensor_tensor(hl[:, e % 2, POOL_C, :], h[:, e % 2, POOL_C, :], hh[:, e % 2, POOL_C, :].bitcast(F32),
                                       ALU.subtract).then_inc(pool_low_ready, 1)
                    if e == 0:
                        pool.wait_ge(logit_ready, i + 1)
                        pool.tensor_tensor(score[:, :, :], euler[:, :, :], logit[:, :, :], ALU.pow).then_inc(exp_ready, 1)
                    if e == T_STATS:
                        rstd_of(i + 2)
                    if e == T_RMS:
                        rms_of(i + 2)
                pool.wait_ge(y_used, i * Y + (1 + Y))
                pool.tensor_tensor(acc[:, :], acc[:, :], weighted[:, E % 2, :], ALU.add).then_inc(added, 1)
                pool.drain()
                pool.wait_ge(y_used, i * Y + (2 + Y))
                pool.tensor_tensor(acc[:, :], acc[:, :], weighted[:, (E - 1) % 2, :], ALU.add).then_inc(summed, 1)

        @block.scalar
        def _(act):
            def turn(count):
                act.wait_ge(xT_psum, count)
                act.activation(xT[:, :], ps_m, ACT.Copy)
                act.activation(xTh[:, :], ps_m, ACT.Copy).then_inc(xT_ready, 1)

            turn(1)
            with act.Fori(0, PASSES) as i:
                for e in range(E):
                    for c in range(C):
                        act.wait_ge(h_psum, i * (E * C) + (e * C + c + 1))
                        if e >= 2 and c == 0:
                            act.wait_ge(high_ready, i * E + (e - 1))
                            act.wait_ge(low_ready, i * E + (e - 1))
                        if e >= 2 and c == POOL_C:
                            act.wait_ge(pool_low_ready, i * E + (e - 1))
                        act.activation(h[:, e % 2, c, :], ps_h[:, c, :], ACT.Gelu,
                                       bias=ex.b1[:, e * C + c:e * C + c + 1]).then_inc(h_ready, 1)
                    if e == T_GATES:
                        act.wait_ge(gT_psum, i + 1)
                        act.activation(gTp[0:2 * E, :], ps_n[0:2 * E, :], ACT.Copy).then_inc(gT_ready, 1)
                    if e >= T_SPREAD and e < T_SPREAD + 4:
                        for q in range(2 * (e - T_SPREAD), 2 * (e - T_SPREAD) + 2):
                            act.wait_ge(spread_psum, i * E_R + (q + 1))
                            if q >= SPREADS:
                                act.wait_ge(y_used, i * Y + (2 + q - SPREADS + E_S))
                            act.activation(spread[:, q % SPREADS, :], (ps_m, ps_n)[q % 2], ACT.Copy).then_inc(spread_ready, 1)
                turn(i + 2)

        @block.tensor
        def _(pe):
            def turn(count):
                pe.wait_ge(xn_ready, count)
                for t in range(G):
                    last = pe.transpose(ps_m[:, t * P:(t + 1) * P], xn[:, t, :], m.ident[:, :])
                last.then_inc(xT_psum, 1)

            def turn_sum(count):
                pe.wait_ge(summed, count)
                for t in range(G):
                    last = pe.transpose(ps_n[:, t * P:(t + 1) * P], acc[:, t * P:(t + 1) * P], m.ident[:, :])
                last.then_inc(sumT_psum, 1)

            turn(1)
            with pe.Fori(0, PASSES) as i:
                def up(e):
                    for c in range(C):
                        if e >= 1:
                            pe.wait_ge(h_ready, i * (E * C) + ((e - 1) * C + c + 1))
                        high, low = ex.high[:, e, c * P:(c + 1) * P], ex.low[:, e, c * P:(c + 1) * P]
                        pe.matmul(ps_h[:, c, :], high, xTh[:, :], start=True, stop=False)
                        pe.matmul(ps_h[:, c, :], high, xTl[:, :], start=False, stop=False)
                        pe.matmul(ps_h[:, c, :], low, xTh[:, :], start=False, stop=True).then_inc(h_psum, 1)

                def down(e):
                    pe.wait_ge(high_ready, i * E + (e + 1))
                    if e != 1:
                        pe.wait_ge(y_used, i * Y + max(e, 2))
                    bank = ps_y[:, 0 if e == 0 else (e - 1) % 2, :]
                    first, last = e != 1, e >= 1
                    for c in range(C):
                        high, low = ex.high[:, E + e, c * P:(c + 1) * P], ex.low[:, E + e, c * P:(c + 1) * P]
                        pe.matmul(bank, high, hh[:, e % 2, c, :], start=(first and c == 0), stop=False)
                        pe.matmul(bank, low, hh[:, e % 2, c, :], start=False, stop=False)
                        if c == 0:
                            pe.wait_ge(low_ready, i * E + (e + 1))
                        if c == POOL_C:
                            pe.wait_ge(pool_low_ready, i * E + (e + 1))
                        mm = pe.matmul(bank, high, hl[:, e % 2, c, :], start=False, stop=(last and c == C - 1))
                    mm.then_inc(y_ready, 1)

                def spread_gates(q):
                    if q == 0:
                        pe.wait_ge(gT_ready, i + 1)
                    if q >= 2:
                        pe.wait_ge(spread_ready, i * E_R + (q - 1))
                    pe.matmul((ps_m, ps_n)[q % 2], ex.select[:, q, :], gTp[:, :],
                              start=True, stop=True).then_inc(spread_psum, 1)

                pe.wait_ge(xT_ready, i + 1)
                for t in range(G):
                    last = pe.matmul(ps_logit[:, t, :], xT[:, t * P:(t + 1) * P], ex.cent[:, :], start=True, stop=True)
                last.then_inc(logit_psum, 1)
                pe.wait_ge(xTl_ready, i + 1)
                up(0)
                pe.wait_ge(logit_ready, i + 1)
                turn_sum(i + 1)
                for e in range(1, E):
                    up(e)
                    if e == E - 1:
                        pe.wait_ge(spread_ready, i * E_R + E_R)
                        turn(i + 2)
                    if e >= T_SPREAD and e < T_SPREAD + 4:
                        spread_gates(2 * (e - T_SPREAD))
                        spread_gates(2 * (e - T_SPREAD) + 1)
                    down(e - 1)
                    if e == T_GATES:
                        pe.wait_ge(gates_ready, i + 1)
                        pe.wait_ge(x_done, i + 1)
                        for t in range(G):
                            last = pe.transpose(ps_n[0:2 * E, t * P:(t + 1) * P], g_parts[:, t, :], m.ident[:, :])
                        last.then_inc(gT_psum, 1)
                down(E - 1)
            turn_sum(PASSES + 1)

        @block.vector
        def _(dve):
            def moments(tile):
                for t in range(G):
                    dve.bn_stats(stats[:, t, :], x_of[:, tile + (t + m.first), :])
                dve.drain()
                for t in range(G):
                    dve.bn_aggr(mv[:, t, :], stats[:, t, :])
                dve.drain()
                dve.tensor_scalar(var_eps[:, :], mv[:, :, 1], LN_EPS, None, ALU.add).then_inc(var_ready, 1)

            def mean_square(count):
                dve.wait_ge(rstd_ready, count)
                dve.tensor_tensor(ms_eps[:, :], mv[:, :, 1], rstd[:, :], ALU.mult)
                dve.drain()
                dve.tensor_tensor(ms_eps[:, :], ms_eps[:, :], rstd[:, :], ALU.mult)
                dve.drain()
                dve.tensor_scalar(ms_eps[:, :], ms_eps[:, :], RMS_EPS, None, ALU.add).then_inc(ms_ready, 1)

            def normalise(tile, count):
                dve.wait_ge(rms_ready, count)
                dve.tensor_tensor(rr[:, :], rstd[:, :], rms_inv[:, :], ALU.mult)
                dve.drain()
                for t in range(G):
                    last = dve.tensor_scalar(xn[:, t, :], x_of[:, tile + (t + m.first), :], mv[:, t, 0:1], rr[:, t:t + 1],
                                             ALU.subtract, ALU.mult)
                last.then_inc(xn_ready, 1)

            dve.memset(gTp[:, :].bitcast(F32), 0.0)
            dve.memset(gates[:, :, :], 1.0).then_inc(y_used, 1)
            dve.memset(idxf[:, :, :], 0.0).then_inc(y_used, 1)
            dve.memset(u[:, :, :], 0.0)
            dve.drain()
            moments(0)
            mean_square(1)
            normalise(0, 1)

            def residual(i):
                dve.wait_ge(sumT_psum, i + 1)
                dve.tensor_tensor(u[:, :, :], tiles(ps_n), u[:, :, :], ALU.add)
                dve.drain()
                x = x_of[:, bass.ds(i * G + (m.first - G), G), :]
                dve.scalar_tensor_tensor(out=x, in0=u[:, :, :], scalar=0.5, in1=x, op0=ALU.mult,
                                         op1=ALU.add).then_inc(x_done, 1)
                dve.drain()

            def low_input(count):
                dve.wait_ge(xT_ready, count)
                dve.tensor_tensor(xTl[:, :], xT[:, :], xTh[:, :].bitcast(F32), ALU.subtract).then_inc(xTl_ready, 1)

            low_input(1)
            with dve.Fori(0, PASSES) as i:
                def scale_logits():
                    dve.wait_ge(logit_psum, i + 1)
                    dve.scalar_tensor_tensor(out=logit[:, :, :], in0=ps_logit, scalar=-1.0,
                                             in1=along(rms[:, :], 2, E_R), op0=ALU.mult,
                                             op1=ALU.mult).then_inc(logit_ready, 1)

                def input_of_experts():
                    for t in range(G):
                        dve.tensor_scalar(u[:, t, :], x_of[:, i * G + (t + m.first), :], mv[:, t, 0:1], rstd[:, t:t + 1],
                                          ALU.subtract, ALU.mult)

                def best_scores():
                    dve.wait_ge(exp_ready, i + 1)
                    dve.tensor_scalar(score[:, :, :], score[:, :, :], 1.0, None, ALU.add)
                    dve.drain()
                    dve.reciprocal(score[:, :, :], score[:, :, :])
                    dve.drain()
                    dve.tensor_reduce(ssum[:, :], score[:, :, :], AX.X, ALU.add)
                    for t in range(G):
                        dve.max(top[:, t, :], score[:, t, :])
                    dve.drain()
                    for t in range(G):
                        dve.max_index(idx[:, t, :], top[:, t, :], score[:, t, :])
                    dve.reciprocal(ssum[:, :], ssum[:, :])
                    dve.drain()

                def gates_of_best():
                    dve.tensor_copy(idxf[:, :, :], idx[:, :, 0:2])
                    dve.tensor_tensor(gk[:, :, :], top[:, :, 0:2], along(ssum[:, :], 2, 2), ALU.mult)
                    dve.drain()
                    for k, hot in enumerate((hot0, hot1)):
                        dve.tensor_tensor(hot[:, :, :], along(m.iota8[:, :], 1, G), along(idxf[:, :, k], 2, E_R),
                                          ALU.is_equal)
                    dve.drain()
                    for k, hot in enumerate((hot0, hot1)):
                        dve.tensor_tensor(hot[:, :, :], hot[:, :, :], along(gk[:, :, k], 2, E_R), ALU.mult)
                    dve.drain()
                    dve.tensor_tensor(gates[:, :, E_S:E], hot0[:, :, :], hot1[:, :, :], ALU.add)
                    dve.drain()
                    dve.tensor_copy(g_high[:, :, :], gates[:, :, :])
                    dve.drain()
                    dve.tensor_copy(g_parts[:, :, 0:E], g_high[:, :, :].bitcast(F32))
                    dve.tensor_tensor(g_parts[:, :, E:2 * E], gates[:, :, :], g_high[:, :, :].bitcast(F32),
                                      ALU.subtract).then_inc(gates_ready, 1)

                def split(e):
                    if e >= 2:
                        dve.wait_ge(y_ready, i * E + (e - 1))
                    pieces = ((0, C // 2), (C // 2, C)) if e == E - 1 else ((0, C),)
                    for first, end in pieces:
                        dve.wait_ge(h_ready, i * (E * C) + (e * C + end))
                        high = dve.tensor_copy(hh[:, e % 2, first:end, :], h[:, e % 2, first:end, :])
                        dve.drain()
                        end_low = min(end, POOL_C)
                        low = dve.tensor_tensor(hl[:, e % 2, first:end_low, :], h[:, e % 2, first:end_low, :],
                                                hh[:, e % 2, first:end_low, :].bitcast(F32), ALU.subtract)
                        if end == C:
                            high.then_inc(high_ready, 1)
                            low.then_inc(low_ready, 1)

                def weigh(e):
                    dve.wait_ge(y_ready, i * E + (e + 1))
                    if e == 1:
                        dve.tensor_scalar(acc[:, :], ps_y[:, 0, :], ex.b2[:, 0:1], ex.b2[:, 1:2], ALU.add,
                                          ALU.add).then_inc(y_used, 1)
                    elif e > 1:
                        dve.wait_ge(spread_ready, i * E_R + (e - E_S + 1))
                        if e >= 4:
                            dve.wait_ge(added, i * (E_R - 1) + (e - 3))
                        dve.scalar_tensor_tensor(out=weighted[:, e % 2, :], in0=ps_y[:, (e - 1) % 2, :],
                                                 scalar=ex.b2[:, e:e + 1], in1=spread[:, (e - E_S) % SPREADS, :],
                                                 op0=ALU.add, op1=ALU.mult).then_inc(y_used, 1)

                scale_logits()
                for e in range(E):
                    if e > E_S and e != T_SPREAD:
                        weigh(e - 2)
                    split(e)
                    if e == T_SPREAD:
                        weigh(e - 2)
                    if e == 0:
                        residual(i)
                        input_of_experts()
                    if e == 1:
                        best_scores()
                    if e == 2:
                        gates_of_best()
                    if e == T_STATS:
                        moments(i * G + G)
                    if e == T_RMS:
                        mean_square(i + 2)
                    if e == T_NORM:
                        normalise(i * G + G, i + 2)
                low_input(i + 2)
                weigh(E - 2)
                weigh(E - 1)
            residual(PASSES)




def gla_stage(nc, m, name, w):
    DH = 8
    N = SEQ
    SCALE = DH ** -0.5
    DV_BANKS = 4
    TERMS = DH + 1
    with ExitStack() as ctx:
        def sb(n, shape, dt=F32):
            return ctx.enter_context(nc.sbuf_tensor(f"{name}_{n}", shape, dt))

        def sem(n):
            return ctx.enter_context(nc.semaphore(f"{name}_{n}"))

        w_qf = sb("w_qf", [P, 2 * P])
        w_i = sb("w_i", [P, P])
        w_irep = sb("w_irep", [P, DH, P])
        w_orep = sb("w_orep", [P, DH, P])
        w_o = sb("w_o", [P, P])
        head_ones = sb("head_ones", [P, P])
        stats = sb("stats", [P, NT, 6])
        mv = sb("mv", [P, NT, 2])
        var_eps = sb("var_eps", [P, NT])
        rstd = sb("rstd", [P, NT])
        xn = sb("xn", [P, NT, P])
        xT = sb("xT", [P, N])
        dxT = [sb(f"dxT{k}", [P, N]) for k in range(2)]
        xTk = [sb(f"xT{k}", [P, N]) for k in range(2)]
        nmax = sb("nmax", [P, 2 * NT])
        qf = sb("qf", [P, 2 * NT, P])
        qfsum = sb("qfsum", [P, 2 * NT])
        qfinv = sb("qfinv", [P, 2 * NT])
        qT = [sb(f"qT{k}", [P, N]) for k in range(2)]
        pT = [sb(f"pT{k}", [P, N]) for k in range(2)]
        vT = sb("vT", [P, N])
        state = [sb(f"state{k}", [P, TERMS, N]) for k in range(2)]

        weights_in = sem("weights_in")
        var_ready = sem("var_ready")
        rstd_ready = sem("rstd_ready")
        xn_ready = sem("xn_ready")
        xT_psum = sem("xT_psum")
        xT_ready = sem("xT_ready")
        dx_ready = sem("dx_ready")
        qf_psum = sem("qf_psum")
        nmax_ready = sem("nmax_ready")
        qf_exp = sem("qf_exp")
        qf_ready = sem("qf_ready")
        qpT_psum = sem("qpT_psum")
        qpT_ready = sem("qpT_ready")
        dv_psum = sem("dv_psum")
        dv_used = sem("dv_used")
        o_used = sem("o_used")
        term_ready = sem("term_ready")
        vT_ready = sem("vT_ready")
        o_psum = sem("o_psum")

        ps_T = m.psum[:, 0, :]
        ps_qf = m.psum[:, 1:3, :].rearrange("p k (t c) -> p (k t) c", c=P)
        ps_qT, ps_pT = m.psum[:, 1, :], m.psum[:, 2, :]
        ps_dv = [m.psum[:, 3 + k, :] for k in range(DV_BANKS)]
        ps_o = m.psum[:, 7, :].rearrange("p (t c) -> p t c", c=P)
        x_of = m.x
        SCANS = DH + 2

        block = ctx.enter_context(nc.Block())

        @block.sync
        def _(sp):
            for dst, src in ((w_qf, "w_qf"), (w_i, "w_i"), (w_irep, "w_irep"), (w_orep, "w_orep"),
                             (w_o, "w_o"), (head_ones, "head_ones")):
                sp.dma_start(dst[:], w[src]).then_inc(weights_in, 16)

        N_WEIGHTS = 16 * 6
        BODIES = NB // 2

        @block.gpsimd
        def _(pool):
            def inv_std(count):
                pool.wait_ge(var_ready, count)
                pool.tensor_tensor(rstd[:, :], var_eps[:, :], m.minus_half[:, 0:NT], ALU.pow).then_inc(rstd_ready, 1)

            pool.memset(state[1][:, :, :], 0.0).then_inc(term_ready, 1)
            inv_std(1)
            inv_std(2)
            with pool.Fori(0, BODIES) as i:
                for k in range(2):
                    for v in range(DH):
                        if v == 3:
                            inv_std(i * 2 + (k + 3))
                        pool.wait_ge(dv_used, (i * 2 + k) * TERMS + (DV_BANKS + v + 1))
                        pool.tensor_tensor(state[k][:, v, :], state[k][:, v, :], qT[k][:, :],
                                           ALU.mult).then_inc(term_ready, 1)

        @block.scalar
        def _(act):
            def turn(k, count):
                act.wait_ge(xT_psum, count)
                act.activation(xTk[k][:, :], ps_T, ACT.Copy).then_inc(xT_ready, 1)

            def softmax(k, count):
                act.wait_ge(nmax_ready, count)
                for j in range(2 * NT):
                    last = act.activation(qf[:, j, :], ps_qf[:, j, :], ACT.Exp, bias=nmax[:, j:j + 1],
                                          accum_out=qfsum[:, j:j + 1])
                last.then_inc(qf_exp, 1)

            def turn_qp(k, count):
                act.wait_ge(qpT_psum, count)
                act.activation(qT[k][:, :], ps_qT, ACT.Copy)
                act.activation(pT[k][:, :], ps_pT, ACT.Copy).then_inc(qpT_ready, 1)

            turn(0, 1)
            softmax(0, 1)
            turn_qp(0, 1)
            with act.Fori(0, BODIES) as i:
                for k in range(2):
                    nxt = i * 2 + (k + 2)
                    turn(1 - k, nxt)
                    softmax(1 - k, nxt)
                    turn_qp(1 - k, nxt)
                    act.wait_ge(dv_psum, (i * 2 + k) * SCANS + SCANS)
                    act.activation(vT[:, :], ps_dv[(k * SCANS + SCANS - 1) % DV_BANKS], ACT.Copy).then_inc(vT_ready, 1)

        @block.tensor
        def _(pe):
            def turn(count):
                pe.wait_ge(xn_ready, count)
                for t in range(NT):
                    last = pe.transpose(ps_T[:, t * P:(t + 1) * P], xn[:, t, :], m.ident[:, :])
                last.then_inc(xT_psum, 1)

            def logits(k, count):
                pe.wait_ge(xT_ready, count)
                for t in range(NT):
                    last = pe.matmul(m.psum[:, 1 + t // 2, (t % 2) * 256:(t % 2) * 256 + 256],
                                     xTk[k][:, t * P:(t + 1) * P], w_qf[:, :], start=True, stop=True)
                last.then_inc(qf_psum, 1)

            def turn_qp(count):
                pe.wait_ge(qf_ready, count)
                for t in range(NT):
                    pe.transpose(ps_qT[:, t * P:(t + 1) * P], qf[:, 2 * t, :], m.ident[:, :])
                    last = pe.transpose(ps_pT[:, t * P:(t + 1) * P], qf[:, 2 * t + 1, :], m.ident[:, :])
                last.then_inc(qpT_psum, 1)

            def output(k, s, tiles):
                if tiles[0] == 0:
                    pe.wait_ge(term_ready, s * DH + 1)
                    pe.wait_ge(dv_used, s * TERMS + DV_BANKS)
                    pe.wait_ge(o_used, s + 1)
                for t in tiles:
                    for v in range(TERMS):
                        last = pe.matmul(ps_o[:, t, :], state[1 - k][:, v, t * P:(t + 1) * P],
                                         w_orep[:, v, :] if v < DH else w_o[:, :], start=(v == 0), stop=(v == DH))
                if tiles[-1] == NT - 1:
                    last.then_inc(o_psum, 1)

            pe.wait_ge(weights_in, N_WEIGHTS)
            turn(1)
            logits(0, 1)
            turn_qp(1)
            with pe.Fori(0, BODIES) as i:
                for k in range(2):
                    nxt = i * 2 + (k + 2)

                    def scan_input(j):
                        n = k * SCANS + j
                        pe.wait_ge(dv_used, (i * 2 + k) * TERMS + (DV_BANKS + (-2, -1, 0, 0, 1, 2, 3, 4, 5, 6)[j]))
                        if j == 0:
                            pe.wait_ge(dx_ready, i * 2 + (k + 1))
                        if j < DH:
                            mm = pe.matmul(ps_dv[n % DV_BANKS], w_irep[:, j, :], dxT[k][:, :], start=True, stop=True)
                        elif j == DH:
                            mm = pe.matmul(ps_dv[n % DV_BANKS], head_ones[:, :], qT[k][:, :], start=True, stop=True)
                        else:
                            mm = pe.matmul(ps_dv[n % DV_BANKS], w_i[:, :], xTk[k][:, :], start=True, stop=True)
                        mm.then_inc(dv_psum, 1)

                    for j in (0, 1, 2):
                        scan_input(j)
                    turn(nxt)
                    output(k, i * 2 + k, (0, 1))
                    logits(1 - k, nxt)
                    for j in (3, 4, 5):
                        scan_input(j)
                    output(k, i * 2 + k, (2, 3))
                    for j in (6, 7):
                        scan_input(j)
                    turn_qp(nxt)
                    for j in (8, 9):
                        scan_input(j)
            output(0, NB, (0, 1, 2, 3))

        @block.vector
        def _(dve):
            def layer_norm(tile, count):
                for t in range(NT):
                    dve.bn_stats(stats[:, t, :], x_of[:, tile + (t + m.first), :])
                dve.drain()
                for t in range(NT):
                    dve.bn_aggr(mv[:, t, :], stats[:, t, :])
                dve.drain()
                dve.tensor_scalar(var_eps[:, :], mv[:, :, 1], LN_EPS, None, ALU.add).then_inc(var_ready, 1)

            def normalise(tile, count):
                dve.wait_ge(rstd_ready, count)
                for t in range(NT):
                    last = dve.tensor_scalar(xn[:, t, :], x_of[:, tile + (t + m.first), :], mv[:, t, 0:1], rstd[:, t:t + 1],
                                             ALU.subtract, ALU.mult)
                last.then_inc(xn_ready, 1)

            def difference(k, count):
                dve.wait_ge(xT_ready, count)
                dve.tensor_scalar(dxT[k][:, 0:1], xTk[k][:, 0:1], -1.0, None, ALU.mult)
                dve.tensor_tensor(dxT[k][:, 1:N], xTk[k][:, 0:N - 1], xTk[k][:, 1:N], ALU.subtract).then_inc(dx_ready, 1)

            def maxima(count):
                dve.wait_ge(qf_psum, count)
                dve.tensor_reduce(nmax[:, :], ps_qf, AX.X, ALU.max)
                dve.drain()
                dve.tensor_scalar(nmax[:, :], nmax[:, :], -1.0, None, ALU.mult).then_inc(nmax_ready, 1)

            def divide(count):
                dve.wait_ge(qf_exp, count)
                dve.reciprocal(qfinv[:, :], qfsum[:, :])
                dve.drain()
                for j in range(2 * NT):
                    last = dve.tensor_scalar(qf[:, j, :], qf[:, j, :], qfinv[:, j:j + 1],
                                             SCALE if j % 2 == 0 else 1.0, ALU.mult, ALU.mult)
                last.then_inc(qf_ready, 1)

            def residual(s):
                x = x_of[:, bass.ds(s * NT + m.first - NT, NT), :]
                dve.wait_ge(o_psum, s + 1)
                dve.tensor_tensor(x, ps_o, x, ALU.add).then_inc(o_used, 1)

            dve.wait_ge(weights_in, N_WEIGHTS)
            for k in range(DV_BANKS):
                dve.memset(nmax[:, k:k + 1], 0.0).then_inc(dv_used, 1)
            dve.memset(nmax[:, DV_BANKS:DV_BANKS + 1], 0.0).then_inc(o_used, 1)
            dve.drain()
            layer_norm(0, 1)
            normalise(0, 1)
            difference(0, 1)
            layer_norm(NT, 2)
            maxima(1)
            normalise(NT, 2)
            divide(1)
            with dve.Fori(0, BODIES) as i:
                for k in range(2):
                    nxt = i * 2 + (k + 2)
                    tile = (i * 2 + (k + 2)) * NT

                    def scan(v):
                        n = k * SCANS + v
                        if v == 0:
                            dve.wait_ge(qpT_ready, i * 2 + (k + 1))
                        dve.wait_ge(dv_psum, i * (2 * SCANS) + (n + 1))
                        dve.tensor_tensor_scan(state[k][:, v, :], ps_dv[n % DV_BANKS], pT[k][:, :], 0.0,
                                               ALU.add, ALU.mult).then_inc(dv_used, 1)

                    scan(0)
                    scan(1)
                    layer_norm(tile, i * 2 + (k + 3))
                    scan(2)
                    difference(1 - k, nxt)
                    maxima(nxt)
                    scan(3)
                    scan(4)
                    scan(5)
                    divide(nxt)
                    residual(i * 2 + k)
                    normalise(tile, i * 2 + (k + 3))
                    scan(6)
                    scan(7)
                    dve.wait_ge(vT_ready, i * 2 + (k + 1))
                    dve.tensor_tensor(state[k][:, DH, :], ps_dv[(k * SCANS + DH) % DV_BANKS], vT[:, :],
                                      ALU.mult).then_inc(dv_used, 1)
            residual(NB)



def store_stage(nc, m, out):
    with ExitStack() as ctx:
        stored = ctx.enter_context(nc.semaphore("stored"))
        block = ctx.enter_context(nc.Block())

        @block.sync
        def _(sp):
            sp.dma_start(out.rearrange("b (t p) d -> p (b t) d", p=P), m.x[:, m.first:m.first + TILES, :]).then_inc(stored, 16)
            sp.wait_ge(stored, 16)


def build(nc, c, out):
    with ExitStack() as ctx:
        m = Mem()
        m.x = ctx.enter_context(nc.sbuf_tensor("x", [P, NT + TILES + 2 * NT, D], F32))
        m.first = NT
        m.ident = ctx.enter_context(nc.sbuf_tensor("ident", [P, P], F32))
        m.iota8 = ctx.enter_context(nc.sbuf_tensor("iota8", [P, 8], F32))
        m.minus_half = ctx.enter_context(nc.sbuf_tensor("minus_half", [P, 8], F32))
        m.half = ctx.enter_context(nc.sbuf_tensor("half", [P, 8], F32))
        m.psum = ctx.enter_context(nc.psum_tensor("psum", [P, 8, PSUM_BANK], F32))
        lora = {k: c[k] for k in ("loraA_T", "gate_T", "base_T", "loraB_T", "bias", "ident", "iota8")}
        lora_moe_stage(nc, m, "ffn0a", lora, x_dram=c["x"])
        experts = {k: c[k] for k in ("w12", "b1", "b2", "cent", "gain", "select")}
        attn = {k: c[k] for k in ("w_proj", "w_v", "wo_T", "cos", "sin", "ident_b", "mask_qk", "mask_kq")}
        gla = {k: c[k] for k in ("w_qf", "w_i", "w_irep", "w_orep", "w_o", "head_ones")}
        attention_stage(nc, m, "attn", attn)
        ex = Experts(nc, ctx, experts)
        lora_moe_stage(nc, m, "ffn0b", lora, experts=ex)
        expert_stage(nc, m, "ffn1a", ex)
        gla_stage(nc, m, "gla", gla)
        expert_stage(nc, m, "ffn1b", ex)
        store_stage(nc, m, out)


def layout(inputs):
    a = {k: np.asarray(v) for k, v in inputs.items()}
    f = lambda v: np.ascontiguousarray(v)
    c = {"x": a["L0_attn_x"]}
    c["loraA_T"] = a["L0_ffn_lora_A"].reshape(P, D).T
    c["gate_T"] = a["L0_ffn_gate_w"].T
    c["base_T"] = a["L0_ffn_base_w"].T
    c["loraB_T"] = a["L0_ffn_lora_B"].transpose(0, 2, 1).reshape(P, D)
    c["bias"] = a["L0_ffn_base_b"]
    c["ident"] = np.eye(P, dtype=np.float32)
    c["iota8"] = np.tile(np.arange(8, dtype=np.float32), (P, 1))
    w1 = np.concatenate([a["L1_ffn_W1_s"], a["L1_ffn_W1_r"]])
    w2 = np.concatenate([a["L1_ffn_W2_s"], a["L1_ffn_W2_r"]])
    b1 = np.concatenate([a["L1_ffn_b1_s"], a["L1_ffn_b1_r"]])
    w2 = w2.reshape(10, 4, P, D).transpose(2, 0, 1, 3).reshape(P, 10, 512)
    c["w12"] = np.concatenate([w1.transpose(1, 0, 2), w2], axis=1)
    c["b1"] = b1.reshape(40, P).T
    c["b2"] = np.concatenate([a["L1_ffn_b2_s"], a["L1_ffn_b2_r"]]).T
    c["select"] = np.zeros((P, 8, P), np.float32)
    for e in range(8):
        c["select"][[2 + e, 10 + 2 + e], e] = 1.0
    c["cent"] = a["L1_ffn_centroids"]
    c["gain"] = np.stack([a["L1_ffn_g_shared"]] * 2 + [a["L1_ffn_g_routed"]] * 8
                         + [np.ones(P, np.float32)] * 10, axis=1)
    c["w_qf"] = np.concatenate([a["L1_attn_Wq"], a["L1_attn_Wf"]], axis=1)
    c["w_i"] = a["L1_attn_Wi"]
    c["w_irep"] = np.repeat(a["L1_attn_Wi"].reshape(D, 16, 1, 8), 8, axis=2).transpose(0, 3, 1, 2).reshape(D, 8, P)
    c["w_orep"] = np.repeat(a["L1_attn_Wo"].reshape(16, 1, 8, D), 8, axis=1).transpose(0, 1, 2, 3).reshape(P, 8, D)
    c["w_o"] = a["L1_attn_Wo"]
    c["head_ones"] = np.kron(np.eye(16, dtype=np.float32), np.ones((8, 8), np.float32))
    wq, wk, wv = a["L0_attn_W_qkv"].reshape(3, 16, 8, D)
    by_d = lambda t: t.reshape(2, 8, 8, D).transpose(0, 2, 1, 3).reshape(P, D).T
    swapped = lambda t: t.reshape(16, 4, 2, D)[:, :, ::-1].reshape(16, 8, D)
    c["w_proj"] = np.stack([by_d(wq), by_d(swapped(wq)), by_d(wk), by_d(swapped(wk))], axis=1)
    c["w_v"] = wv.reshape(P, D).T
    c["wo_T"] = a["L0_attn_W_o"].T
    inv_freq = np.float32(10000.0) ** (np.arange(0, 8, 2, dtype=np.float32) / np.float32(8))
    ang = np.arange(SEQ, dtype=np.float32)[None, :] / inv_freq[:, None]
    table = lambda t: np.tile(np.repeat(t, 8, axis=0), (2, 1))
    c["cos"] = table(np.repeat(np.cos(ang), 2, axis=0))
    sin = np.stack([-np.sin(ang), np.sin(ang)], axis=1).reshape(8, SEQ)
    c["sin"] = table(sin)
    BIG = -1e30
    bf = mybir.dt.np(BF16)
    c["ident_b"] = np.eye(P, dtype=np.float32).astype(bf)
    c["mask_qk"] = np.triu(np.full((P, P), BIG, np.float32), 1).astype(bf)
    c["mask_kq"] = np.tril(np.full((P, P), BIG, np.float32), -1).astype(bf)
    return {k: f(v) for k, v in c.items()}


def kernel(**inputs):
    import concourse.bacc as bacc
    from concourse.bass_utils import run_bass_kernel_spmd

    nc = bacc.Bacc("TRN2", target_bir_lowering=False, num_devices=1)
    arrays = {f"in_{k}": v for k, v in layout(inputs).items()}
    c = {k[3:]: nc.dram_tensor(k, v.shape, mybir.dt.from_np(v.dtype), kind="ExternalInput").ap()
         for k, v in arrays.items()}
    nc.disable_value_cache = True
    out = nc.dram_tensor("out_0", (NB, SEQ, D), F32, kind="ExternalOutput").ap()
    build(nc, c, out)
    return run_bass_kernel_spmd(nc, [arrays], core_ids=[0]).results[0]["out_0"]
```

```python
from contextlib import ExitStack

import numpy as np

import concourse.bass as bass
from concourse import mybir

ALU = mybir.AluOpType
ACT = mybir.ActivationFunctionType
AX = mybir.AxisListType
F32 = mybir.dt.float32
F32R = mybir.dt.float32r
BF16 = mybir.dt.bfloat16
U32 = mybir.dt.uint32

P = 128
NB, SEQ, D = 16, 512, 128
NT = SEQ // P
TILES = NB * NT
LN_EPS = 1e-5
RMS_EPS = float(np.finfo(np.float32).eps)
PSUM_BANK = 512


class Mem:
    pass


def along(ap, axis, count):
    a = ap.unsqueeze(axis)
    shape = list(a.shape)
    shape[axis] = count
    return a.broadcast_to(shape)


class Experts:
    E, HID = 10, 512
    JOBS = 2 * E
    RING = 5

    def __init__(self, nc, ctx, w):
        def sb(n, shape, dt=F32):
            return ctx.enter_context(nc.sbuf_tensor(f"experts_{n}", shape, dt))

        self.nc, self.w = nc, w
        self.high = sb("high", [P, self.JOBS, self.HID], F32R)
        self.low = sb("low", [P, self.JOBS, self.HID], F32R)
        self.b1 = sb("b1", [P, self.E * self.HID // P])
        self.b2 = sb("b2", [P, self.E])
        self.cent = sb("cent", [P, 8])
        self.select = sb("select", [P, 8, P], F32R)

    def allocate(self, own):
        nc, R = self.nc, self.RING
        self.raw = own.enter_context(nc.sbuf_tensor("experts_raw", [P, R, self.HID], F32))
        self.scaled = own.enter_context(nc.sbuf_tensor("experts_scaled", [P, R, self.HID], F32))
        self.select_raw = own.enter_context(nc.sbuf_tensor("experts_select_raw", [P, 8, P], F32))
        self.gain = own.enter_context(nc.sbuf_tensor("experts_gain", [P, self.JOBS], F32))
        self.small_in = own.enter_context(nc.semaphore("experts_small_in"))
        self.raw_in = [own.enter_context(nc.semaphore(f"experts_raw_in{r}")) for r in range(R)]
        self.scaled_ready = own.enter_context(nc.semaphore("experts_scaled_ready"))
        self.high_ready = own.enter_context(nc.semaphore("experts_high_ready"))
        self.low_ready = own.enter_context(nc.semaphore("experts_low_ready"))

    def load(self, sp):
        w, R = self.w, self.RING
        for dst, src in ((self.b1, "b1"), (self.b2, "b2"), (self.cent, "cent"), (self.gain, "gain"),
                         (self.select_raw, "select")):
            sp.dma_start(dst[:], w[src]).then_inc(self.small_in, 16)
        for r in range(R):
            sp.dma_start(self.raw[:, r, :], w["w12"][:, r, :]).then_inc(self.raw_in[r], 16)
        with sp.Fori(1, self.JOBS // R) as i:
            for r in range(R):
                sp.wait_ge(self.high_ready, i * R + (r + 1 - R))
                sp.dma_start(self.raw[:, r, :], w["w12"][:, bass.ds(i * R + r, 1), :]).then_inc(self.raw_in[r], 16)

    def split_high(self, act, r, i):
        job = i * self.RING + r
        act.wait_ge(self.raw_in[r], i * 16 + 16)
        if not isinstance(i, int) or i > 0:
            act.wait_ge(self.low_ready, job - (self.RING - 1))
        gain = self.gain[:, bass.ds(job, 1)]
        act.activation(self.scaled[:, r, :], self.raw[:, r, :], ACT.Copy, scale=gain).then_inc(self.scaled_ready, 1)
        act.activation(self.high[:, bass.ds(job, 1), :], self.raw[:, bass.ds(r, 1), :], ACT.Copy,
                       scale=gain).then_inc(self.high_ready, 1)

    def split_low(self, pool, r, i):
        job = i * self.RING + r
        pool.wait_ge(self.scaled_ready, job + 1)
        pool.wait_ge(self.high_ready, job + 1)
        pool.tensor_tensor(self.low[:, bass.ds(job, 1), :], self.scaled[:, bass.ds(r, 1), :],
                           self.high[:, bass.ds(job, 1), :].bitcast(F32), ALU.subtract).then_inc(self.low_ready, 1)


def lora_moe_stage(nc, m, name, w, x_dram=None, experts=None):
    G = 8
    HALVES = (range(0, G // 2), range(G // 2, G))
    PASSES = TILES // G
    E_TRUE, E_ALL, RANK = 8, 10, 16
    with ExitStack() as ctx:
        def sb(n, shape, dt=F32):
            return ctx.enter_context(nc.sbuf_tensor(f"{name}_{n}", shape, dt))

        def sem(n):
            return ctx.enter_context(nc.semaphore(f"{name}_{n}"))

        w_zg = sb("w_zg", [P, P + E_ALL])
        w_base = sb("w_base", [P, P])
        w_loraB = sb("w_loraB", [P, P])
        bias = sb("bias", [P, P])
        stats = sb("stats", [P, G, 6])
        mv = sb("mv", [P, G, 2])
        var_eps = sb("var_eps", [P, G])
        minus_mean = sb("minus_mean", [P, G])
        rstd = sb("rstd", [P, G])
        shift = sb("shift", [P, G])
        xn = sb("xn", [P, G, P])
        xT = [sb(f"xT{k}", [P, G, P]) for k in range(2)]
        gmax = sb("gmax", [P, G])
        gexp = sb("gexp", [P, G, E_ALL])
        top = sb("top", [P, G, 8])
        idx = sb("idx", [P, G, 8], U32)
        idxf = sb("idxf", [P, G, 2])
        tw = sb("tw", [P, G, 2])
        den = sb("den", [P, G])
        rden = sb("rden", [P, G])
        hot0 = sb("hot0", [P, G, E_TRUE])
        hot1 = sb("hot1", [P, G, E_TRUE])
        ew = sb("ew", [P, G, E_TRUE])
        zw = sb("zw", [P, G, P])
        zwT = sb("zwT", [P, G, P])

        weights_in = sem("weights_in")
        x_in = sem("x_in")
        half_bias = sem("half_bias")
        var_ready = sem("var_ready")
        rstd_ready = sem("rstd_ready")
        xn_ready = sem("xn_ready")
        xT_psum = sem("xT_psum")
        xT_ready = sem("xT_ready")
        zg_ready = sem("zg_ready")
        gates_shifted = sem("gates_shifted")
        gates_exp = sem("gates_exp")
        zw_ready = sem("zw_ready")
        zwT_psum = sem("zwT_psum")
        zwT_ready = sem("zwT_ready")
        y_ready = sem("y_ready")
        biased = sem("biased")
        x_done = sem("x_done")

        ps_T = m.psum[:, 0:2, :].rearrange("p k (t c) -> p (k t) c", c=P)
        ps_zg = m.psum[:, 2:6, :].rearrange("p k (t c) -> p (k t) c", c=256)
        ps_y = m.psum[:, 6:8, :].rearrange("p k (t c) -> p (k t) c", c=P)
        x_of = m.x

        jobs_of = lambda k: ((0, 1, 2), (3, 4))[k] if experts is not None else ()
        if experts is not None:
            experts.allocate(ctx)

        block = ctx.enter_context(nc.Block())

        @block.sync
        def _(sp):
            if x_dram is not None:
                x_view = x_dram.rearrange("b (t p) d -> p (b t) d", p=P)
                sp.dma_start(x_of[:, m.first:m.first + G, :], x_view[:, 0:G, :]).then_inc(x_in, 16)
            sp.dma_start(w_zg[:, 0:P], w["loraA_T"]).then_inc(weights_in, 16)
            sp.dma_start(w_zg[:, P:P + E_ALL], w["gate_T"]).then_inc(weights_in, 16)
            sp.dma_start(w_base[:, :], w["base_T"]).then_inc(weights_in, 16)
            sp.dma_start(w_loraB[:, :], w["loraB_T"]).then_inc(weights_in, 16)
            sp.dma_start(bias[:, :], w["bias"].partition_broadcast(P)).then_inc(weights_in, 16)
            if x_dram is not None:
                sp.dma_start(m.ident[:, :], w["ident"]).then_inc(weights_in, 16)
                sp.dma_start(m.iota8[:, :], w["iota8"]).then_inc(weights_in, 16)
                with sp.Fori(1, PASSES) as i:
                    sp.wait_ge(x_in, i * 16)
                    sp.dma_start(x_of[:, bass.ds(i * G + m.first, G), :], x_view[:, bass.ds(i * G, G), :]).then_inc(x_in, 16)
            if experts is not None:
                experts.load(sp)
                sp.wait_ge(experts.small_in, 16 * 5)

        n_weights = 16 * (7 if x_dram is not None else 5)

        def steps(engine, body):
            for k in range(2):
                body(k, 0)
            with engine.Fori(1, PASSES // 2 - 1) as i:
                for k in range(2):
                    body(k, i)
            for k in range(2):
                body(k, PASSES // 2 - 1)

        is_first = lambda n: isinstance(n, int) and n == 0
        is_last = lambda n: isinstance(n, int) and n == PASSES - 1

        @block.gpsimd
        def _(pool):
            def inverse_std(n):
                pool.wait_ge(var_ready, n + 1)
                if not is_first(n):
                    pool.wait_ge(xn_ready, n * 2)
                pool.tensor_tensor(rstd[:, :], var_eps[:, :], m.minus_half[:, 0:G], ALU.pow)
                pool.drain()
                pool.tensor_tensor(shift[:, :], minus_mean[:, :], rstd[:, :], ALU.mult).then_inc(rstd_ready, 1)

            def body(k, i):
                n = i * 2 + k
                if not is_last(n):
                    inverse_std(n + 1)
                x = x_of[:, bass.ds(n * G + m.first, G), :]
                pool.wait_ge(xn_ready, n * 2 + 2)
                pool.tensor_tensor(x, x, along(bias[:, :], 1, G), ALU.add).then_inc(biased, 1)
                for r in jobs_of(k):
                    experts.split_low(pool, r, i)

            inverse_std(0)
            steps(pool, body)

        @block.scalar
        def _(act):
            def normalise(n):
                act.wait_ge(rstd_ready, n + 1)
                for half in HALVES:
                    for t in half:
                        last = act.activation(xn[:, t, :], x_of[:, n * G + (t + m.first), :], ACT.Identity,
                                              scale=rstd[:, t:t + 1], bias=shift[:, t:t + 1])
                    last.then_inc(xn_ready, 1)

            def copy(to, psum, ready, n):
                for f, half in enumerate(HALVES):
                    act.wait_ge(psum, n * 2 + (f + 1))
                    act.activation(to[:, half.start:half.stop, :], ps_T[:, half.start:half.stop, :],
                                   ACT.Copy).then_inc(ready, 1)

            def copy_xT(k, n):
                copy(xT[k], xT_psum, xT_ready, n)

            def copy_zwT(n):
                copy(zwT, zwT_psum, zwT_ready, n)

            def body(k, i):
                n = i * 2 + k
                if not is_first(n):
                    copy_zwT(n - 1)
                act.wait_ge(gates_shifted, n + 1)
                act.activation(gexp[:, :, :], gexp[:, :, :], ACT.Exp).then_inc(gates_exp, 1)
                if not is_last(n):
                    normalise(n + 1)
                if not is_last(n):
                    copy_xT(1 - k, n + 1)
                for r in jobs_of(k):
                    experts.split_high(act, r, i)

            normalise(0)
            copy_xT(0, 0)
            if experts is not None:
                act.wait_ge(experts.small_in, 16 * 5)
                act.activation(experts.select[:, :, :], experts.select_raw[:, :, :], ACT.Copy)
            steps(act, body)
            copy_zwT(PASSES - 1)

        @block.tensor
        def _(pe):
            def turn(n):
                for f, half in enumerate(HALVES):
                    pe.wait_ge(xn_ready, n * 2 + (f + 1))
                    for t in half:
                        last = pe.transpose(ps_T[:, t, :], xn[:, t, :], m.ident[:, :])
                    last.then_inc(xT_psum, 1)

            def first_products(k, n):
                for f, half in enumerate(HALVES):
                    pe.wait_ge(xT_ready, n * 2 + (f + 1))
                    for t in half:
                        last = pe.matmul(ps_zg[:, t, 0:P + E_ALL], xT[k][:, t, :], w_zg[:, :], start=True, stop=True)
                last.then_inc(zg_ready, 1)

            def turn_zw(n):
                pe.wait_ge(zw_ready, n + 1)
                for half in HALVES:
                    for t in half:
                        last = pe.transpose(ps_T[:, t, :], zw[:, t, :], m.ident[:, :])
                    last.then_inc(zwT_psum, 1)

            def outputs(k, n):
                if not is_first(n):
                    pe.wait_ge(x_done, n)
                for f, half in enumerate(HALVES):
                    pe.wait_ge(zwT_ready, n * 2 + (f + 1))
                    for t in half:
                        pe.matmul(ps_y[:, t, :], xT[k][:, t, :], w_base[:, :], start=True, stop=False)
                        last = pe.matmul(ps_y[:, t, :], zwT[:, t, :], w_loraB[:, :], start=False, stop=True)
                last.then_inc(y_ready, 1)

            def body(k, i):
                n = i * 2 + k
                if not is_first(n):
                    turn_zw(n - 1)
                    outputs(1 - k, n - 1)
                if not is_last(n):
                    turn(n + 1)
                    pe.wait_ge(zw_ready, n + 1)
                    first_products(1 - k, n + 1)

            pe.wait_ge(weights_in, n_weights)
            turn(0)
            first_products(0, 0)
            steps(pe, body)
            turn_zw(PASSES - 1)
            outputs(1, PASSES - 1)

        @block.vector
        def _(dve):
            def moments(n):
                if x_dram is not None:
                    dve.wait_ge(x_in, n * 16 + 16)
                if not is_first(n):
                    dve.wait_ge(rstd_ready, n)
                for t in range(G):
                    dve.bn_stats(stats[:, t, :], x_of[:, n * G + (t + m.first), :])
                dve.drain()
                for t in range(G):
                    dve.bn_aggr(mv[:, t, :], stats[:, t, :])
                dve.drain()
                dve.tensor_scalar(minus_mean[:, :], mv[:, :, 0], -1.0, None, ALU.mult)
                dve.tensor_scalar(var_eps[:, :], mv[:, :, 1], LN_EPS, None, ALU.add).then_inc(var_ready, 1)

            def shift_gates(n):
                dve.wait_ge(zg_ready, n + 1)
                dve.tensor_reduce(gmax[:, :], ps_zg[:, :, P:P + E_ALL], AX.X, ALU.max)
                dve.drain()
                dve.tensor_tensor(gexp[:, :, :], ps_zg[:, :, P:P + E_ALL], along(gmax[:, :], 2, E_ALL),
                                  ALU.subtract).then_inc(gates_shifted, 1)

            def weigh(n):
                dve.wait_ge(gates_exp, n + 1)
                dve.memset(den[:, :], 0.0)
                for t in range(G):
                    dve.max(top[:, t, :], gexp[:, t, :])
                dve.drain()
                for t in range(G):
                    dve.max_index(idx[:, t, :], top[:, t, :], gexp[:, t, :])
                dve.drain()
                dve.tensor_copy(idxf[:, :, :], idx[:, :, 0:2])
                dve.drain()
                dve.scalar_tensor_tensor(out=tw[:, :, :], in0=idxf[:, :, :], scalar=float(E_TRUE),
                                         in1=top[:, :, 0:2], op0=ALU.is_lt, op1=ALU.mult)
                iota = along(m.iota8[:, :], 1, G)
                for k, hot in enumerate((hot0, hot1)):
                    dve.tensor_tensor(hot[:, :, :], iota, along(idxf[:, :, k], 2, E_TRUE), ALU.is_equal)
                dve.drain()
                dve.tensor_tensor(den[:, :], tw[:, :, 0], tw[:, :, 1], ALU.add)
                dve.drain()
                dve.scalar_tensor_tensor(out=den[:, :], in0=den[:, :], scalar=0.0, in1=den[:, :],
                                         op0=ALU.is_le, op1=ALU.add)
                dve.drain()
                dve.reciprocal(rden[:, :], den[:, :])
                dve.drain()
                dve.scalar_tensor_tensor(out=tw[:, :, :], in0=tw[:, :, :], scalar=2.0,
                                         in1=along(rden[:, :], 2, 2), op0=ALU.mult, op1=ALU.mult)
                dve.drain()
                for k, hot in enumerate((hot0, hot1)):
                    dve.tensor_tensor(hot[:, :, :], hot[:, :, :], along(tw[:, :, k], 2, E_TRUE), ALU.mult)
                dve.drain()
                dve.tensor_tensor(ew[:, :, :], hot0[:, :, :], hot1[:, :, :], ALU.add)
                dve.drain()
                if not is_first(n):
                    dve.wait_ge(zwT_psum, n * 2)
                dve.tensor_tensor(zw[:, :, :].rearrange("p t (e r) -> p t e r", r=RANK),
                                  ps_zg[:, :, 0:P].rearrange("p t (e r) -> p t e r", r=RANK),
                                  along(ew[:, :, :], 3, RANK), ALU.mult).then_inc(zw_ready, 1)

            def residual(n):
                x = x_of[:, bass.ds(n * G + m.first, G), :]
                dve.wait_ge(biased, n + 1)
                dve.wait_ge(y_ready, n + 1)
                dve.scalar_tensor_tensor(out=x, in0=ps_y, scalar=0.5, in1=x, op0=ALU.mult,
                                         op1=ALU.add).then_inc(x_done, 1)

            def body(k, i):
                n = i * 2 + k
                if not is_last(n):
                    moments(n + 1)
                shift_gates(n)
                weigh(n)
                if not is_first(n):
                    residual(n - 1)

            if x_dram is not None:
                dve.memset(m.minus_half[:, :], -0.5)
                dve.memset(m.half[:, :], 0.5)
                dve.memset(x_of[:, 0:m.first, :], 0.0)
                dve.memset(x_of[:, m.first + TILES:m.first + TILES + 2 * NT, :], 0.0)
            moments(0)
            dve.wait_ge(weights_in, n_weights)
            dve.tensor_scalar(bias[:, :], bias[:, :], 0.5, None, ALU.mult)
            dve.drain()
            steps(dve, body)
            residual(PASSES - 1)




def attention_stage(nc, m, name, w):
    H, DH = 16, 8
    N = SEQ
    SCALE = DH ** -0.5
    PAIRS = ((0, 0), (0, 1), (1, 0), (0, 2), (2, 0), (1, 1))
    K_QK = 72
    K_ALL = K_QK + 3
    FILLS = [(w, (h,)) for w in range(2) for h in range(4)] + [(2, (0, 1)), (2, (2, 3)), (3, (0, 1, 2, 3))]
    GROUPS = H // 4
    UNITS = GROUPS * len(FILLS)
    width_of = lambda w: (NT - w) * P
    HALF = H // 2
    RING = len(FILLS)
    E_MAXIMA, E_LAST_O, E_TOKENS, E_OUT, E_TURN, E_Q, E_K, E_V, E_HALF = 2, 3, 5, 7, 9, 11, 15, 19, 25
    A_TOKENS, A_TURN, A_V = 6, 10, 21
    V_MAXIMA, V_LAST_O, V_NORM, V_OUT, V_Q, V_K, V_HALF, V_HALF_READ = 3, 4, 5, 8, 12, 16, 22, 26
    E_O, A_O, V_O = (21, 30, 40), (14, 25, 36), (23, 32, 42)
    V_W = 32
    with ExitStack() as ctx:
        def sb(n, shape, dt=F32):
            return ctx.enter_context(nc.sbuf_tensor(f"{name}_{n}", shape, dt))

        def sem(n):
            return ctx.enter_context(nc.semaphore(f"{name}_{n}"))

        w_proj = sb("w_proj", [P, 4, P])
        w_v = sb("w_v", [P, P])
        w_o = sb("w_o", [P, P])
        cos = sb("cos", [P, N])
        sin = sb("sin", [P, N])
        ident_b = sb("ident_b", [P, P], BF16)
        mask_qk = sb("mask_qk", [P, P], BF16)
        mask_kq = sb("mask_kq", [P, P], BF16)
        stats = sb("stats", [P, NT, 6])
        mv = sb("mv", [P, NT, 2])
        var_eps = sb("var_eps", [P, NT])
        rstd = sb("rstd", [P, NT])
        xn = sb("xn", [P, NT, P])
        xT = sb("xT", [P, N])
        rot = [sb("q_rot", [P, N]), sb("k_rot", [P, N])]
        rot_sin = [sb("q_rot_sin", [P, N]), sb("k_rot_sin", [P, N])]
        parts = [sb("qparts", [P, 3, N], BF16), sb("kparts", [P, 3, N], BF16)]
        v_new = sb("v_new", [P, NT, P])
        qs = [sb(f"qs{k}", [K_ALL, H, N], BF16) for k in range(2)]
        ks = [sb(f"ks{k}", [K_ALL, H, N], BF16) for k in range(2)]
        v_aug = [sb(f"v_aug{k}", [P, NT, H, V_W]) for k in range(2)]
        rowmax = sb("rowmax", [P, NT, H])
        mparts = [sb(f"mparts{f}", [P, NT, P // HALF, HALF], BF16) for f in range(2)]
        mT = [sb(f"mT{f}", [3 * HALF, N], BF16) for f in range(2)]
        probs = sb("probs", [P, RING, N])
        oT = sb("oT", [P, N])
        inv = sb("inv", [P, NT, 4])
        o_tok = sb("o_tok", [P, NT, P])
        o_tokT = sb("o_tokT", [P, N])
        junk = sb("junk", [P, 4])

        weights_in = sem("weights_in")
        stacks_set = [sem(f"stacks_set{k}") for k in range(2)]
        var_ready = sem("var_ready")
        rstd_ready = sem("rstd_ready")
        xn_ready = sem("xn_ready")
        xT_psum = sem("xT_psum")
        xT_ready = sem("xT_ready")
        proj_psum = sem("proj_psum")
        rope_read = sem("rope_read")
        rot_used = sem("rot_used")
        parts_ready = sem("parts_ready")
        v_psum = sem("v_psum")
        v_read = sem("v_read")
        v_ready = sem("v_ready")
        stack_in = [sem(f"stack_in{f}") for f in range(2)]
        score_psum = sem("score_psum")
        max_read = sem("max_read")
        mparts_ready = sem("mparts_ready")
        mT_psum = sem("mT_psum")
        mT_ready = sem("mT_ready")
        m_in = [sem(f"m_in{f}") for f in range(2)]
        exp_psum = sem("exp_psum")
        exp_ready = sem("exp_ready")
        pv_done = sem("pv_done")
        o_read = sem("o_read")
        oT_psum = sem("oT_psum")
        o_norm = sem("o_norm")
        o_tokT_psum = sem("o_tokT_psum")
        o_tokT_ready = sem("o_tokT_ready")
        out_psum = sem("out_psum")
        x_done = sem("x_done")

        ps_exp = [m.psum[:, 0, :], m.psum[:, 1, :]]
        ps_score = [m.psum[:, 2, :], m.psum[:, 3, :]]
        ps_o = [m.psum[:, 4, :], m.psum[:, 5, :]]
        is_first = lambda n: isinstance(n, int)
        score_bank = lambda n, j: (ps_score + ps_exp)[j % 4] if is_first(n) else ps_score[j % 2]
        ps_a, ps_b = m.psum[:, 6, :], m.psum[:, 7, :]
        tiles = lambda bank: bank.rearrange("p (t c) -> p t c", c=P)
        ps_mT = m.psum[:, 6, 0:N // 2].bitcast(BF16)
        x_of = m.x
        BODIES = NB // 2
        BLOCKS = 2 * len(PAIRS)
        N_WEIGHTS = 16 * 8

        block = ctx.enter_context(nc.Block())

        @block.sync
        def _(sp):
            for dst, src in ((w_proj, "w_proj"), (w_v, "w_v"), (w_o, "wo_T"), (cos, "cos"), (sin, "sin"),
                             (ident_b, "ident_b"), (mask_qk, "mask_qk"), (mask_kq, "mask_kq")):
                sp.dma_start(dst[:], w[src]).then_inc(weights_in, 16)

            def stack(f, k, count):
                sp.wait_ge(parts_ready, count)
                for side, stacks in enumerate((qs, ks)):
                    for n, pair in enumerate(PAIRS):
                        sp.dma_start(stacks[k][n * DH:(n + 1) * DH, f * HALF:(f + 1) * HALF, :],
                                     parts[side][f * P // 2:(f + 1) * P // 2, pair[side], :]).then_inc(stack_in[f], 16)

            def maxima(f, k, n):
                sp.wait_ge(mT_ready, n * 2 + (f + 1))
                sp.dma_start(qs[k][K_QK:K_ALL, f * HALF:(f + 1) * HALF, :], mT[f][:, :]).then_inc(m_in[f], 16)

            sp.wait_ge(stacks_set[0], 4)
            stack(0, 0, 1)
            stack(1, 0, 1)
            sp.wait_ge(stacks_set[1], 4)
            stack(0, 1, 2)
            maxima(0, 0, 0)
            stack(1, 1, 2)
            with sp.Fori(0, BODIES) as i:
                for k in range(2):
                    maxima(1, k, i * 2 + k)
                    for f in range(2):
                        sp.wait_ge(exp_psum, (i * 2 + k) * UNITS + (f + 1) * UNITS // 2)
                        stack(f, k, i * 2 + (k + 3))
                        if f == 0:
                            maxima(0, 1 - k, i * 2 + (k + 1))
            for f in range(2):
                sp.wait_ge(stack_in[f], 16 * BLOCKS * (NB + 2))
            sp.wait_ge(m_in[0], 16 * (NB + 1))
            sp.wait_ge(m_in[1], 16 * NB)

        def set_stacks(engine, k, stacks, values):
            for stack, value in stacks:
                engine.memset(stack[k][:, :, :], value).then_inc(stacks_set[k], 1)
            if values:
                engine.memset(v_aug[k][:, :, :, :], 0.0).then_inc(stacks_set[k], 1)
                engine.drain()
                engine.memset(v_aug[k][:, :, :, DH:DH + 1], 1.0).then_inc(stacks_set[k], 1)

        @block.gpsimd
        def _(pool):
            def inverse_std(count):
                pool.wait_ge(var_ready, count)
                pool.tensor_tensor(rstd[:, :], var_eps[:, :], m.minus_half[:, 0:NT], ALU.pow).then_inc(rstd_ready, 1)

            def split(count, copied, sides=(0, 1)):
                for side in sides:
                    part, r = parts[side], rot[side]
                    pool.wait_ge(rope_read, count * 4 + (side * 2 - 2))
                    if side == 0 and copied is not None:
                        for f in range(2):
                            pool.wait_ge(stack_in[f], copied * (16 * BLOCKS))
                    pool.tensor_tensor(part[:, 0, :], r[:, :], rot_sin[side][:, :], ALU.add)
                    pool.tensor_tensor(r[:, :], r[:, :], rot_sin[side][:, :], ALU.add)
                    pool.drain()
                    pool.tensor_tensor(part[:, 1, :], r[:, :], part[:, 0, :], ALU.subtract)
                    pool.tensor_tensor(r[:, :], r[:, :], part[:, 0, :], ALU.subtract)
                    pool.drain()
                    pool.tensor_tensor(part[:, 2, :], r[:, :], part[:, 1, :], ALU.subtract).then_inc(rot_used, 1)
                    if side == 1:
                        pool.drain()
                        pool.memset(junk[:, 0:1], 0.0).then_inc(parts_ready, 1)

            inverse_std(1)
            set_stacks(pool, 0, ((ks, -1.0),), True)
            split(1, None, (0,))
            inverse_std(2)
            split(1, None, (1,))
            set_stacks(pool, 1, ((ks, -1.0),), True)
            split(2, 1)
            with pool.Fori(0, BODIES) as i:
                for k in range(2):
                    inverse_std(i * 2 + (k + 3))
                    split(i * 2 + (k + 3), i * 2 + (k + 2))

        @block.scalar
        def _(act):
            def turn(count):
                act.wait_ge(xT_psum, count)
                act.activation(xT[:, :], ps_a, ACT.Copy).then_inc(xT_ready, 1)

            def read_v(count):
                act.wait_ge(v_psum, count)
                act.activation(v_new[:, :, :], tiles(ps_a), ACT.Copy).then_inc(v_read, 1)

            act.activation(junk[:, 2:3], m.half[:, 0:1], ACT.Exp).then_inc(exp_ready, 1)
            act.activation(junk[:, 3:4], m.half[:, 0:1], ACT.Exp).then_inc(exp_ready, 1)
            act.activation(junk[:, 1:2], m.half[:, 0:1], ACT.Exp).then_inc(o_read, 1)
            act.drain()
            def values(k):
                act.activation(v_aug[k][:, :, :, 0:DH], v_new[:, :, :].rearrange("p t (h d) -> p t h d", d=DH),
                               ACT.Copy).then_inc(v_ready, 1)

            for s in range(2):
                turn(s + 1)
                read_v(s + 1)
                act.drain()
                if s == 0:
                    act.wait_ge(stacks_set[0], 4)
                    values(0)
            act.wait_ge(stacks_set[1], 4)

            def end_of(s):
                act.wait_ge(pv_done, s * (GROUPS * NT) + 4)
                act.wait_ge(oT_psum, s * 4 + 1)
                act.activation(oT[:, :], ps_o[1], ACT.Copy).then_inc(o_read, 1)

            def tokens_of(s):
                act.wait_ge(o_tokT_psum, s + 1)
                act.activation(o_tokT[:, :], ps_a, ACT.Copy).then_inc(o_tokT_ready, 1)

            with act.Fori(0, BODIES) as i:
                for k in range(2):
                    s = i * 2 + k

                    def read_o(g):
                        act.wait_ge(pv_done, s * (GROUPS * NT) + (4 + NT * (g + 1)))
                        act.wait_ge(oT_psum, s * 4 + (g + 2))
                        act.activation(oT[:, :], ps_o[g % 2], ACT.Copy).then_inc(o_read, 1)

                    for j in range(UNITS):
                        g, (kt, heads) = j // RING, FILLS[j % RING]
                        n = len(heads) * width_of(kt)
                        act.wait_ge(exp_psum, s * UNITS + (j + 1))
                        act.wait_ge(pv_done, s * (GROUPS * NT) + (g * NT + kt + 1))
                        act.activation(probs[:, j % RING, 0:n], ps_exp[j % 2][:, 0:n], ACT.Exp,
                                       scale=SCALE).then_inc(exp_ready, 1)
                        if j == 0:
                            end_of(s)
                        if j == 2:
                            values(1 - k)
                        if j == A_TOKENS:
                            tokens_of(s)
                        if j == A_TURN:
                            turn(s + 3)
                        if j == A_V:
                            read_v(s + 3)
                        if j in A_O:
                            read_o(A_O.index(j))
            end_of(NB)
            tokens_of(NB)

        @block.tensor
        def _(pe):
            def turn(count):
                pe.wait_ge(xn_ready, count)
                for t in range(NT):
                    last = pe.transpose(ps_a[:, t * P:(t + 1) * P], xn[:, t, :], m.ident[:, :])
                last.then_inc(xT_psum, 1)

            def project(side, count):
                if side == 0:
                    pe.wait_ge(xT_ready, count)
                    pe.wait_ge(x_done, count)
                else:
                    pe.wait_ge(rope_read, count * 4 - 2)
                pe.matmul(ps_a, w_proj[:, 2 * side, :], xT[:, :], start=True, stop=True)
                pe.matmul(ps_b, w_proj[:, 2 * side + 1, :], xT[:, :], start=True, stop=True).then_inc(proj_psum, 1)

            def values(count):
                pe.wait_ge(rope_read, count * 4)
                for t in range(NT):
                    last = pe.matmul(ps_a[:, t * P:(t + 1) * P], xT[:, t * P:(t + 1) * P], w_v[:, :],
                                     start=True, stop=True)
                last.then_inc(v_psum, 1)

            def score(k, n, j):
                g, (w, heads) = j // RING, FILLS[j % RING]
                qt, n_keys = NT - 1 - w, width_of(w)
                if not is_first(n):
                    pe.wait_ge(max_read, n * UNITS + (j + 1))
                elif j >= 4:
                    pe.wait_ge(max_read, j - 1)
                if j % (UNITS // 2) == 0:
                    pe.wait_ge(stack_in[2 * j // UNITS], n * (16 * BLOCKS) + 16 * BLOCKS)
                for a, hh in enumerate(heads):
                    out = score_bank(n, j)[:, a * n_keys:(a + 1) * n_keys]
                    pe.matmul(out, qs[k][0:K_QK, 4 * g + hh, qt * P:(qt + 1) * P],
                              ks[k][0:K_QK, 4 * g + hh, 0:n_keys], start=True, stop=False)
                    last = pe.matmul(out[:, qt * P:n_keys], ident_b[:, :], mask_qk[:, :], start=False, stop=True)
                last.then_inc(score_psum, 1)

            def turn_maxima(f, n):
                pe.wait_ge(mparts_ready, n * 2 + (f + 1))
                for t in range(NT):
                    last = pe.transpose(ps_mT[:, t * P:(t + 1) * P], mparts[f][:, t].rearrange("p a h -> p (a h)"),
                                        ident_b[:, :])
                last.then_inc(mT_psum, 1)

            def turn_last_o(s):
                pe.wait_ge(o_read, s * 4 + 2)
                for t in range(NT):
                    last = pe.transpose(ps_b[:, t * P:(t + 1) * P], oT[:, t * P:(t + 1) * P], m.ident[:, :])
                last.then_inc(oT_psum, 1)

            def turn_tokens(s):
                pe.wait_ge(o_norm, s * 4 + 1)
                if not isinstance(s, int):
                    pe.wait_ge(mT_ready, s * 2 + 2)
                for t in range(NT):
                    last = pe.transpose(ps_a[:, t * P:(t + 1) * P], o_tok[:, t, :], m.ident[:, :])
                last.then_inc(o_tokT_psum, 1)

            def project_out(s):
                pe.wait_ge(o_tokT_ready, s + 1)
                for t in range(NT):
                    last = pe.matmul(ps_b[:, t * P:(t + 1) * P], o_tokT[:, t * P:(t + 1) * P], w_o[:, :],
                                     start=True, stop=True)
                last.then_inc(out_psum, 1)

            for k in range(2):
                turn(k + 1)
                if k == 0:
                    pe.wait_ge(weights_in, N_WEIGHTS)
                else:
                    pe.wait_ge(v_read, 1)
                project(0, k + 1)
                project(1, k + 1)
                values(k + 1)
                if k == 0:
                    pe.wait_ge(v_read, 1)
            pe.wait_ge(v_read, 2)
            for j in range(UNITS):
                score(0, 0, j)
            turn_maxima(0, 0)
            pe.wait_ge(mT_ready, 1)
            with pe.Fori(0, BODIES) as i:
                for k in range(2):
                    s = i * 2 + k

                    def exponent(j):
                        g, (kt, heads) = j // RING, FILLS[j % RING]
                        n = width_of(kt)
                        pe.wait_ge(exp_ready, s * UNITS + (j + 1))
                        if j % (UNITS // 2) == 0:
                            pe.wait_ge(m_in[2 * j // UNITS], s * 16 + 16)
                        for a, hh in enumerate(heads):
                            out = ps_exp[j % 2][:, a * n:(a + 1) * n]
                            pe.matmul(out, ks[k][:, 4 * g + hh, kt * P:(kt + 1) * P],
                                      qs[k][:, 4 * g + hh, kt * P:N], start=True, stop=False)
                            last = pe.matmul(out[:, 0:P], ident_b[:, :], mask_kq[:, :], start=False, stop=True)
                        last.then_inc(exp_psum, 1)

                    def weigh(g, kt):
                        n = width_of(kt)
                        fills = {hh: (f, a * n) for f, (w, heads) in enumerate(FILLS) if w == kt
                                 for a, hh in enumerate(heads)}
                        pe.wait_ge(exp_ready, s * UNITS + (2 + g * RING + fills[3][0] + 1))
                        if g == 0 and kt == 0:
                            pe.wait_ge(v_ready, s + 1)
                        if kt == 0:
                            pe.wait_ge(o_read, s * 4 + (g + 1))
                        for hh in range(4):
                            f, at = fills[hh]
                            last = pe.matmul(ps_o[g % 2][32 * hh:32 * hh + 32, kt * P:N], v_aug[k][:, kt, 4 * g + hh, :],
                                             probs[:, f, at:at + n], start=(kt == 0), stop=(kt == NT - 1),
                                             tile_position=(0, 32 * hh))
                        last.then_inc(pv_done, 1)

                    weigh_at = {g * RING + max(f for f, (w, _) in enumerate(FILLS) if w == kt) + 2: (g, kt)
                                for g in range(GROUPS) for kt in range(NT)}

                    def turn_o(g):
                        pe.wait_ge(o_read, s * 4 + (2 + g + 1))
                        if g > 0:
                            pe.wait_ge(o_norm, s * 4 + (g + 1))
                        else:
                            pe.wait_ge(rope_read, (s + 3) * 4)
                        for t in range(NT):
                            last = pe.transpose(ps_b[:, t * P:(t + 1) * P], oT[:, t * P:(t + 1) * P], m.ident[:, :])
                        last.then_inc(oT_psum, 1)

                    for j in range(UNITS):
                        exponent(j)
                        score(1 - k, s + 1, j)
                        if j in weigh_at:
                            weigh(*weigh_at[j])
                        if j == E_MAXIMA:
                            turn_maxima(1, s)
                        if j == E_LAST_O:
                            turn_last_o(s)
                        if j == E_TOKENS:
                            turn_tokens(s)
                        if j == E_OUT:
                            project_out(s)
                        if j == E_TURN:
                            turn(s + 3)
                        if j == E_Q:
                            project(0, s + 3)
                        if j == E_K:
                            project(1, s + 3)
                        if j == E_V:
                            values(s + 3)
                        if j == E_HALF:
                            pe.wait_ge(v_read, s + 3)
                            turn_maxima(0, s + 1)
                        if j in E_O:
                            turn_o(E_O.index(j))
                    weigh(GROUPS - 1, NT - 2)
                    weigh(GROUPS - 1, NT - 1)
            pe.wait_ge(o_norm, NB * 4)
            turn_last_o(NB)
            turn_tokens(NB)
            project_out(NB)

        @block.vector
        def _(dve):
            def moments(tile):
                for t in range(NT):
                    dve.bn_stats(stats[:, t, :], x_of[:, tile + (t + m.first), :])
                dve.drain()
                for t in range(NT):
                    dve.bn_aggr(mv[:, t, :], stats[:, t, :])
                dve.drain()
                dve.tensor_scalar(var_eps[:, :], mv[:, :, 1], LN_EPS, None, ALU.add).then_inc(var_ready, 1)

            def normalise_x(tile, count):
                dve.wait_ge(rstd_ready, count)
                for t in range(NT):
                    last = dve.tensor_scalar(xn[:, t, :], x_of[:, tile + (t + m.first), :], mv[:, t, 0:1], rstd[:, t:t + 1],
                                             ALU.subtract, ALU.mult)
                last.then_inc(xn_ready, 1)

            def rotate(side, count, tables=(0, 1)):
                if 0 in tables:
                    dve.wait_ge(proj_psum, count * 2 + (side - 1))
                    if not isinstance(count, int) or count > 1:
                        dve.wait_ge(rot_used, count * 2 + (side - 3))
                    dve.tensor_tensor(rot[side][:, :], ps_a, cos[:, :], ALU.mult).then_inc(rope_read, 1)
                if 1 in tables:
                    dve.tensor_tensor(rot_sin[side][:, :], ps_b, sin[:, :], ALU.mult).then_inc(rope_read, 1)

            def row_max(n, j):
                g, (w, heads) = j // RING, FILLS[j % RING]
                h = 4 * g + heads[0]
                dve.wait_ge(score_psum, n * UNITS + (j + 1))
                dve.tensor_reduce(rowmax[:, NT - 1 - w, h:h + len(heads)],
                                  score_bank(n, j)[:, 0:len(heads) * width_of(w)].rearrange("p (a c) -> p a c", a=len(heads)),
                                  AX.X, ALU.max).then_inc(max_read, 1)

            def split_maxima(f):
                r, parts_of = rowmax[:, :, f * HALF:(f + 1) * HALF], mparts[f]
                dve.drain()
                dve.tensor_copy(parts_of[:, :, 0, :], r)
                dve.drain()
                dve.tensor_tensor(r, r, parts_of[:, :, 0, :], ALU.subtract)
                dve.drain()
                dve.tensor_copy(parts_of[:, :, 1, :], r)
                dve.drain()
                dve.tensor_tensor(parts_of[:, :, 2, :], r, parts_of[:, :, 1, :], ALU.subtract).then_inc(mparts_ready, 1)

            def read_maxima(f, n):
                dve.wait_ge(mT_psum, n * 2 + (f + 1))
                dve.tensor_copy(mT[f][:, :], ps_mT[0:3 * HALF]).then_inc(mT_ready, 1)

            def normalise(o, channels, count):
                dve.wait_ge(oT_psum, count)
                dve.reciprocal(inv[:, :, :], o[:, :, :, DH])
                dve.drain()
                dve.tensor_tensor(o_tok[:, :, channels].rearrange("p t (h d) -> p t h d", d=DH),
                                  o[:, :, :, 0:DH], along(inv[:, :, :], 3, DH), ALU.mult).then_inc(o_norm, 1)

            o_heads = tiles(ps_b).rearrange("p t (h c) -> p t h c", c=V_W)
            channels_of = lambda g: slice(4 * DH * g, 4 * DH * (g + 1))

            def add_out(s):
                dve.wait_ge(out_psum, s + 1)
                x = x_of[:, bass.ds(s * NT + m.first - NT, NT), :]
                dve.tensor_tensor(x, tiles(ps_b), x, ALU.add).then_inc(x_done, 1)

            dve.memset(rowmax[:, 0, 0:1], 0.0).then_inc(max_read, 1)
            dve.memset(rowmax[:, 0, 1:2], 0.0).then_inc(max_read, 1)
            dve.memset(rowmax[:, 0, 2:3], 0.0).then_inc(x_done, 1)
            dve.memset(rowmax[:, 0, 3:4], 0.0).then_inc(x_done, 1)
            for f in range(2):
                dve.memset(mparts[f][:, :, 3:P // HALF, :], 0.0)
            dve.memset(ps_o[1], 1.0).then_inc(pv_done, 1)
            for c in range(3):
                dve.memset(oT[:, c:c + 1], 0.0).then_inc(pv_done, 1)
            dve.memset(o_tok[:, :, :], 0.0).then_inc(oT_psum, 1)
            dve.drain()

            for s in range(2):
                moments(s * NT)
                normalise_x(s * NT, s + 1)
                if s == 0:
                    set_stacks(dve, 0, ((qs, 0.0),), False)
                    dve.wait_ge(weights_in, N_WEIGHTS)
                rotate(0, s + 1)
                rotate(1, s + 1)
            set_stacks(dve, 1, ((qs, 0.0),), False)
            for j in range(UNITS):
                row_max(0, j)
                if j == UNITS // 2 - 1:
                    split_maxima(0)
            split_maxima(1)
            read_maxima(0, 0)
            with dve.Fori(0, BODIES) as i:
                for k in range(2):
                    s = i * 2 + k
                    for j in range(UNITS):
                        row_max(s + 1, j)
                        if j == 1:
                            moments((s + 2) * NT)
                        if j == V_MAXIMA:
                            read_maxima(1, s)
                        if j == V_LAST_O:
                            normalise(o_heads, channels_of(3), s * 4 + 2)
                        if j == V_NORM:
                            normalise_x((s + 2) * NT, s + 3)
                        if j == V_OUT:
                            add_out(s)
                        if j in (V_Q, V_Q + 1):
                            rotate(0, s + 3, (j - V_Q,))
                        if j in (V_K, V_K + 1):
                            rotate(1, s + 3, (j - V_K,))
                        if j in V_O:
                            g = V_O.index(j)
                            normalise(o_heads, channels_of(g), s * 4 + (g + 3))
                        if j == V_HALF:
                            split_maxima(0)
                        if j == V_HALF_READ:
                            read_maxima(0, s + 1)
                    split_maxima(1)
            normalise(o_heads, channels_of(3), NB * 4 + 2)
            add_out(NB)




def expert_stage(nc, m, name, ex):
    G = NT
    PASSES = TILES // G
    N = G * P
    E_S, E_R, HID = 2, 8, 512
    E = E_S + E_R
    C = HID // P
    T_GATES, T_SPREAD = 3, 4
    T_STATS, T_RMS, T_NORM = 5, 6, 7
    SPREADS = 6
    POOL_C = 3
    with ExitStack() as ctx:
        def sb(n, shape, dt=F32):
            return ctx.enter_context(nc.sbuf_tensor(f"{name}_{n}", shape, dt))

        def sem(n):
            return ctx.enter_context(nc.semaphore(f"{name}_{n}"))

        euler = sb("euler", [P, G, E_R])
        stats = sb("stats", [P, G, 6])
        mv = sb("mv", [P, G, 2])
        var_eps = sb("var_eps", [P, G])
        rstd = sb("rstd", [P, G])
        ms_eps = sb("ms_eps", [P, G])
        rms_inv = sb("rms_inv", [P, G])
        rms = sb("rms", [P, G])
        rr = sb("rr", [P, G])
        xn = sb("xn", [P, G, P])
        u = sb("u", [P, G, P])
        xT = sb("xT", [P, N])
        xTh = sb("xTh", [P, N], F32R)
        xTl = sb("xTl", [P, N], F32R)
        logit = sb("logit", [P, G, E_R])
        score = sb("score", [P, G, E_R])
        ssum = sb("ssum", [P, G])
        top = sb("top", [P, G, 8])
        idx = sb("idx", [P, G, 8], U32)
        idxf = sb("idxf", [P, G, 2])
        gk = sb("gk", [P, G, 2])
        hot0 = sb("hot0", [P, G, E_R])
        hot1 = sb("hot1", [P, G, E_R])
        gates = sb("gates", [P, G, E])
        g_high = sb("g_high", [P, G, E], F32R)
        g_parts = sb("g_parts", [P, G, 2 * E])
        gTp = sb("gTp", [P, N], F32R)
        spread = sb("spread", [P, SPREADS, N])
        h = sb("h", [P, 2, C, N])
        hh = sb("hh", [P, 2, C, N], F32R)
        hl = sb("hl", [P, 2, C, N], F32R)
        weighted = sb("weighted", [P, 2, N])
        acc = sb("acc", [P, N])

        pool_const = sem("pool_const")
        var_ready = sem("var_ready")
        rstd_ready = sem("rstd_ready")
        ms_ready = sem("ms_ready")
        rms_ready = sem("rms_ready")
        xn_ready = sem("xn_ready")
        xT_psum = sem("xT_psum")
        xT_ready = sem("xT_ready")
        xTl_ready = sem("xTl_ready")
        logit_psum = sem("logit_psum")
        logit_ready = sem("logit_ready")
        exp_ready = sem("exp_ready")
        gates_ready = sem("gates_ready")
        gT_psum = sem("gT_psum")
        gT_ready = sem("gT_ready")
        spread_psum = sem("spread_psum")
        spread_ready = sem("spread_ready")
        h_psum = sem("h_psum")
        h_ready = sem("h_ready")
        high_ready = sem("high_ready")
        low_ready = sem("low_ready")
        pool_low_ready = sem("pool_low_ready")
        y_ready = sem("y_ready")
        y_used = sem("y_used")
        added = sem("added")
        summed = sem("summed")
        sumT_psum = sem("sumT_psum")
        x_done = sem("x_done")

        ps_h = m.psum[:, 0:C, :]
        ps_y = m.psum[:, C:C + 2, :]
        ps_m = m.psum[:, 6, :]
        ps_n = m.psum[:, 7, :]
        tiles = lambda bank: bank.rearrange("p (t c) -> p t c", c=P)
        ps_logit = ps_n[:, 0:G * E_R].rearrange("p (t e) -> p t e", e=E_R)
        x_of = m.x
        Y = E_R + 1

        block = ctx.enter_context(nc.Block())

        @block.gpsimd
        def _(pool):
            pool.memset(euler[:, :, :], float(np.e)).then_inc(pool_const, 1)
            pool.memset(acc[:, :], 0.0).then_inc(summed, 1)
            pool.wait_ge(pool_const, 1)

            def rstd_of(count):
                pool.wait_ge(var_ready, count)
                pool.tensor_tensor(rstd[:, :], var_eps[:, :], m.minus_half[:, 0:G], ALU.pow).then_inc(rstd_ready, 1)

            def rms_of(count):
                pool.wait_ge(ms_ready, count)
                pool.tensor_tensor(rms_inv[:, :], ms_eps[:, :], m.minus_half[:, 0:G], ALU.pow)
                pool.tensor_tensor(rms[:, :], ms_eps[:, :], m.half[:, 0:G], ALU.pow).then_inc(rms_ready, 1)

            rstd_of(1)
            rms_of(1)
            with pool.Fori(0, PASSES) as i:
                for e in range(E):
                    if e >= E_S + 2:
                        pool.wait_ge(y_used, i * Y + (e - E_S + 2))
                        pool.tensor_tensor(acc[:, :], acc[:, :], weighted[:, e % 2, :], ALU.add).then_inc(added, 1)
                        pool.drain()
                    pool.wait_ge(high_ready, i * E + (e + 1))
                    if e >= 2:
                        pool.wait_ge(y_ready, i * E + (e - 1))
                    pool.tensor_tensor(hl[:, e % 2, POOL_C, :], h[:, e % 2, POOL_C, :], hh[:, e % 2, POOL_C, :].bitcast(F32),
                                       ALU.subtract).then_inc(pool_low_ready, 1)
                    if e == 0:
                        pool.wait_ge(logit_ready, i + 1)
                        pool.tensor_tensor(score[:, :, :], euler[:, :, :], logit[:, :, :], ALU.pow).then_inc(exp_ready, 1)
                    if e == T_STATS:
                        rstd_of(i + 2)
                    if e == T_RMS:
                        rms_of(i + 2)
                pool.wait_ge(y_used, i * Y + (1 + Y))
                pool.tensor_tensor(acc[:, :], acc[:, :], weighted[:, E % 2, :], ALU.add).then_inc(added, 1)
                pool.drain()
                pool.wait_ge(y_used, i * Y + (2 + Y))
                pool.tensor_tensor(acc[:, :], acc[:, :], weighted[:, (E - 1) % 2, :], ALU.add).then_inc(summed, 1)

        @block.scalar
        def _(act):
            def turn(count):
                act.wait_ge(xT_psum, count)
                act.activation(xT[:, :], ps_m, ACT.Copy)
                act.activation(xTh[:, :], ps_m, ACT.Copy).then_inc(xT_ready, 1)

            turn(1)
            with act.Fori(0, PASSES) as i:
                for e in range(E):
                    for c in range(C):
                        act.wait_ge(h_psum, i * (E * C) + (e * C + c + 1))
                        if e >= 2 and c == 0:
                            act.wait_ge(high_ready, i * E + (e - 1))
                            act.wait_ge(low_ready, i * E + (e - 1))
                        if e >= 2 and c == POOL_C:
                            act.wait_ge(pool_low_ready, i * E + (e - 1))
                        act.activation(h[:, e % 2, c, :], ps_h[:, c, :], ACT.Gelu,
                                       bias=ex.b1[:, e * C + c:e * C + c + 1]).then_inc(h_ready, 1)
                    if e == T_GATES:
                        act.wait_ge(gT_psum, i + 1)
                        act.activation(gTp[0:2 * E, :], ps_n[0:2 * E, :], ACT.Copy).then_inc(gT_ready, 1)
                    if e >= T_SPREAD and e < T_SPREAD + 4:
                        for q in range(2 * (e - T_SPREAD), 2 * (e - T_SPREAD) + 2):
                            act.wait_ge(spread_psum, i * E_R + (q + 1))
                            if q >= SPREADS:
                                act.wait_ge(y_used, i * Y + (2 + q - SPREADS + E_S))
                            act.activation(spread[:, q % SPREADS, :], (ps_m, ps_n)[q % 2], ACT.Copy).then_inc(spread_ready, 1)
                turn(i + 2)

        @block.tensor
        def _(pe):
            def turn(count):
                pe.wait_ge(xn_ready, count)
                for t in range(G):
                    last = pe.transpose(ps_m[:, t * P:(t + 1) * P], xn[:, t, :], m.ident[:, :])
                last.then_inc(xT_psum, 1)

            def turn_sum(count):
                pe.wait_ge(summed, count)
                for t in range(G):
                    last = pe.transpose(ps_n[:, t * P:(t + 1) * P], acc[:, t * P:(t + 1) * P], m.ident[:, :])
                last.then_inc(sumT_psum, 1)

            turn(1)
            with pe.Fori(0, PASSES) as i:
                def up(e):
                    for c in range(C):
                        if e >= 1:
                            pe.wait_ge(h_ready, i * (E * C) + ((e - 1) * C + c + 1))
                        high, low = ex.high[:, e, c * P:(c + 1) * P], ex.low[:, e, c * P:(c + 1) * P]
                        pe.matmul(ps_h[:, c, :], high, xTh[:, :], start=True, stop=False)
                        pe.matmul(ps_h[:, c, :], high, xTl[:, :], start=False, stop=False)
                        pe.matmul(ps_h[:, c, :], low, xTh[:, :], start=False, stop=True).then_inc(h_psum, 1)

                def down(e):
                    pe.wait_ge(high_ready, i * E + (e + 1))
                    if e != 1:
                        pe.wait_ge(y_used, i * Y + max(e, 2))
                    bank = ps_y[:, 0 if e == 0 else (e - 1) % 2, :]
                    first, last = e != 1, e >= 1
                    for c in range(C):
                        high, low = ex.high[:, E + e, c * P:(c + 1) * P], ex.low[:, E + e, c * P:(c + 1) * P]
                        pe.matmul(bank, high, hh[:, e % 2, c, :], start=(first and c == 0), stop=False)
                        pe.matmul(bank, low, hh[:, e % 2, c, :], start=False, stop=False)
                        if c == 0:
                            pe.wait_ge(low_ready, i * E + (e + 1))
                        if c == POOL_C:
                            pe.wait_ge(pool_low_ready, i * E + (e + 1))
                        mm = pe.matmul(bank, high, hl[:, e % 2, c, :], start=False, stop=(last and c == C - 1))
                    mm.then_inc(y_ready, 1)

                def spread_gates(q):
                    if q == 0:
                        pe.wait_ge(gT_ready, i + 1)
                    if q >= 2:
                        pe.wait_ge(spread_ready, i * E_R + (q - 1))
                    pe.matmul((ps_m, ps_n)[q % 2], ex.select[:, q, :], gTp[:, :],
                              start=True, stop=True).then_inc(spread_psum, 1)

                pe.wait_ge(xT_ready, i + 1)
                for t in range(G):
                    last = pe.matmul(ps_logit[:, t, :], xT[:, t * P:(t + 1) * P], ex.cent[:, :], start=True, stop=True)
                last.then_inc(logit_psum, 1)
                pe.wait_ge(xTl_ready, i + 1)
                up(0)
                pe.wait_ge(logit_ready, i + 1)
                turn_sum(i + 1)
                for e in range(1, E):
                    up(e)
                    if e == E - 1:
                        pe.wait_ge(spread_ready, i * E_R + E_R)
                        turn(i + 2)
                    if e >= T_SPREAD and e < T_SPREAD + 4:
                        spread_gates(2 * (e - T_SPREAD))
                        spread_gates(2 * (e - T_SPREAD) + 1)
                    down(e - 1)
                    if e == T_GATES:
                        pe.wait_ge(gates_ready, i + 1)
                        pe.wait_ge(x_done, i + 1)
                        for t in range(G):
                            last = pe.transpose(ps_n[0:2 * E, t * P:(t + 1) * P], g_parts[:, t, :], m.ident[:, :])
                        last.then_inc(gT_psum, 1)
                down(E - 1)
            turn_sum(PASSES + 1)

        @block.vector
        def _(dve):
            def moments(tile):
                for t in range(G):
                    dve.bn_stats(stats[:, t, :], x_of[:, tile + (t + m.first), :])
                dve.drain()
                for t in range(G):
                    dve.bn_aggr(mv[:, t, :], stats[:, t, :])
                dve.drain()
                dve.tensor_scalar(var_eps[:, :], mv[:, :, 1], LN_EPS, None, ALU.add).then_inc(var_ready, 1)

            def mean_square(count):
                dve.wait_ge(rstd_ready, count)
                dve.tensor_tensor(ms_eps[:, :], mv[:, :, 1], rstd[:, :], ALU.mult)
                dve.drain()
                dve.tensor_tensor(ms_eps[:, :], ms_eps[:, :], rstd[:, :], ALU.mult)
                dve.drain()
                dve.tensor_scalar(ms_eps[:, :], ms_eps[:, :], RMS_EPS, None, ALU.add).then_inc(ms_ready, 1)

            def normalise(tile, count):
                dve.wait_ge(rms_ready, count)
                dve.tensor_tensor(rr[:, :], rstd[:, :], rms_inv[:, :], ALU.mult)
                dve.drain()
                for t in range(G):
                    last = dve.tensor_scalar(xn[:, t, :], x_of[:, tile + (t + m.first), :], mv[:, t, 0:1], rr[:, t:t + 1],
                                             ALU.subtract, ALU.mult)
                last.then_inc(xn_ready, 1)

            dve.memset(gTp[:, :].bitcast(F32), 0.0)
            dve.memset(gates[:, :, :], 1.0).then_inc(y_used, 1)
            dve.memset(idxf[:, :, :], 0.0).then_inc(y_used, 1)
            dve.memset(u[:, :, :], 0.0)
            dve.drain()
            moments(0)
            mean_square(1)
            normalise(0, 1)

            def residual(i):
                dve.wait_ge(sumT_psum, i + 1)
                dve.tensor_tensor(u[:, :, :], tiles(ps_n), u[:, :, :], ALU.add)
                dve.drain()
                x = x_of[:, bass.ds(i * G + (m.first - G), G), :]
                dve.scalar_tensor_tensor(out=x, in0=u[:, :, :], scalar=0.5, in1=x, op0=ALU.mult,
                                         op1=ALU.add).then_inc(x_done, 1)
                dve.drain()

            def low_input(count):
                dve.wait_ge(xT_ready, count)
                dve.tensor_tensor(xTl[:, :], xT[:, :], xTh[:, :].bitcast(F32), ALU.subtract).then_inc(xTl_ready, 1)

            low_input(1)
            with dve.Fori(0, PASSES) as i:
                def scale_logits():
                    dve.wait_ge(logit_psum, i + 1)
                    dve.scalar_tensor_tensor(out=logit[:, :, :], in0=ps_logit, scalar=-1.0,
                                             in1=along(rms[:, :], 2, E_R), op0=ALU.mult,
                                             op1=ALU.mult).then_inc(logit_ready, 1)

                def input_of_experts():
                    for t in range(G):
                        dve.tensor_scalar(u[:, t, :], x_of[:, i * G + (t + m.first), :], mv[:, t, 0:1], rstd[:, t:t + 1],
                                          ALU.subtract, ALU.mult)

                def best_scores():
                    dve.wait_ge(exp_ready, i + 1)
                    dve.tensor_scalar(score[:, :, :], score[:, :, :], 1.0, None, ALU.add)
                    dve.drain()
                    dve.reciprocal(score[:, :, :], score[:, :, :])
                    dve.drain()
                    dve.tensor_reduce(ssum[:, :], score[:, :, :], AX.X, ALU.add)
                    for t in range(G):
                        dve.max(top[:, t, :], score[:, t, :])
                    dve.drain()
                    for t in range(G):
                        dve.max_index(idx[:, t, :], top[:, t, :], score[:, t, :])
                    dve.reciprocal(ssum[:, :], ssum[:, :])
                    dve.drain()

                def gates_of_best():
                    dve.tensor_copy(idxf[:, :, :], idx[:, :, 0:2])
                    dve.tensor_tensor(gk[:, :, :], top[:, :, 0:2], along(ssum[:, :], 2, 2), ALU.mult)
                    dve.drain()
                    for k, hot in enumerate((hot0, hot1)):
                        dve.tensor_tensor(hot[:, :, :], along(m.iota8[:, :], 1, G), along(idxf[:, :, k], 2, E_R),
                                          ALU.is_equal)
                    dve.drain()
                    for k, hot in enumerate((hot0, hot1)):
                        dve.tensor_tensor(hot[:, :, :], hot[:, :, :], along(gk[:, :, k], 2, E_R), ALU.mult)
                    dve.drain()
                    dve.tensor_tensor(gates[:, :, E_S:E], hot0[:, :, :], hot1[:, :, :], ALU.add)
                    dve.drain()
                    dve.tensor_copy(g_high[:, :, :], gates[:, :, :])
                    dve.drain()
                    dve.tensor_copy(g_parts[:, :, 0:E], g_high[:, :, :].bitcast(F32))
                    dve.tensor_tensor(g_parts[:, :, E:2 * E], gates[:, :, :], g_high[:, :, :].bitcast(F32),
                                      ALU.subtract).then_inc(gates_ready, 1)

                def split(e):
                    if e >= 2:
                        dve.wait_ge(y_ready, i * E + (e - 1))
                    pieces = ((0, C // 2), (C // 2, C)) if e in (0, E - 1) else ((0, C),)
                    for first, end in pieces:
                        dve.wait_ge(h_ready, i * (E * C) + (e * C + end))
                        high = dve.tensor_copy(hh[:, e % 2, first:end, :], h[:, e % 2, first:end, :])
                        dve.drain()
                        end_low = min(end, POOL_C)
                        low = dve.tensor_tensor(hl[:, e % 2, first:end_low, :], h[:, e % 2, first:end_low, :],
                                                hh[:, e % 2, first:end_low, :].bitcast(F32), ALU.subtract)
                        if end == C:
                            high.then_inc(high_ready, 1)
                            low.then_inc(low_ready, 1)

                def weigh(e):
                    dve.wait_ge(y_ready, i * E + (e + 1))
                    if e == 1:
                        dve.tensor_scalar(acc[:, :], ps_y[:, 0, :], ex.b2[:, 0:1], ex.b2[:, 1:2], ALU.add,
                                          ALU.add).then_inc(y_used, 1)
                    elif e > 1:
                        dve.wait_ge(spread_ready, i * E_R + (e - E_S + 1))
                        if e >= 4:
                            dve.wait_ge(added, i * (E_R - 1) + (e - 3))
                        dve.scalar_tensor_tensor(out=weighted[:, e % 2, :], in0=ps_y[:, (e - 1) % 2, :],
                                                 scalar=ex.b2[:, e:e + 1], in1=spread[:, (e - E_S) % SPREADS, :],
                                                 op0=ALU.add, op1=ALU.mult).then_inc(y_used, 1)

                scale_logits()
                for e in range(E):
                    if e > E_S and e != T_SPREAD:
                        weigh(e - 2)
                    split(e)
                    if e == T_SPREAD:
                        weigh(e - 2)
                    if e == 0:
                        residual(i)
                    if e == 1:
                        best_scores()
                    if e == 2:
                        gates_of_best()
                    if e == T_GATES:
                        input_of_experts()
                    if e == T_STATS:
                        moments(i * G + G)
                    if e == T_RMS:
                        mean_square(i + 2)
                    if e == T_NORM:
                        normalise(i * G + G, i + 2)
                low_input(i + 2)
                weigh(E - 2)
                weigh(E - 1)
            residual(PASSES)




def gla_stage(nc, m, name, w):
    DH = 8
    N = SEQ
    SCALE = DH ** -0.5
    DV_BANKS = 4
    TERMS = DH + 1
    with ExitStack() as ctx:
        def sb(n, shape, dt=F32):
            return ctx.enter_context(nc.sbuf_tensor(f"{name}_{n}", shape, dt))

        def sem(n):
            return ctx.enter_context(nc.semaphore(f"{name}_{n}"))

        w_qf = sb("w_qf", [P, 2 * P])
        w_i = sb("w_i", [P, P])
        select = sb("select", [P, DH, P], F32R)
        select_raw = sb("select_raw", [P, DH, P])
        w_orep = sb("w_orep", [P, DH, P])
        w_o = sb("w_o", [P, P])
        head_ones = sb("head_ones", [P, P])
        stats = sb("stats", [P, NT, 6])
        mv = sb("mv", [P, NT, 2])
        var_eps = sb("var_eps", [P, NT])
        rstd = sb("rstd", [P, NT])
        xn = sb("xn", [P, NT, P])
        xT = sb("xT", [P, N])
        dv = sb("dv", [P, N])
        dv_high = [sb(f"dv_high{k}", [P, N], F32R) for k in range(2)]
        dv_low = [sb(f"dv_low{k}", [P, N], F32R) for k in range(2)]
        xTk = [sb(f"xT{k}", [P, N]) for k in range(2)]
        nmax = sb("nmax", [P, 2 * NT])
        qf = sb("qf", [P, 2 * NT, P])
        qfsum = sb("qfsum", [P, 2 * NT])
        qfinv = sb("qfinv", [P, 2 * NT])
        qT = [sb(f"qT{k}", [P, N]) for k in range(2)]
        pT = [sb(f"pT{k}", [P, N]) for k in range(2)]
        vT = [sb(f"vT{k}", [P, N]) for k in range(2)]
        state = [sb(f"state{k}", [P, TERMS, N]) for k in range(2)]

        weights_in = sem("weights_in")
        var_ready = sem("var_ready")
        rstd_ready = sem("rstd_ready")
        xn_ready = sem("xn_ready")
        xT_psum = sem("xT_psum")
        xT_ready = sem("xT_ready")
        select_ready = sem("select_ready")
        v_psum = sem("v_psum")
        diff_ready = sem("diff_ready")
        dv_high_ready = sem("dv_high_ready")
        dv_low_ready = sem("dv_low_ready")
        qf_psum = sem("qf_psum")
        nmax_ready = sem("nmax_ready")
        qf_exp = sem("qf_exp")
        qf_ready = sem("qf_ready")
        qpT_psum = sem("qpT_psum")
        qpT_ready = sem("qpT_ready")
        dv_psum = sem("dv_psum")
        dv_used = sem("dv_used")
        o_used = sem("o_used")
        term_ready = sem("term_ready")
        vT_ready = sem("vT_ready")
        o_psum = sem("o_psum")

        ps_T = m.psum[:, 0, :]
        ps_qf = m.psum[:, 1:3, :].rearrange("p k (t c) -> p (k t) c", c=P)
        ps_qT, ps_pT = m.psum[:, 1, :], m.psum[:, 2, :]
        ps_dv = [m.psum[:, 3 + k, :] for k in range(DV_BANKS)]
        ps_o = m.psum[:, 7, :].rearrange("p (t c) -> p t c", c=P)
        x_of = m.x
        USES = DH + 2
        V_USE = 6
        use_of = lambda j: j if j < V_USE else j + 1

        block = ctx.enter_context(nc.Block())

        @block.sync
        def _(sp):
            for dst, src in ((w_qf, "w_qf"), (w_i, "w_i"), (select_raw, "select_v"), (w_orep, "w_orep"),
                             (w_o, "w_o"), (head_ones, "head_ones")):
                sp.dma_start(dst[:], w[src]).then_inc(weights_in, 16)

        N_WEIGHTS = 16 * 6
        BODIES = NB // 2

        @block.gpsimd
        def _(pool):
            def inv_std(count):
                pool.wait_ge(var_ready, count)
                pool.tensor_tensor(rstd[:, :], var_eps[:, :], m.minus_half[:, 0:NT], ALU.pow).then_inc(rstd_ready, 1)

            def low_part(k, count):
                pool.wait_ge(dv_high_ready, count)
                pool.tensor_tensor(dv_low[k][:, :], dv[:, :], dv_high[k][:, :].bitcast(F32),
                                   ALU.subtract).then_inc(dv_low_ready, 1)

            inv_std(1)
            pool.memset(state[1][:, :, :], 0.0).then_inc(term_ready, 1)
            inv_std(2)
            low_part(0, 1)
            with pool.Fori(0, BODIES) as i:
                for k in range(2):
                    for v in range(DH):
                        if v == 6:
                            low_part(1 - k, i * 2 + (k + 2))
                        if v == 3:
                            inv_std(i * 2 + (k + 3))
                        pool.wait_ge(dv_used, (i * 2 + k) * TERMS + (DV_BANKS + v + 1))
                        pool.tensor_tensor(state[k][:, v, :], state[k][:, v, :], qT[k][:, :],
                                           ALU.mult).then_inc(term_ready, 1)

        @block.scalar
        def _(act):
            def turn(k, count):
                act.wait_ge(xT_psum, count)
                act.activation(xTk[k][:, :], ps_T, ACT.Copy).then_inc(xT_ready, 1)

            def softmax(k, count):
                act.wait_ge(nmax_ready, count)
                for j in range(2 * NT):
                    last = act.activation(qf[:, j, :], ps_qf[:, j, :], ACT.Exp, bias=nmax[:, j:j + 1],
                                          accum_out=qfsum[:, j:j + 1])
                last.then_inc(qf_exp, 1)

            def turn_qp(k, count):
                act.wait_ge(qpT_psum, count)
                act.activation(qT[k][:, :], ps_qT, ACT.Copy)
                act.activation(pT[k][:, :], ps_pT, ACT.Copy).then_inc(qpT_ready, 1)

            def values(k, count, bank):
                act.wait_ge(v_psum, count)
                act.activation(vT[k][:, :], bank, ACT.Copy).then_inc(vT_ready, 1)

            def high_part(k, count):
                act.wait_ge(diff_ready, count)
                act.activation(dv_high[k][:, :], dv[:, :], ACT.Copy).then_inc(dv_high_ready, 1)

            turn(0, 1)
            act.wait_ge(weights_in, N_WEIGHTS)
            act.activation(select[:, :, :], select_raw[:, :, :], ACT.Copy).then_inc(select_ready, 1)
            values(0, 1, m.psum[:, 7, :])
            high_part(0, 1)
            softmax(0, 1)
            turn_qp(0, 1)
            with act.Fori(0, BODIES) as i:
                for k in range(2):
                    nxt = i * 2 + (k + 2)
                    turn(1 - k, nxt)
                    softmax(1 - k, nxt)
                    values(1 - k, nxt, ps_dv[(k * USES + V_USE) % DV_BANKS])
                    high_part(1 - k, nxt)
                    turn_qp(1 - k, nxt)

        @block.tensor
        def _(pe):
            def turn(count):
                pe.wait_ge(xn_ready, count)
                for t in range(NT):
                    last = pe.transpose(ps_T[:, t * P:(t + 1) * P], xn[:, t, :], m.ident[:, :])
                last.then_inc(xT_psum, 1)

            def logits(k, count):
                pe.wait_ge(xT_ready, count)
                for t in range(NT):
                    last = pe.matmul(m.psum[:, 1 + t // 2, (t % 2) * 256:(t % 2) * 256 + 256],
                                     xTk[k][:, t * P:(t + 1) * P], w_qf[:, :], start=True, stop=True)
                last.then_inc(qf_psum, 1)

            def values(k, count, bank):
                pe.wait_ge(xT_ready, count)
                pe.matmul(bank, w_i[:, :], xTk[k][:, :], start=True, stop=True).then_inc(v_psum, 1)

            def turn_qp(count):
                pe.wait_ge(qf_ready, count)
                for t in range(NT):
                    pe.transpose(ps_qT[:, t * P:(t + 1) * P], qf[:, 2 * t, :], m.ident[:, :])
                    last = pe.transpose(ps_pT[:, t * P:(t + 1) * P], qf[:, 2 * t + 1, :], m.ident[:, :])
                last.then_inc(qpT_psum, 1)

            def output(k, s, tiles):
                if tiles[0] == 0:
                    pe.wait_ge(term_ready, s * DH + 1)
                    pe.wait_ge(dv_used, s * TERMS + DV_BANKS)
                    pe.wait_ge(o_used, s + 1)
                for t in tiles:
                    for v in range(TERMS):
                        last = pe.matmul(ps_o[:, t, :], state[1 - k][:, v, t * P:(t + 1) * P],
                                         w_orep[:, v, :] if v < DH else w_o[:, :], start=(v == 0), stop=(v == DH))
                if tiles[-1] == NT - 1:
                    last.then_inc(o_psum, 1)

            turn(1)
            pe.wait_ge(weights_in, N_WEIGHTS)
            values(0, 1, m.psum[:, 7, :])
            logits(0, 1)
            turn_qp(1)
            pe.wait_ge(select_ready, 1)
            with pe.Fori(0, BODIES) as i:
                for k in range(2):
                    nxt = i * 2 + (k + 2)

                    s = i * 2 + k

                    def bank_of(use):
                        if use == 0:
                            pe.wait_ge(vT_ready, s + 1)
                        else:
                            pe.wait_ge(dv_used, s * TERMS + (DV_BANKS + use - 3))
                        return ps_dv[(k * USES + use) % DV_BANKS]

                    def scan_input(j):
                        bank = bank_of(use_of(j))
                        if j == 0:
                            pe.wait_ge(dv_low_ready, s + 1)
                        if j < DH:
                            pe.matmul(bank, select[:, j, :], dv_high[k][:, :], start=True, stop=False)
                            mm = pe.matmul(bank, select[:, j, :], dv_low[k][:, :], start=False, stop=True)
                        else:
                            mm = pe.matmul(bank, head_ones[:, :], qT[k][:, :], start=True, stop=True)
                        mm.then_inc(dv_psum, 1)

                    for j in (0, 1, 2):
                        scan_input(j)
                    turn(nxt)
                    logits(1 - k, nxt)
                    output(k, s, (0, 1))
                    for j in (3, 4, 5):
                        scan_input(j)
                    values(1 - k, nxt, bank_of(V_USE))
                    output(k, s, (2, 3))
                    for j in (6, 7):
                        scan_input(j)
                    turn_qp(nxt)
                    scan_input(DH)
            output(0, NB, (0, 1, 2, 3))

        @block.vector
        def _(dve):
            def layer_norm(tile, count):
                for t in range(NT):
                    dve.bn_stats(stats[:, t, :], x_of[:, tile + (t + m.first), :])
                dve.drain()
                for t in range(NT):
                    dve.bn_aggr(mv[:, t, :], stats[:, t, :])
                dve.drain()
                dve.tensor_scalar(var_eps[:, :], mv[:, :, 1], LN_EPS, None, ALU.add).then_inc(var_ready, 1)

            def normalise(tile, count):
                dve.wait_ge(rstd_ready, count)
                for t in range(NT):
                    last = dve.tensor_scalar(xn[:, t, :], x_of[:, tile + (t + m.first), :], mv[:, t, 0:1], rstd[:, t:t + 1],
                                             ALU.subtract, ALU.mult)
                last.then_inc(xn_ready, 1)

            def difference(k, count):
                dve.wait_ge(vT_ready, count)
                dve.tensor_scalar(dv[:, 0:1], vT[k][:, 0:1], -1.0, None, ALU.mult)
                dve.tensor_tensor(dv[:, 1:N], vT[k][:, 0:N - 1], vT[k][:, 1:N], ALU.subtract).then_inc(diff_ready, 1)

            def maxima(count):
                dve.wait_ge(qf_psum, count)
                dve.tensor_reduce(nmax[:, :], ps_qf, AX.X, ALU.max)
                dve.drain()
                dve.tensor_scalar(nmax[:, :], nmax[:, :], -1.0, None, ALU.mult).then_inc(nmax_ready, 1)

            def divide(count):
                dve.wait_ge(qf_exp, count)
                dve.reciprocal(qfinv[:, :], qfsum[:, :])
                dve.drain()
                for j in range(2 * NT):
                    last = dve.tensor_scalar(qf[:, j, :], qf[:, j, :], qfinv[:, j:j + 1],
                                             SCALE if j % 2 == 0 else 1.0, ALU.mult, ALU.mult)
                last.then_inc(qf_ready, 1)

            def residual(s):
                x = x_of[:, bass.ds(s * NT + m.first - NT, NT), :]
                dve.wait_ge(o_psum, s + 1)
                dve.tensor_tensor(x, ps_o, x, ALU.add).then_inc(o_used, 1)

            for k in range(DV_BANKS):
                dve.memset(nmax[:, k:k + 1], 0.0).then_inc(dv_used, 1)
            dve.memset(nmax[:, DV_BANKS:DV_BANKS + 1], 0.0).then_inc(o_used, 1)
            dve.drain()
            layer_norm(0, 1)
            normalise(0, 1)
            difference(0, 1)
            layer_norm(NT, 2)
            maxima(1)
            normalise(NT, 2)
            divide(1)
            with dve.Fori(0, BODIES) as i:
                for k in range(2):
                    nxt = i * 2 + (k + 2)
                    tile = (i * 2 + (k + 2)) * NT

                    def scan(v):
                        if v == 0:
                            dve.wait_ge(qpT_ready, i * 2 + (k + 1))
                        dve.wait_ge(dv_psum, (i * 2 + k) * TERMS + (v + 1))
                        bank = ps_dv[(k * USES + use_of(v)) % DV_BANKS]
                        dve.tensor_tensor_scan(state[k][:, v, :], bank, pT[k][:, :], 0.0,
                                               ALU.add, ALU.mult).then_inc(dv_used, 1)

                    scan(0)
                    scan(1)
                    layer_norm(tile, i * 2 + (k + 3))
                    scan(2)
                    maxima(nxt)
                    scan(3)
                    scan(4)
                    scan(5)
                    divide(nxt)
                    difference(1 - k, nxt)
                    residual(i * 2 + k)
                    normalise(tile, i * 2 + (k + 3))
                    scan(6)
                    scan(7)
                    dve.wait_ge(dv_psum, (i * 2 + k) * TERMS + TERMS)
                    dve.tensor_tensor(state[k][:, DH, :], ps_dv[(k * USES + use_of(DH)) % DV_BANKS], vT[k][:, :],
                                      ALU.mult).then_inc(dv_used, 1)
            residual(NB)



def store_stage(nc, m, out):
    with ExitStack() as ctx:
        stored = ctx.enter_context(nc.semaphore("stored"))
        block = ctx.enter_context(nc.Block())

        @block.sync
        def _(sp):
            sp.dma_start(out.rearrange("b (t p) d -> p (b t) d", p=P), m.x[:, m.first:m.first + TILES, :]).then_inc(stored, 16)
            sp.wait_ge(stored, 16)


def build(nc, c, out):
    with ExitStack() as ctx:
        m = Mem()
        m.x = ctx.enter_context(nc.sbuf_tensor("x", [P, NT + TILES + 2 * NT, D], F32))
        m.first = NT
        m.ident = ctx.enter_context(nc.sbuf_tensor("ident", [P, P], F32))
        m.iota8 = ctx.enter_context(nc.sbuf_tensor("iota8", [P, 8], F32))
        m.minus_half = ctx.enter_context(nc.sbuf_tensor("minus_half", [P, 8], F32))
        m.half = ctx.enter_context(nc.sbuf_tensor("half", [P, 8], F32))
        m.psum = ctx.enter_context(nc.psum_tensor("psum", [P, 8, PSUM_BANK], F32))
        lora = {k: c[k] for k in ("loraA_T", "gate_T", "base_T", "loraB_T", "bias", "ident", "iota8")}
        lora_moe_stage(nc, m, "ffn0a", lora, x_dram=c["x"])
        experts = {k: c[k] for k in ("w12", "b1", "b2", "cent", "gain", "select")}
        attn = {k: c[k] for k in ("w_proj", "w_v", "wo_T", "cos", "sin", "ident_b", "mask_qk", "mask_kq")}
        gla = {k: c[k] for k in ("w_qf", "w_i", "select_v", "w_orep", "w_o", "head_ones")}
        attention_stage(nc, m, "attn", attn)
        ex = Experts(nc, ctx, experts)
        lora_moe_stage(nc, m, "ffn0b", lora, experts=ex)
        expert_stage(nc, m, "ffn1a", ex)
        gla_stage(nc, m, "gla", gla)
        expert_stage(nc, m, "ffn1b", ex)
        store_stage(nc, m, out)


def layout(inputs):
    a = {k: np.asarray(v) for k, v in inputs.items()}
    f = lambda v: np.ascontiguousarray(v)
    c = {"x": a["L0_attn_x"]}
    c["loraA_T"] = a["L0_ffn_lora_A"].reshape(P, D).T
    c["gate_T"] = a["L0_ffn_gate_w"].T
    c["base_T"] = a["L0_ffn_base_w"].T
    c["loraB_T"] = a["L0_ffn_lora_B"].transpose(0, 2, 1).reshape(P, D)
    c["bias"] = a["L0_ffn_base_b"]
    c["ident"] = np.eye(P, dtype=np.float32)
    c["iota8"] = np.tile(np.arange(8, dtype=np.float32), (P, 1))
    w1 = np.concatenate([a["L1_ffn_W1_s"], a["L1_ffn_W1_r"]])
    w2 = np.concatenate([a["L1_ffn_W2_s"], a["L1_ffn_W2_r"]])
    b1 = np.concatenate([a["L1_ffn_b1_s"], a["L1_ffn_b1_r"]])
    w2 = w2.reshape(10, 4, P, D).transpose(2, 0, 1, 3).reshape(P, 10, 512)
    c["w12"] = np.concatenate([w1.transpose(1, 0, 2), w2], axis=1)
    c["b1"] = b1.reshape(40, P).T
    c["b2"] = np.concatenate([a["L1_ffn_b2_s"], a["L1_ffn_b2_r"]]).T
    c["select"] = np.zeros((P, 8, P), np.float32)
    for e in range(8):
        c["select"][[2 + e, 10 + 2 + e], e] = 1.0
    c["cent"] = a["L1_ffn_centroids"]
    c["gain"] = np.stack([a["L1_ffn_g_shared"]] * 2 + [a["L1_ffn_g_routed"]] * 8
                         + [np.ones(P, np.float32)] * 10, axis=1)
    c["w_qf"] = np.concatenate([a["L1_attn_Wq"], a["L1_attn_Wf"]], axis=1)
    c["w_i"] = a["L1_attn_Wi"]
    c["select_v"] = np.stack([np.kron(np.eye(16), np.outer(np.eye(8)[v], np.ones(8))) for v in range(8)],
                             axis=1).astype(np.float32)
    c["w_orep"] = np.repeat(a["L1_attn_Wo"].reshape(16, 1, 8, D), 8, axis=1).transpose(0, 1, 2, 3).reshape(P, 8, D)
    c["w_o"] = a["L1_attn_Wo"]
    c["head_ones"] = np.kron(np.eye(16, dtype=np.float32), np.ones((8, 8), np.float32))
    wq, wk, wv = a["L0_attn_W_qkv"].reshape(3, 16, 8, D)
    by_d = lambda t: t.reshape(2, 8, 8, D).transpose(0, 2, 1, 3).reshape(P, D).T
    swapped = lambda t: t.reshape(16, 4, 2, D)[:, :, ::-1].reshape(16, 8, D)
    c["w_proj"] = np.stack([by_d(wq), by_d(swapped(wq)), by_d(wk), by_d(swapped(wk))], axis=1)
    c["w_v"] = wv.reshape(P, D).T
    c["wo_T"] = a["L0_attn_W_o"].T
    inv_freq = np.float32(10000.0) ** (np.arange(0, 8, 2, dtype=np.float32) / np.float32(8))
    ang = np.arange(SEQ, dtype=np.float32)[None, :] / inv_freq[:, None]
    table = lambda t: np.tile(np.repeat(t, 8, axis=0), (2, 1))
    c["cos"] = table(np.repeat(np.cos(ang), 2, axis=0))
    sin = np.stack([-np.sin(ang), np.sin(ang)], axis=1).reshape(8, SEQ)
    c["sin"] = table(sin)
    BIG = -1e30
    bf = mybir.dt.np(BF16)
    c["ident_b"] = np.eye(P, dtype=np.float32).astype(bf)
    c["mask_qk"] = np.triu(np.full((P, P), BIG, np.float32), 1).astype(bf)
    c["mask_kq"] = np.tril(np.full((P, P), BIG, np.float32), -1).astype(bf)
    return {k: f(v) for k, v in c.items()}


def kernel(**inputs):
    import concourse.bacc as bacc
    from concourse.bass_utils import run_bass_kernel_spmd

    nc = bacc.Bacc("TRN2", target_bir_lowering=False, num_devices=1)
    arrays = {f"in_{k}": v for k, v in layout(inputs).items()}
    c = {k[3:]: nc.dram_tensor(k, v.shape, mybir.dt.from_np(v.dtype), kind="ExternalInput").ap()
         for k, v in arrays.items()}
    nc.disable_value_cache = True
    out = nc.dram_tensor("out_0", (NB, SEQ, D), F32, kind="ExternalOutput").ap()
    build(nc, c, out)
    return run_bass_kernel_spmd(nc, [arrays], core_ids=[0]).results[0]["out_0"]
```
